# Optimizing a Trainium2 kernel written in Bass

```python
import numpy as np
import jax
import jax.numpy as jnp

def _softmax(x, axis=-1):
    return jax.nn.softmax(x, axis=axis)

def _gelu(x):
    return jax.nn.gelu(x, approximate=True)

def _silu(x):
    return jax.nn.silu(x)

def _sigmoid(x):
    return jax.nn.sigmoid(x)

def _layernorm(x, axis=-1, eps=1e-05):
    m = jnp.mean(x, axis=axis, keepdims=True)
    v = jnp.var(x, axis=axis, keepdims=True)
    return (x - m) / jnp.sqrt(v + eps)

def _scatter_add(tgt, idx, src, axis=0):
    return tgt.at[idx].add(src)

def _segment_sum(src, seg, n):
    return jax.ops.segment_sum(src, seg, n)
kernel_name = 'mk_xattn_ffn_d2_seqx_r8_4af030'

def setup_inputs(seed: int=0):
    np.random.seed(seed)
    _w = jnp.asarray

    def _rec_inputs():
        import jax
        import jax.numpy as jnp
        _rk = jax.random.key(seed)
        x = 0.002226 + 0.9996 * jax.random.normal(jax.random.fold_in(_rk, 1), (64, 128, 128), jnp.float32)
        _lenS = 128 - jax.random.randint(jax.random.fold_in(_rk, 7), (64,), 0, max(1, 128 // 4) + 1, jnp.int32)
        _lenS2 = 77 - jax.random.randint(jax.random.fold_in(_rk, 8), (64,), 0, max(1, 77 // 4) + 1, jnp.int32)
        _ctx_1024P = jax.random.normal(jax.random.fold_in(_rk, 11), (64, 16, 128), jnp.float32)
        _ctx_1024c = jax.random.dirichlet(jax.random.fold_in(_rk, 511), 0.3 * jnp.ones((16,), jnp.float32), (64, 77))
        _ctx_1024t = jnp.einsum('bsk,bkd->bsd', _ctx_1024c, _ctx_1024P)
        _ctx_1024t = _ctx_1024t * jax.lax.rsqrt(jnp.mean(jnp.square(_ctx_1024t)) + 1e-12) * 0.953939
        ctx_1024 = -7.10856e-05 + 0.999911 * (_ctx_1024t + 0.3 * jax.random.normal(jax.random.fold_in(_rk, 611), (64, 77, 128), jnp.float32))
        _validS = jnp.arange(128)[None, :] < _lenS[:, None]
        _validS2 = jnp.arange(77)[None, :] < _lenS2[:, None]
        _causal = jnp.tril(jnp.ones((128, 128), dtype=bool))
        mask_BxS2_bk0 = jnp.logical_not(jnp.broadcast_to(_validS2[:, :], (64, 77)))
        return (x, ctx_1024, mask_BxS2_bk0)
    x, ctx_1024, mask_BxS2_bk0 = _rec_inputs()

    def _L0_xattn_setup():
        import jax, jax.numpy as jnp
        import numpy as np
        DIM, DIM_HEAD, HEADS, SCALE = (128, 64, 8, 8.0)
        INNER = DIM_HEAD * HEADS
        LN_EPS = 1e-05
        L2_EPS = 1e-12

        def layer_norm(x, w, b):
            mu = jnp.mean(x, axis=-1, keepdims=True)
            var = jnp.mean(jnp.square(x - mu), axis=-1, keepdims=True)
            return (x - mu) * jax.lax.rsqrt(var + LN_EPS) * w + b

        def l2norm(t):
            n = jnp.sqrt(jnp.sum(jnp.square(t), axis=-1, keepdims=True))
            return t / jnp.maximum(n, L2_EPS)
        key = jax.random.key(seed)
        ks = jax.random.split(key, 8)
        b, n, m = (8, 1024, 64)
        x = jax.random.normal(ks[0], (b, n, DIM), dtype=jnp.float32)
        latents = jax.random.normal(ks[1], (b, m, DIM), dtype=jnp.float32)
        mask = jax.random.randint(ks[2], (b, n), 0, 2) > 0
        Wq = jax.random.normal(ks[3], (DIM, INNER), dtype=jnp.float32) * DIM ** (-0.5)
        Wkv = jax.random.normal(ks[4], (DIM, 2 * INNER), dtype=jnp.float32) * DIM ** (-0.5)
        Wo = jax.random.normal(ks[5], (INNER, DIM), dtype=jnp.float32) * INNER ** (-0.5)
        return {'x': x, 'latents': latents, 'mask': mask, 'ln_x_w': jnp.ones((DIM,)), 'ln_x_b': jnp.zeros((DIM,)), 'ln_l_w': jnp.ones((DIM,)), 'ln_l_b': jnp.zeros((DIM,)), 'Wq': Wq, 'Wkv': Wkv, 'q_scale': jnp.ones((DIM_HEAD,)), 'k_scale': jnp.ones((DIM_HEAD,)), 'Wo': Wo, 'ln_o_w': jnp.ones((DIM,)), 'ln_o_b': jnp.zeros((DIM,))}
    _L0_xattn_all = _L0_xattn_setup()
    _L0_xattn_in = {k: v for k, v in _L0_xattn_all.items() if k in ('ln_x_w', 'ln_x_b', 'ln_l_w', 'ln_l_b', 'Wq', 'Wkv', 'q_scale', 'k_scale', 'Wo', 'ln_o_w', 'ln_o_b')}
    del _L0_xattn_all

    def _L0_ffn_setup():
        import jax, jax.numpy as jnp
        import numpy as np
        B, S, IN, OUT = (4, 1024, 128, 128)
        EPS = 1e-06

        def _xla_quantized_matmul(x2d, weight_q, weight_scale):
            amax = jnp.max(jnp.abs(x2d), axis=-1, keepdims=True)
            x_scale = jnp.maximum(amax, EPS) / 127.0
            x_q = jnp.clip(jnp.round(x2d / x_scale), -128, 127).astype(jnp.int8)
            acc = jax.lax.dot_general(x_q, weight_q, (((1,), (1,)), ((), ())), preferred_element_type=jnp.int32)
            return acc.astype(jnp.float32) * x_scale * weight_scale[None, :]
        key = jax.random.key(seed)
        k1, k2, k3, k4 = jax.random.split(key, 4)
        x = jax.random.normal(k1, (B, S, IN), dtype=jnp.float32)
        weight_q = jax.random.randint(k2, (OUT, IN), -128, 128, dtype=jnp.int32).astype(jnp.int8)
        weight_scale = jax.random.uniform(k3, (OUT,), dtype=jnp.float32, minval=0.001, maxval=0.01)
        bias = jax.random.normal(k4, (OUT,), dtype=jnp.float32) * 0.01
        return {'x': x, 'weight_q': weight_q, 'weight_scale': weight_scale, 'bias': bias}
    _L0_ffn_all = _L0_ffn_setup()
    _L0_ffn_in = {k: v for k, v in _L0_ffn_all.items() if k in ('weight_q', 'weight_scale', 'bias')}
    del _L0_ffn_all

    def _L1_xattn_setup():
        import jax, jax.numpy as jnp
        import numpy as np
        B, N, M, D = (8, 256, 256, 128)
        key = jax.random.key(seed)
        k1, k2, k3, k4 = jax.random.split(key, 4)
        glorot = (2.0 / (D + D)) ** 0.5
        return {'text': jax.random.normal(k1, (B, N, D), dtype=jnp.float32), 'context': jax.random.normal(k2, (B, M, D), dtype=jnp.float32), 'We': jax.random.normal(k3, (D, D), dtype=jnp.float32) * glorot, 'W2': jax.random.normal(k4, (D, D), dtype=jnp.float32) * glorot}
    _L1_xattn_all = _L1_xattn_setup()
    _L1_xattn_in = {k: v for k, v in _L1_xattn_all.items() if k in ('We', 'W2')}
    del _L1_xattn_all

    def _L1_ffn_setup():
        import jax, jax.numpy as jnp
        import numpy as np
        D_MODEL, D_FF, N_EXP = (128, 512, 8)
        key = jax.random.key(seed)
        ks = jax.random.split(key, 8)
        s = lambda fan_in: 1.0 / np.sqrt(fan_in)
        x = jax.random.normal(ks[0], (4, 256, D_MODEL), dtype=jnp.float32)
        Wr = jax.random.uniform(ks[1], (N_EXP, D_MODEL), jnp.float32, -s(D_MODEL), s(D_MODEL))
        br = jax.random.uniform(ks[2], (N_EXP,), jnp.float32, -s(D_MODEL), s(D_MODEL))
        W1 = jax.random.uniform(ks[3], (N_EXP, D_FF, D_MODEL), jnp.float32, -s(D_MODEL), s(D_MODEL))
        b1 = jax.random.uniform(ks[4], (N_EXP, D_FF), jnp.float32, -s(D_MODEL), s(D_MODEL))
        W2 = jax.random.uniform(ks[5], (N_EXP, D_MODEL, D_FF), jnp.float32, -s(D_FF), s(D_FF))
        b2 = jax.random.uniform(ks[6], (N_EXP, D_MODEL), jnp.float32, -s(D_FF), s(D_FF))
        return {'x': x, 'Wr': Wr, 'br': br, 'W1': W1, 'b1': b1, 'W2': W2, 'b2': b2}
    _L1_ffn_all = _L1_ffn_setup()
    _L1_ffn_in = {k: v for k, v in _L1_ffn_all.items() if k in ('Wr', 'br', 'W1', 'b1', 'W2', 'b2')}
    del _L1_ffn_all
    return {'x': x, 'ctx_1024': ctx_1024, 'mask_BxS2_bk0': mask_BxS2_bk0, 'L0_xattn_ln_x_w': _L0_xattn_in['ln_x_w'], 'L0_xattn_ln_x_b': _L0_xattn_in['ln_x_b'], 'L0_xattn_ln_l_w': _L0_xattn_in['ln_l_w'], 'L0_xattn_ln_l_b': _L0_xattn_in['ln_l_b'], 'L0_xattn_Wq': _L0_xattn_in['Wq'], 'L0_xattn_Wkv': _L0_xattn_in['Wkv'], 'L0_xattn_q_scale': _L0_xattn_in['q_scale'], 'L0_xattn_k_scale': _L0_xattn_in['k_scale'], 'L0_xattn_Wo': _L0_xattn_in['Wo'], 'L0_xattn_ln_o_w': _L0_xattn_in['ln_o_w'], 'L0_xattn_ln_o_b': _L0_xattn_in['ln_o_b'], 'L0_ffn_weight_q': _L0_ffn_in['weight_q'], 'L0_ffn_weight_scale': _L0_ffn_in['weight_scale'], 'L0_ffn_bias': _L0_ffn_in['bias'], 'L1_xattn_We': _L1_xattn_in['We'], 'L1_xattn_W2': _L1_xattn_in['W2'], 'L1_ffn_Wr': _L1_ffn_in['Wr'], 'L1_ffn_br': _L1_ffn_in['br'], 'L1_ffn_W1': _L1_ffn_in['W1'], 'L1_ffn_b1': _L1_ffn_in['b1'], 'L1_ffn_W2': _L1_ffn_in['W2'], 'L1_ffn_b2': _L1_ffn_in['b2']}

def reference(x, ctx_1024, mask_BxS2_bk0, L0_xattn_ln_x_w, L0_xattn_ln_x_b, L0_xattn_ln_l_w, L0_xattn_ln_l_b, L0_xattn_Wq, L0_xattn_Wkv, L0_xattn_q_scale, L0_xattn_k_scale, L0_xattn_Wo, L0_xattn_ln_o_w, L0_xattn_ln_o_b, L0_ffn_weight_q, L0_ffn_weight_scale, L0_ffn_bias, L1_xattn_We, L1_xattn_W2, L1_ffn_Wr, L1_ffn_br, L1_ffn_W1, L1_ffn_b1, L1_ffn_W2, L1_ffn_b2):
    import jax
    import jax.numpy as jnp

    def _L0_xattn_ref(x, latents, mask, ln_x_w, ln_x_b, ln_l_w, ln_l_b, Wq, Wkv, q_scale, k_scale, Wo, ln_o_w, ln_o_b):
        import jax, jax.numpy as jnp
        import numpy as np
        DIM, DIM_HEAD, HEADS, SCALE = (128, 64, 8, 8.0)
        INNER = DIM_HEAD * HEADS
        LN_EPS = 1e-05
        L2_EPS = 1e-12

        def layer_norm(x, w, b):
            mu = jnp.mean(x, axis=-1, keepdims=True)
            var = jnp.mean(jnp.square(x - mu), axis=-1, keepdims=True)
            return (x - mu) * jax.lax.rsqrt(var + LN_EPS) * w + b

        def l2norm(t):
            n = jnp.sqrt(jnp.sum(jnp.square(t), axis=-1, keepdims=True))
            return t / jnp.maximum(n, L2_EPS)
        b, n, _ = x.shape
        m = latents.shape[1]
        x = layer_norm(x, ln_x_w, ln_x_b)
        latents = layer_norm(latents, ln_l_w, ln_l_b)
        q = latents @ Wq
        kv_input = jnp.concatenate([x, latents], axis=1)
        kv = kv_input @ Wkv
        k, v = jnp.split(kv, 2, axis=-1)

        def to_heads(t):
            return t.reshape(t.shape[0], t.shape[1], HEADS, DIM_HEAD).transpose(0, 2, 1, 3)
        q, k, v = map(to_heads, (q, k, v))
        q = l2norm(q) * q_scale
        k = l2norm(k) * k_scale
        sim = jnp.einsum('bhid,bhjd->bhij', q, k) * SCALE
        full_mask = jnp.concatenate([mask, jnp.ones((b, m), dtype=bool)], axis=1)[:, None, None, :]
        max_neg = -jnp.finfo(sim.dtype).max
        sim = jnp.where(full_mask, sim, max_neg)
        attn = jax.nn.softmax(sim.astype(jnp.float32), axis=-1).astype(sim.dtype)
        out = jnp.einsum('bhij,bhjd->bhid', attn, v)
        out = out.transpose(0, 2, 1, 3).reshape(b, m, INNER)
        return layer_norm(out @ Wo, ln_o_w, ln_o_b)

    def _L0_ffn_ref(x, weight_q, weight_scale, bias):
        import jax, jax.numpy as jnp
        import numpy as np
        B, S, IN, OUT = (4, 1024, 128, 128)
        EPS = 1e-06

        def _xla_quantized_matmul(x2d, weight_q, weight_scale):
            amax = jnp.max(jnp.abs(x2d), axis=-1, keepdims=True)
            x_scale = jnp.maximum(amax, EPS) / 127.0
            x_q = jnp.clip(jnp.round(x2d / x_scale), -128, 127).astype(jnp.int8)
            acc = jax.lax.dot_general(x_q, weight_q, (((1,), (1,)), ((), ())), preferred_element_type=jnp.int32)
            return acc.astype(jnp.float32) * x_scale * weight_scale[None, :]
        orig_shape = x.shape
        x2d = x.reshape(-1, orig_shape[-1])
        out = _xla_quantized_matmul(x2d, weight_q, weight_scale)
        out = out.reshape(*orig_shape[:-1], out.shape[-1])
        out = out + bias
        return out

    def _L1_xattn_ref(text, context, We, W2):
        import jax, jax.numpy as jnp
        import numpy as np
        B, N, M, D = (8, 256, 256, 128)
        scores = jnp.einsum('bnd,bmd->bnm', text @ We, context)
        attn = jax.nn.softmax(scores, axis=1)
        res = jnp.einsum('bnm,bmd->bnd', attn, context)
        return res @ W2.T

    def _L1_ffn_ref(x, Wr, br, W1, b1, W2, b2):
        import jax, jax.numpy as jnp
        import numpy as np
        D_MODEL, D_FF, N_EXP = (128, 512, 8)
        B, S, D = x.shape
        xf = x.reshape(-1, D)
        logits = xf @ Wr.T + br
        expert_idx = jnp.argmax(logits, axis=-1)
        h = jax.nn.relu(jnp.einsum('td,efd->etf', xf, W1) + b1[:, None, :])
        y = jnp.einsum('etf,edf->etd', h, W2) + b2[:, None, :]
        out = y[expert_idx, jnp.arange(xf.shape[0])]
        return out.reshape(B, S, D)
    x = x + _L0_xattn_ref(ctx_1024, _layernorm(x, axis=-1), mask_BxS2_bk0, L0_xattn_ln_x_w, L0_xattn_ln_x_b, L0_xattn_ln_l_w, L0_xattn_ln_l_b, L0_xattn_Wq, L0_xattn_Wkv, L0_xattn_q_scale, L0_xattn_k_scale, L0_xattn_Wo, L0_xattn_ln_o_w, L0_xattn_ln_o_b)
    x = x + _L0_ffn_ref(_layernorm(x, axis=-1), L0_ffn_weight_q, L0_ffn_weight_scale, L0_ffn_bias)
    x = x + _L1_xattn_ref(_layernorm(x, axis=-1), ctx_1024, L1_xattn_We, L1_xattn_W2)
    x = x + _L1_ffn_ref(_layernorm(x, axis=-1), L1_ffn_Wr, L1_ffn_br, L1_ffn_W1, L1_ffn_b1, L1_ffn_W2, L1_ffn_b2)
    return x

_drawn_inputs = setup_inputs


def setup_inputs(seed=0):
    import zlib

    import numpy as np

    out = dict(_drawn_inputs(seed))
    spreads = {'L0_xattn_ln_x_w': (1.0, 0.2),
     'L0_xattn_ln_x_b': (0.0, 0.1),
     'L0_xattn_ln_l_w': (1.0, 0.2),
     'L0_xattn_ln_l_b': (0.0, 0.1),
     'L0_xattn_q_scale': (1.0, 0.2),
     'L0_xattn_k_scale': (1.0, 0.2),
     'L0_xattn_ln_o_w': (1.0, 0.2),
     'L0_xattn_ln_o_b': (0.0, 0.1)}
    factors = {'L0_ffn_bias': 27.829, 'L1_ffn_br': 4.656, 'L1_ffn_b1': 8.0, 'L1_ffn_b2': 8.0}
    for name, (base, spread) in spreads.items():
        noise = np.random.default_rng([zlib.crc32(name.encode()), seed]).standard_normal(out[name].shape)
        drawn = base * np.exp(spread * noise) if base else spread * noise
        out[name] = jnp.asarray(drawn.astype(out[name].dtype))
    for name, factor in factors.items():
        out[name] = (out[name] * factor).astype(out[name].dtype)
    return out
```

```python
import math
from contextlib import ExitStack

import concourse.bass as bass
from concourse import mybir

F32 = mybir.dt.float32
F32R = mybir.dt.float32r
BF16 = mybir.dt.bfloat16
I32 = mybir.dt.int32
U32 = mybir.dt.uint32
I8 = mybir.dt.int8
U8 = mybir.dt.uint8
ALU = mybir.AluOpType
ACT = mybir.ActivationFunctionType
AX = mybir.AxisListType.X

P = 128
LN_EPS = 1e-5
L2_EPS = 1e-12
SIM_SCALE = 8.0
EXP_ROOM = 80.0
MASKED = -1e30
LN_LIFT = 20
LN2 = math.log(2.0)
VW = 96
Q_EPS = 1e-6
Q_MAX = 127.0
ROUND = 1.5 * 2.0 ** 23
G = 4
FILL = 20000.0
LOT = 8
SLOT_R = 6 + 1 + 6 + 3 + 3 + 2 + 5


def latent_attention(nc, x_res, ctx_res, ident, sorted_rows, x, ctx, mask, ln_x_w, ln_x_b, ln_l_w, ln_l_b, Wq, Wkv,
                     q_scale, k_scale, Wo, ln_o_w, ln_o_b):
    B, S, D = x.shape
    M = ctx.shape[1]
    DH = q_scale.shape[0]
    INNER = Wq.shape[1]
    H = INNER // DH
    PAIRS = H // 2
    assert S == P and D == P and INNER == PAIRS * P and 2 * DH == P

    with ExitStack() as stack:
        def sb(name, shape, dt=F32):
            return stack.enter_context(nc.sbuf_tensor(name, shape, dt))

        def sem(name):
            return stack.enter_context(nc.semaphore(name))

        fill = sb("fill", [P, 1, D + 3])
        ids = sb("ids", [P, B], I32)
        ones_col = sb("ones_col", [P, 1])
        mask_raw = sb("mask_raw", [P, P], U8)
        mask_f = sb("mask_f", [P, P])
        mask_bias = sb("mask_bias", [P, P])
        neg_shift = sb("neg_shift", [P, 1])
        qs_b = sb("qs_b", [P, DH])
        ks_b = sb("ks_b", [P, DH])
        qk_prod = sb("qk_prod", [P, DH])
        qk_max = sb("qk_max", [P, 1])
        scale_col = sb("scale_col", [P, 4])
        ln_cols = sb("ln_cols", [P, 4])
        lno_w = sb("lno_w", [P, D])
        lno_b = sb("lno_b", [P, D])
        w_raw = sb("w_raw", [P, 3 * INNER])
        w_hi = sb("w_hi", [P, 3 * INNER], F32R)
        w_lo = sb("w_lo", [P, 3 * INNER], F32R)
        wo_sb = sb("wo_sb", [P, PAIRS, D])

        bn6 = sb("bn6", [P, 2, 6])
        xc_stat = sb("xc_stat", [P, 2, 2, 2])
        lift_bias = sb("lift_bias", [P, 1])
        var_in = sb("var_in", [P, 32])
        rs_ln = sb("rs_ln", [P, 32])
        rs_y0 = sb("rs_y0", [P, 32])
        rs_t1 = sb("rs_t1", [P, 32])
        rs_t2 = sb("rs_t2", [P, 32])
        rs_t3 = sb("rs_t3", [P, 32])
        rs_t4 = sb("rs_t4", [P, 32])
        rstd = sb("rstd", [P, 2, 32])
        xc_hat = sb("xc_hat", [P, 2, 2, D])
        xc_t = sb("xc_t", [P, 2, 2, P])
        xc_hi = sb("xc_hi", [P, 2, 2, P], F32R)
        xc_lo = sb("xc_lo", [P, 2, 2, P], F32R)
        mask_now = sb("mask_now", [P, 2])
        sq = sb("sq", [P, 3 * INNER])
        sumsq = sb("sumsq", [P, 3 * H])
        three = sb("three", [P, 32])
        var_mul = sb("var_mul", [P, 2])
        var_add = sb("var_add", [P, 3])
        var_tmp = sb("var_tmp", [P, 2])
        qk_hat = sb("qk_hat", [P, 3 * INNER])
        q_bd = sb("q_bd", [P, PAIRS, 2, P])
        k_t = sb("k_t", [P, 2, INNER])
        prob = sb("prob", [P, 2, H * P])
        v_sb = sb("v_sb", [P, 2, H, VW])
        rden = sb("rden", [P, H])
        o_n = sb("o_n", [P, INNER])
        o_t = sb("o_t", [P, INNER])
        o6 = sb("o6", [P, 6])
        o_stat = sb("o_stat", [P, 2, 2])
        o_c = sb("o_c", [P, 2, D])
        x_b = sb("x_b", [P, 2, D])

        ps = stack.enter_context(nc.psum_tensor("ps", [P, 8, 512], F32))
        ps_qk = ps[:, 0:3, :]
        ps_v, ps_ot = (ps[:, 4, :], ps[:, 5, :]), ps[:, 3, :]
        ps_s = (ps[:, 4, :], ps[:, 5, :], ps[:, 3, :], ps[:, 4, :])
        ps_pv = ps[:, 6, 0:(H - 1) * (DH + 1)].rearrange("p (h e) -> p h e", e=DH + 1)
        ps_xc = ps[:, 7, 0:2 * P]
        ps_o = ps[:, 7, 2 * P:3 * P]
        ps_pv7 = ps[:, 7, 3 * P:3 * P + DH + 1]

        lots = [slice(0, 4)] + [slice(n, min(n + 12, B)) for n in range(4, B, 12)]
        ld_lot = [sem(f"ld_lot{n}") for n in range(len(lots))]
        tokens_in = sem("tokens_in")
        ld_w = sem("ld_w")
        ctx_zeroed = sem("ctx_zeroed")
        const_ready = sem("const_ready")
        setup_v = sem("setup_v")
        setup_p = sem("setup_p")
        setup_g = sem("setup_g")
        s_maskT = sem("s_maskT")
        xc_bn = sem("xc_bn")
        xc_mv = sem("xc_mv")
        var_t = sem("var_t")
        ss_raw = sem("ss_raw")
        ss_done = sem("ss_done")
        var_ready = sem("var_ready")
        ln_done = sem("ln_done")
        y0_done = sem("y0_done")
        nwt = sem("nwt")
        rs_ready = sem("rs_ready")
        hat_ready = sem("hat_ready")
        xct_sb = sem("xct_sb")
        hi_done = sem("hi_done")
        lo_done = sem("lo_done")
        qk_done = sem("qk_done")
        sq_done = sem("sq_done")
        scaled = sem("scaled")
        qkT_done = sem("qkT_done")
        qbd_done = sem("qbd_done")
        kt_done = sem("kt_done")
        sim_done = sem("sim_done")
        exp_done = sem("exp_done")
        v_done = sem("v_done")
        v_copied = sem("v_copied")
        pv_done = sem("pv_done")
        rl_done = sem("rl_done")
        on_done = sem("on_done")
        onT_done = sem("onT_done")
        ot_done = sem("ot_done")
        wo_done = sem("wo_done")
        xcT_done = sem("xcT_done")
        o_bn = sem("o_bn")
        o_mv = sem("o_mv")
        o_cent = sem("o_cent")
        xb_done = sem("xb_done")
        mask_set = sem("mask_set")
        x1_done = sem("x1_done")
        fill_out = sem("fill_out")

        N_W = 16 * 16

        SETUP_V, SETUP_G = 12, 11

        def rounds(run, eng):
            for j in range(-3, 5):
                run(j, j % 2)
            with eng.Fori(0, (B - 8) // 2) as turn:
                run(5 + 2 * turn, 1, True)
                run(6 + 2 * turn, 0, True)
            for j in range(B - 3, B + 2):
                run(j, j % 2)

        def has(b, inside):
            return inside or 0 <= b < B

        block = stack.enter_context(nc.Block())

        @block.sync
        def _(sp):
            for n, lot in enumerate(lots):
                sp.dma_start(x_res[:, lot, 0:D], x[lot].rearrange("b s d -> s b d")).then_inc(ld_lot[n], 16)
                if n == 0:
                    sp.wait_ge(ctx_zeroed, 1)
                sp.dma_start(ctx_res[0:M, lot, :], ctx[lot].rearrange("b m d -> m b d")).then_inc(ld_lot[n], 16)
            for n, lot in enumerate(lots):
                sp.wait_ge(ld_lot[n], 32)
                sp.sem_inc(tokens_in, lot.stop - lot.start)
            sp.wait_ge(setup_v, SETUP_V)
            tiles = sorted_rows.shape[0] // P
            sp.dma_start(sorted_rows.rearrange("(t p) w -> p t w", p=P),
                         fill[:, :, :].to_broadcast([P, tiles, D + 3])).then_inc(fill_out, 16)
            sp.wait_ge(fill_out, 16)

        @block.scalar
        def _(act):
            act.dma_start(w_raw[:, 0:INNER], Wq).then_inc(ld_w, 16)
            act.dma_start(w_raw[:, INNER:3 * INNER], Wkv).then_inc(ld_w, 16)
            act.dma_start(wo_sb[:, :, :], Wo.rearrange("(t p) d -> p t d", p=P)).then_inc(ld_w, 16)
            act.dma_start(mask_raw[0:B, 0:M], mask).then_inc(ld_w, 16)
            for n, v in enumerate((ln_l_w, ln_l_b, ln_x_w, ln_x_b)):
                act.dma_start(ln_cols[:, n:n + 1], v.rearrange("(p a) -> p a", a=1)).then_inc(ld_w, 16)
            act.dma_start(qs_b[:, :], q_scale.partition_broadcast(P)).then_inc(ld_w, 16)
            act.dma_start(ks_b[:, :], k_scale.partition_broadcast(P)).then_inc(ld_w, 16)
            act.dma_start(lno_w[:, :], ln_o_w.partition_broadcast(P)).then_inc(ld_w, 16)
            act.dma_start(lno_b[:, :], ln_o_b.partition_broadcast(P)).then_inc(ld_w, 16)
            for n, v in enumerate((q_scale, k_scale)):
                for half in (0, 1):
                    act.dma_start(scale_col[half * DH:(half + 1) * DH, n:n + 1],
                                  v.rearrange("(p a) -> p a", a=1)).then_inc(ld_w, 16)
            act.wait_ge(setup_v, SETUP_V)
            act.wait_ge(setup_g, SETUP_G)
            nc.scalar.preload_act_table_set("natural_log_exp_and_others")

            def run(j, par, inside=False):
                if has(j, inside):
                    act.wait_ge(qkT_done, 3 * j + 1)
                    if inside or j > 0:
                        act.wait_ge(sim_done, 4 * j)
                    for half in (0, 1):
                        rows = slice(half * DH, (half + 1) * DH)
                        last = nc.scalar.activation(q_bd[rows, :, half, :],
                                                    ps_qk[rows, 0, :].rearrange("p (t q) -> p t q", q=P),
                                                    ACT.Copy, scale=scale_col[rows, 2:3])
                    last.then_inc(qbd_done, 1)
                if has(j, inside):
                    if inside or j > 0:
                        act.wait_ge(pv_done, j)
                    for kt in (0, 1):
                        act.wait_ge(v_done, 2 * j + kt + 1)
                        nc.scalar.activation(v_sb[:, kt, :, 0:DH], ps_v[kt].rearrange("p (h d) -> p h d", d=DH),
                                             ACT.Copy).then_inc(v_copied, 1)
                if has(j + 1, inside):
                    if inside or j >= 0:
                        act.wait_ge(ss_raw, 3 * j + 3)
                    for n in range(3):
                        act.wait_ge(qk_done, 3 * j + 4 + n)
                        nc.scalar.activation(sq[:, n * INNER:(n + 1) * INNER], ps_qk[:, n, :],
                                             ACT.Square).then_inc(sq_done, 1)
                if has(j - 1, inside):
                    act.wait_ge(onT_done, j)
                    if inside or j > 1:
                        act.wait_ge(wo_done, j - 1)
                    nc.scalar.activation(o_t[:, :], ps_ot, ACT.Copy).then_inc(ot_done, 1)

                def exps(units):
                    for n in units:
                        if n == 2:
                            act.wait_ge(mask_set, j + 1)
                        act.wait_ge(sim_done, 4 * j + n + 1)
                        nc.scalar.activation(prob[:, n // 2, n % 2 * INNER:(n % 2 + 1) * INNER], ps_s[n], ACT.Exp,
                                             bias=(mask_now[:, par:par + 1] if n > 1 else
                                                   neg_shift[:, 0:1])).then_inc(exp_done, 1)

                act.wait_ge(var_ready, j + 4)
                if has(j + 1, inside):
                    act.wait_ge(ss_done, j + 2)
                if inside or j > -3:
                    act.wait_ge(rs_ready, j + 3)
                nc.scalar.activation(rs_ln[:, :], var_in[:, :], ACT.Ln, scale=float(2 ** LN_LIFT)).then_inc(ln_done, 1)
                act.wait_ge(ln_done, j + 4)
                nc.scalar.activation(rs_y0[:, :], rs_ln[:, :], ACT.Exp, scale=-0.5,
                                     bias=lift_bias[:, 0:1]).then_inc(y0_done, 1)
                if has(j, inside):
                    exps((0, 1, 2, 3))
                if has(j + 2, inside):
                    act.wait_ge(xct_sb, j + 3)
                    if inside or j > -1:
                        act.wait_ge(v_done, 2 * j + 2)
                    nc.scalar.activation(xc_hi[:, par, :, :], xc_t[:, par, :, :], ACT.Copy).then_inc(hi_done, 1)

            rounds(run, act)

        @block.gpsimd
        def _(pool):
            nc.gpsimd.memset(ctx_res[:, :, :], 0.0).then_inc(ctx_zeroed, 1)
            nc.gpsimd.memset(mask_f[:, :], 0.0).then_inc(setup_p, 1)
            nc.gpsimd.memset(ident[:, :], 0.0).then_inc(setup_p, 1)
            nc.gpsimd.memset(var_in[:, :], 1.0).then_inc(setup_p, 1)
            nc.gpsimd.memset(fill[:, :, :], FILL).then_inc(setup_p, 1)
            nc.gpsimd.iota(ids[:, :], pattern=[[P, B]], base=0, channel_multiplier=1).then_inc(setup_p, 1)
            pool.wait_ge(setup_p, 5)
            nc.gpsimd.affine_select(out=ident[:, :], in_=ident[:, :], compare_op=ALU.not_equal, fill=1.0,
                                    base=0, pattern=[[-1, P]], channel_multiplier=1).then_inc(setup_g, 1)
            nc.gpsimd.memset(q_bd[:, :, :, :], 0.0).then_inc(setup_g, 1)
            nc.gpsimd.memset(v_sb[:, :, :, DH + 1:VW], 0.0).then_inc(setup_g, 1)
            nc.gpsimd.memset(v_sb[:, :, :, DH:DH + 1], 1.0).then_inc(setup_g, 1)
            nc.gpsimd.memset(ones_col[:, :], 1.0).then_inc(setup_g, 1)
            nc.gpsimd.memset(three[:, :], 3.0).then_inc(setup_g, 1)
            nc.gpsimd.memset(var_mul[:, 0:1], 1.0 + LN_EPS).then_inc(setup_g, 1)
            nc.gpsimd.memset(var_mul[:, 1:2], 1.0).then_inc(setup_g, 1)
            nc.gpsimd.memset(var_add[:, 0:1], LN_EPS * LN_EPS).then_inc(setup_g, 1)
            nc.gpsimd.memset(var_add[:, 1:3], LN_EPS).then_inc(setup_g, 1)
            nc.gpsimd.memset(lift_bias[:, :], 0.5 * LN_LIFT * LN2).then_inc(setup_g, 1)
            pool.wait_ge(ld_w, N_W)
            pool.wait_ge(setup_g, SETUP_G)

            def run(j, par, inside=False):
                if inside or j > -3:
                    pool.wait_ge(rs_ready, j + 3)
                if has(j + 3, inside):
                    pool.wait_ge(xc_mv, j + 4)
                    nc.gpsimd.tensor_tensor(var_tmp[:, :], xc_stat[:, 1 - par, :, 1], var_mul[:, :],
                                            ALU.mult).then_inc(var_t, 1)
                    pool.wait_ge(var_t, j + 4)
                    last = nc.gpsimd.tensor_tensor(var_in[:, 24:26], var_tmp[:, :], var_add[:, 0:2], ALU.add)
                if has(j - 2, inside):
                    pool.wait_ge(o_mv, j - 1)
                    last = nc.gpsimd.tensor_tensor(var_in[:, 26:27], o_stat[:, par, 1:2], var_add[:, 2:3], ALU.add)
                last.then_inc(var_ready, 1)
                pool.wait_ge(y0_done, j + 4)
                nc.gpsimd.tensor_tensor(rs_t1[:, :], rs_y0[:, :], rs_y0[:, :], ALU.mult).then_inc(nwt, 1)
                nc.gpsimd.tensor_scalar(rs_t3[:, :], rs_y0[:, :], -0.5, None, ALU.mult).then_inc(nwt, 1)
                pool.wait_ge(nwt, 4 * (j + 3) + 1)
                nc.gpsimd.tensor_tensor(rs_t2[:, :], rs_t1[:, :], var_in[:, :], ALU.mult).then_inc(nwt, 1)
                if has(j - 1, inside):
                    pool.wait_ge(scaled, j)
                if inside or -1 <= j < B - 1:
                    pool.wait_ge(hat_ready, j + 2)
                if inside or j > 3:
                    pool.wait_ge(x1_done, j - 3)
                pool.wait_ge(nwt, 4 * (j + 3) + 3)
                nc.gpsimd.tensor_tensor(rs_t4[:, :], rs_t2[:, :], three[:, :], ALU.subtract).then_inc(nwt, 1)
                pool.wait_ge(nwt, 4 * (j + 3) + 4)
                nc.gpsimd.tensor_tensor(rstd[:, par, :], rs_t4[:, :], rs_t3[:, :], ALU.mult).then_inc(rs_ready, 1)
                if has(j + 2, inside):
                    pool.wait_ge(hi_done, j + 3)
                    nc.gpsimd.tensor_tensor(xc_lo[:, par, :, :], xc_t[:, par, :, :],
                                            xc_hi[:, par, :, :].bitcast(F32), ALU.subtract).then_inc(lo_done, 1)
                if has(j, inside):
                    if inside or j > 0:
                        pool.wait_ge(exp_done, 4 * j)
                    if inside or j > 1:
                        pool.wait_ge(x1_done, j - 1)
                    nc.gpsimd.tensor_tensor(x_b[:, par, :], x_res[:, bass.ds(j, 1), 0:D].rearrange("p a d -> p (a d)"),
                                            lno_b[:, :], ALU.add).then_inc(xb_done, 1)
                if has(j + 1, inside):
                    if not has(j, inside):
                        pool.wait_ge(setup_v, SETUP_V)
                    nc.gpsimd.tensor_copy(mask_now[:, 1 - par:2 - par], mask_bias[:, bass.ds(j + 1, 1)]).then_inc(mask_set, 1)

            rounds(run, pool)

        @block.vector
        def _(dve):
            dve.wait_ge(ld_w, N_W)
            nc.vector.tensor_copy(w_hi[:, :], w_raw[:, :]).then_inc(setup_v, 1)
            nc.vector.tensor_tensor(qk_prod[:, :], qs_b[:, :], ks_b[:, :], ALU.mult).then_inc(setup_v, 1)
            dve.wait_ge(setup_p, 5)
            nc.vector.tensor_copy(mask_f[0:B, 0:M], mask_raw[0:B, 0:M]).then_inc(setup_v, 1)
            dve.wait_ge(setup_v, 3)
            nc.vector.tensor_tensor(w_lo[:, :], w_raw[:, :], w_hi[:, :].bitcast(F32), ALU.subtract).then_inc(setup_v, 1)
            nc.vector.tensor_reduce(qk_max[:, :], qk_prod[:, :], AX, ALU.max,
                                    apply_absolute_value=True).then_inc(setup_v, 1)
            nc.vector.tensor_tensor(scale_col[:, 3:4], scale_col[:, 0:1], scale_col[:, 1:2],
                                    ALU.mult).then_inc(setup_v, 1)
            dve.wait_ge(setup_v, 6)
            nc.vector.tensor_scalar(scale_col[:, 2:3], scale_col[:, 3:4], SIM_SCALE, None, ALU.mult).then_inc(setup_v, 1)
            nc.vector.tensor_scalar(neg_shift[:, :], qk_max[:, :], -SIM_SCALE, EXP_ROOM, ALU.mult,
                                    ALU.add).then_inc(setup_v, 1)
            dve.wait_ge(setup_v, 8)
            nc.vector.tensor_scalar(neg_shift[:, :], neg_shift[:, :], 0.0, None, ALU.min).then_inc(setup_v, 1)
            dve.wait_ge(s_maskT, 1)
            nc.vector.tensor_scalar(mask_bias[:, :], ps[:, 7, 0:P], 1.0, -MASKED, ALU.subtract,
                                    ALU.mult).then_inc(setup_v, 1)
            dve.wait_ge(setup_v, 10)
            nc.vector.tensor_copy(x_res[:, :, D + 2:D + 3], ids[:, :].unsqueeze(2)).then_inc(setup_v, 1)
            nc.vector.tensor_scalar(mask_bias[:, :], mask_bias[:, :], neg_shift[:, 0:1], None,
                                    ALU.add).then_inc(setup_v, 1)

            def run(j, par, inside=False):
                if has(j + 3, inside):
                    dve.wait_ge(tokens_in, j + 4)
                    if inside or j > -3:
                        dve.wait_ge(xc_mv, j + 3)
                    if inside or j > -2:
                        dve.wait_ge(hat_ready, j + 2)
                        dve.wait_ge(var_ready, j + 3)
                    for n, res in enumerate((x_res, ctx_res)):
                        last = nc.vector.bn_stats(bn6[:, n, :], res[:, bass.ds(j + 3, 1), 0:D].rearrange("p a d -> p (a d)"))
                    last.then_inc(xc_bn, 1)
                if has(j, inside):
                    if has(j + 3, inside):
                        dve.wait_ge(xc_bn, j + 4)
                    if inside or j > 0:
                        dve.wait_ge(sim_done, 4 * j)
                    for kt in (0, 1):
                        dve.wait_ge(qkT_done, 3 * j + 2 + kt)
                        nc.vector.tensor_copy(k_t[:, kt, :], ps_qk[:, 1 + kt, :]).then_inc(kt_done, 1)
                elif has(j + 3, inside):
                    dve.wait_ge(xc_bn, j + 4)
                if has(j + 3, inside):
                    for n in (0, 1):
                        last = nc.vector.bn_aggr(xc_stat[:, 1 - par, n, :], bn6[:, n, :])
                    last.then_inc(xc_mv, 1)
                if has(j - 1, inside):
                    if inside or j > 1:
                        dve.wait_ge(onT_done, j - 1)
                    dve.wait_ge(pv_done, j)
                    nc.vector.reciprocal(rden[:, 0:H - 1], ps_pv[:, :, DH])
                    nc.vector.reciprocal(rden[:, H - 1:H], ps_pv7[:, DH:DH + 1]).then_inc(rl_done, 1)
                    dve.wait_ge(rl_done, j)
                    nc.vector.tensor_tensor(o_n[:, 0:(H - 1) * DH].rearrange("p (h d) -> p h d", d=DH),
                                            ps_pv[:, :, 0:DH],
                                            rden[:, 0:H - 1].unsqueeze(2).to_broadcast([P, H - 1, DH]), ALU.mult)
                    nc.vector.tensor_scalar(o_n[:, (H - 1) * DH:INNER], ps_pv7[:, 0:DH], rden[:, H - 1:H], None,
                                            ALU.mult).then_inc(on_done, 1)
                if has(j + 1, inside):
                    if inside or j > -1:
                        dve.wait_ge(ss_done, j + 1)
                    for n in range(3):
                        dve.wait_ge(sq_done, 3 * j + 4 + n)
                        nc.vector.reduce_sum(sumsq[:, n * H:(n + 1) * H],
                                             sq[:, n * INNER:(n + 1) * INNER].rearrange("p (h d) -> p h d", d=DH),
                                             AX).then_inc(ss_raw, 1)
                    dve.wait_ge(ss_raw, 3 * j + 6)
                    if inside or j > -3:
                        dve.wait_ge(rs_ready, j + 3)
                    nc.vector.tensor_scalar(var_in[:, 0:3 * H], sumsq[:, :], L2_EPS * L2_EPS, None,
                                            ALU.max).then_inc(ss_done, 1)
                dve.wait_ge(rs_ready, j + 4)
                if has(j + 1, inside):
                    if inside or j > -1:
                        dve.wait_ge(qkT_done, 3 * j + 3)
                    for n in range(3):
                        nc.vector.tensor_tensor(qk_hat[:, n * INNER:(n + 1) * INNER].rearrange("p (h d) -> p h d", d=DH),
                                                ps_qk[:, n, :].rearrange("p (h d) -> p h d", d=DH),
                                                rstd[:, par, n * H:(n + 1) * H].unsqueeze(2).to_broadcast([P, H, DH]),
                                                ALU.mult).then_inc(scaled, 1)
                if has(j + 3, inside):
                    if inside or j > -2:
                        dve.wait_ge(xcT_done, j + 2)
                    for n, res in enumerate((x_res, ctx_res)):
                        last = nc.vector.tensor_scalar(xc_hat[:, 1 - par, n, :],
                                                       res[:, bass.ds(j + 3, 1), 0:D].rearrange("p a d -> p (a d)"),
                                                       xc_stat[:, 1 - par, n, 0:1], rstd[:, par, 24 + n:25 + n],
                                                       ALU.subtract, ALU.mult)
                    last.then_inc(hat_ready, 1)
                if has(j - 2, inside):
                    dve.wait_ge(o_cent, j - 1)
                    dve.wait_ge(xb_done, j - 1)
                    nc.vector.scalar_tensor_tensor(x_res[:, bass.ds(j - 2, 1), 0:D].rearrange("p a d -> p (a d)"),
                                                   o_c[:, par, :], rstd[:, par, 26:27], x_b[:, par, :],
                                                   ALU.mult, ALU.add).then_inc(x1_done, 1)
                if has(j - 1, inside):
                    dve.wait_ge(wo_done, j)
                    if has(j + 2, inside):
                        dve.wait_ge(xcT_done, j + 3)
                    if inside or j > 1:
                        dve.wait_ge(o_mv, j - 1)
                    nc.vector.bn_stats(o6[:, :], ps_o).then_inc(o_bn, 1)
                    if inside or j > 2:
                        dve.wait_ge(var_ready, j + 3)
                        dve.wait_ge(x1_done, j - 2)
                    dve.wait_ge(o_bn, j)
                if has(j + 2, inside):
                    if inside or j > -1:
                        dve.wait_ge(lo_done, j + 1)
                    dve.wait_ge(xcT_done, j + 3)
                    for n in (0, 1):
                        last = nc.vector.tensor_scalar(xc_t[:, par, n, :], ps_xc[:, n * P:(n + 1) * P],
                                                       ln_cols[:, 2 * n:2 * n + 1], ln_cols[:, 2 * n + 1:2 * n + 2],
                                                       ALU.mult, ALU.add)
                    last.then_inc(xct_sb, 1)
                if has(j - 1, inside):
                    nc.vector.bn_aggr(o_stat[:, 1 - par, :], o6[:, :]).then_inc(o_mv, 1)
                    dve.wait_ge(o_mv, j)
                    nc.vector.scalar_tensor_tensor(o_c[:, 1 - par, :], ps_o, o_stat[:, 1 - par, 0:1],
                                                   lno_w[:, :], ALU.subtract, ALU.mult).then_inc(o_cent, 1)

            rounds(run, dve)

        @block.tensor
        def _(pe):
            pe.wait_ge(setup_g, SETUP_G)
            pe.wait_ge(setup_v, 3)
            nc.tensor.transpose(ps[:, 7, 0:P], mask_f[:, :], ident[:, :]).then_inc(s_maskT, 1)
            pe.wait_ge(setup_v, SETUP_V)

            def product(dst, tok_hi, tok_lo, w):
                nc.tensor.matmul(dst, tok_hi, w_hi[:, w:w + INNER], start=True, stop=False)
                nc.tensor.matmul(dst, tok_hi, w_lo[:, w:w + INNER], start=False, stop=False)
                return nc.tensor.matmul(dst, tok_lo, w_hi[:, w:w + INNER], start=False, stop=True)

            def run(j, par, inside=False):
                if has(j, inside):
                    for n in range(3):
                        pe.wait_ge(scaled, 3 * j + 1 + n)
                        for t in range(PAIRS):
                            last = nc.tensor.transpose(ps_qk[:, n, t * P:(t + 1) * P],
                                                       qk_hat[:, n * INNER + t * P:n * INNER + (t + 1) * P], ident[:, :])
                        last.then_inc(qkT_done, 1)
                if has(j - 1, inside):
                    pe.wait_ge(v_copied, 2 * j)
                    pe.wait_ge(exp_done, 4 * j)
                    for h in range(H):
                        if h == H - 1 and has(j + 1, inside):
                            pe.wait_ge(xct_sb, j + 2)
                        if h == H - 1 and has(j - 2, inside):
                            pe.wait_ge(o_cent, j - 1)
                        dst = ps[:, 6, h * (DH + 1):h * (DH + 1) + VW] if h < H - 1 else ps[:, 7, 3 * P:3 * P + VW]
                        for kt in (0, 1):
                            last = nc.tensor.matmul(dst, prob[:, kt, h * P:(h + 1) * P], v_sb[:, kt, h, :],
                                                    start=kt == 0, stop=kt == 1)
                    last.then_inc(pv_done, 1)
                if has(j, inside):
                    for kt in (0, 1):
                        last = product(ps_v[kt], xc_hi[:, par, kt, :], xc_lo[:, par, kt, :], 2 * INNER)
                        last.then_inc(v_done, 1)
                if has(j + 1, inside):
                    pe.wait_ge(hi_done, j + 2)
                    pe.wait_ge(lo_done, j + 2)
                    for n, (src, w) in enumerate(((0, 0), (0, INNER), (1, INNER))):
                        if has(j, inside):
                            if n == 0:
                                pe.wait_ge(qbd_done, j + 1)
                            else:
                                pe.wait_ge(kt_done, 2 * j + n)
                        last = product(ps_qk[:, n, :], xc_hi[:, 1 - par, src, :], xc_lo[:, 1 - par, src, :], w)
                        last.then_inc(qk_done, 1)
                if has(j - 1, inside):
                    pe.wait_ge(on_done, j)
                    for t in range(PAIRS):
                        last = nc.tensor.transpose(ps_ot[:, t * P:(t + 1) * P], o_n[:, t * P:(t + 1) * P], ident[:, :])
                    last.then_inc(onT_done, 1)
                if has(j + 2, inside):
                    pe.wait_ge(hat_ready, j + 3)
                    if has(j - 1, inside):
                        pe.wait_ge(on_done, j)
                    elif j > -2:
                        pe.wait_ge(xct_sb, j + 2)
                    for n in (0, 1):
                        last = nc.tensor.transpose(ps_xc[:, n * P:(n + 1) * P], xc_hat[:, par, n, :], ident[:, :])
                    last.then_inc(xcT_done, 1)
                def scores(units):
                    for n in units:
                        if n < 2:
                            pe.wait_ge(v_copied, 2 * j + n + 1)
                        elif n == 2:
                            if inside or j > 0:
                                pe.wait_ge(ot_done, j)
                        else:
                            pe.wait_ge(exp_done, 4 * j + 1)
                        for t in (0, 1):
                            pair = n % 2 * 2 + t
                            last = nc.tensor.matmul(ps_s[n][:, t * 2 * P:(t + 1) * 2 * P],
                                                    k_t[:, n // 2, pair * P:(pair + 1) * P],
                                                    q_bd[:, pair, :, :].rearrange("p a q -> p (a q)"),
                                                    start=True, stop=True)
                        last.then_inc(sim_done, 1)

                if has(j, inside):
                    if not has(j + 1, inside):
                        pe.wait_ge(qbd_done, j + 1)
                    pe.wait_ge(kt_done, 2 * j + 2)
                    scores((0, 1))
                if has(j - 1, inside):
                    pe.wait_ge(ot_done, j)
                    for t in range(PAIRS):
                        last = nc.tensor.matmul(ps_o, o_t[:, t * P:(t + 1) * P], wo_sb[:, t, :],
                                                start=t == 0, stop=t == PAIRS - 1)
                    last.then_inc(wo_done, 1)
                if has(j, inside):
                    scores((2, 3))

            rounds(run, pe)


def ffn_xattn_route(nc, x_res, ctx_res, ident, logits, weight_q, weight_scale, bias, We, W2, Wr, B, D, E):
    NG = B // G
    L = 3 * G
    with ExitStack() as stack:
        def sb(name, shape, dt=F32):
            return stack.enter_context(nc.sbuf_tensor(name, shape, dt))

        def sem(name):
            return stack.enter_context(nc.semaphore(name))

        wq_raw = sb("wq_raw", [P, D], I8)
        wq_f = sb("wq_f", [P, D])
        wq_t = sb("wq_t", [P, D], BF16)
        we_raw = sb("we_raw", [P, D])
        w2_raw = sb("w2_raw", [P, D])
        we_t = sb("we_t", [P, D])
        w2_t = sb("w2_t", [P, D])
        wr_t = sb("wr_t", [P, E])
        ws_b = sb("ws_b", [P, D])
        bias_b = sb("bias_b", [P, D])
        ident_bf = sb("ident_bf", [P, P], BF16)
        eps_t = sb("eps_t", [P, L])
        lift2 = sb("lift2", [P, 1])
        three2 = sb("three2", [P, L])
        bn = sb("bn", [P, L, 6])
        stat = sb("stat", [P, 2, L, 2])
        g_var = sb("g_var", [P, L])
        g_ln = sb("g_ln", [P, L])
        g_y0 = sb("g_y0", [P, L])
        g_y2 = sb("g_y2", [P, L])
        g_half = sb("g_half", [P, L])
        g_vy = sb("g_vy", [P, L])
        g_r = sb("g_r", [P, L])
        g_rstd = sb("g_rstd", [P, 2, L])
        t_a = sb("t_a", [P, G, D])
        amax = sb("amax", [P, G])
        q_step = sb("q_step", [P, G])
        q_inv = sb("q_inv", [P, G])
        q_round = sb("q_round", [P, G, D])
        q_bf = sb("q_bf", [P, G, D], BF16)
        q_t = sb("q_t", [P, G, P], BF16)
        xb = sb("xb", [P, G, D])
        y_a = sb("y_a", [P, G, D])
        t_b = sb("t_b", [P, G, D])
        tb_t = sb("tb_t", [P, G, P])
        ctx_now = sb("ctx_now", [P, G, D])
        ctx_t = sb("ctx_t", [P, G, P])
        ke_t = sb("ke_t", [P, G, P])
        smax = sb("smax", [P, G])
        nmax = sb("nmax", [P, G])
        probs = sb("probs", [P, G, P])
        ssum = sb("ssum", [P, G])
        sinv = sb("sinv", [P, G])
        v_s = sb("v_s", [P, G, D])
        c_cent = sb("c_cent", [P, G, D])
        t_c = sb("t_c", [P, G, D])
        tc_t = sb("tc_t", [P, G, P])

        ps = stack.enter_context(nc.psum_tensor("ps2", [P, 7, 512], F32))
        ps_q = stack.enter_context(nc.psum_tensor("ps_q", [P, 1024], BF16))
        ps_ctx, ps_ke, ps_v, ps_acc, ps_t, ps_s, ps_o = (
            ps[:, n, :].rearrange("p (g d) -> p g d", d=D) for n in range(7))
        ps_qt = ps_q[:, 0:G * P].rearrange("p (g d) -> p g d", d=P)
        ps_lg = ps_q[:, 512:512 + 2 * G * E].bitcast(F32)

        names = ("ld", "setup_g", "setup_v", "setup_t", "setup_c", "a_stats", "a_aggr", "a_var", "a_ln", "a_y0",
                 "a_n1", "a_n2", "a_n3", "a_rs", "ta_done", "amax_done", "step_done", "inv_done", "q1_done", "q2_done", "qT_done",
                 "qt_copied", "acc_done", "ya_done", "xb2_done", "x2_done", "tb_done", "tbT_done", "tb_copied",
                 "ctxT_done", "ctx_copied", "ke_done", "ke_copied", "v2_done", "sc_done", "smax_done",
                 "nmax_done", "pr_done", "sinv_done", "vs_done", "out_done", "x3_done", "cc_done", "tc_done",
                 "tcT_done", "tc_copied", "lg_done", "lg_copied", "cols_done", "ctx_taken")
        s = {n: sem("m_" + n) for n in names}

        FIRST = 6

        def rounds(run, eng):
            for j in range(FIRST):
                run(j, j % 2)
            with eng.Fori(0, (NG - FIRST) // 2) as turn:
                run(FIRST + 2 * turn, 0, True)
                run(FIRST + 1 + 2 * turn, 1, True)
            for j in range(NG, NG + 5):
                run(j, j % 2)

        def has(g, inside):
            return inside or 0 <= g < NG

        def after(eng, name, g, inside):
            if inside or g >= 0:
                eng.wait_ge(s[name], (g if inside else min(g, NG - 1)) + 1)

        def grp(res, g, w=slice(0, D)):
            return res[:, bass.ds(G * g, G), w]

        def one(res, g, i):
            return res[:, bass.ds(G * g + i, 1), 0:D].rearrange("p a d -> p (a d)")

        block = stack.enter_context(nc.Block())

        @block.sync
        def _(sp):
            sp.dma_start(wq_raw[:, :], weight_q).then_inc(s["ld"], 16)
            sp.dma_start(we_raw[:, :], We).then_inc(s["ld"], 16)
            sp.dma_start(w2_raw[:, :], W2).then_inc(s["ld"], 16)
            sp.dma_start(wr_t[:, :], Wr.rearrange("e d -> d e"), allow_slow_non_contiguous=True).then_inc(s["ld"], 16)
            sp.dma_start(ws_b[:, :], weight_scale.partition_broadcast(P)).then_inc(s["ld"], 16)
            sp.dma_start(bias_b[:, :], bias.partition_broadcast(P)).then_inc(s["ld"], 16)
            sp.wait_ge(s["ld"], 96)

        @block.scalar
        def _(act):
            act.wait_ge(s["setup_t"], 1)
            nc.scalar.activation(wq_t[:, :], ps_ctx[:, 0, :], ACT.Copy).then_inc(s["setup_c"], 1)
            nc.scalar.activation(we_t[:, :], ps_ctx[:, 1, :], ACT.Copy).then_inc(s["setup_c"], 1)
            nc.scalar.activation(w2_t[:, :], ps_ctx[:, 2, :], ACT.Copy).then_inc(s["setup_c"], 1)
            act.wait_ge(s["setup_g"], 3)
            nc.scalar.preload_act_table_set("natural_log_exp_and_others")

            def run(j, par, inside=False):
                if has(j - 2, inside):
                    after(act, "sinv_done", j - 2, inside)
                    after(act, "v2_done", j - 2, inside)
                    after(act, "out_done", j - 3, inside)
                    for i in range(G):
                        last = nc.scalar.activation(v_s[:, i, :], ps_v[:, i, :], ACT.Copy, scale=sinv[:, i:i + 1])
                    last.then_inc(s["vs_done"], 1)
                if has(j, inside) or has(j - 1, inside) or has(j - 3, inside):
                    act.wait_ge(s["a_var"], j + 1)
                    after(act, "a_rs", j - 1, inside)
                    nc.scalar.activation(g_ln[:, :], g_var[:, :], ACT.Ln, scale=float(2 ** LN_LIFT)).then_inc(s["a_ln"], 1)
                    act.wait_ge(s["a_ln"], j + 1)
                    nc.scalar.activation(g_y0[:, :], g_ln[:, :], ACT.Exp, scale=-0.5, bias=lift2[:, 0:1]).then_inc(s["a_y0"], 1)
                if has(j - 1, inside):
                    after(act, "ctxT_done", j - 1, inside)
                    after(act, "v2_done", j - 2, inside)
                    nc.scalar.activation(ctx_t[:, :, :], ps_ctx, ACT.Copy).then_inc(s["ctx_copied"], 1)
                if has(j - 1, inside):
                    after(act, "tbT_done", j - 1, inside)
                    after(act, "sc_done", j - 2, inside)
                    nc.scalar.activation(tb_t[:, :, :], ps_t, ACT.Copy).then_inc(s["tb_copied"], 1)
                if has(j - 1, inside):
                    after(act, "ke_done", j - 1, inside)
                    after(act, "sc_done", j - 2, inside)
                    nc.scalar.activation(ke_t[:, :, :], ps_ke, ACT.Copy).then_inc(s["ke_copied"], 1)
                if has(j, inside):
                    after(act, "qT_done", j, inside)
                    after(act, "acc_done", j - 1, inside)
                    nc.scalar.activation(q_t[:, :, :], ps_qt, ACT.Copy).then_inc(s["qt_copied"], 1)
                if has(j - 3, inside):
                    after(act, "tcT_done", j - 3, inside)
                    after(act, "lg_done", j - 4, inside)
                    nc.scalar.activation(tc_t[:, :, :], ps_t, ACT.Copy).then_inc(s["tc_copied"], 1)
                if has(j - 1, inside):
                    after(act, "nmax_done", j - 1, inside)
                    after(act, "out_done", j - 2, inside)
                    after(act, "sinv_done", j - 2, inside)
                    for i in range(G):
                        last = nc.scalar.activation(probs[:, i, :], ps_s[:, i, :], ACT.Exp, bias=nmax[:, i:i + 1],
                                                    accum_out=ssum[:, i:i + 1])
                    last.then_inc(s["pr_done"], 1)

            rounds(run, act)

        @block.gpsimd
        def _(pool):
            nc.gpsimd.memset(eps_t[:, :], LN_EPS).then_inc(s["setup_g"], 1)
            nc.gpsimd.memset(three2[:, :], 3.0).then_inc(s["setup_g"], 1)
            nc.gpsimd.memset(lift2[:, :], 0.5 * LN_LIFT * LN2).then_inc(s["setup_g"], 1)
            pool.wait_ge(s["setup_g"], 3)
            pool.wait_ge(s["ld"], 96)
            pool.wait_ge(s["setup_v"], 3)

            def run(j, par, inside=False):
                if has(j, inside) or has(j - 1, inside) or has(j - 3, inside):
                    after(pool, "a_rs", j - 1, inside)
                    pool.wait_ge(s["a_aggr"], j + 1)
                    nc.gpsimd.tensor_tensor(g_var[:, :], stat[:, par, :, 1], eps_t[:, :], ALU.add).then_inc(s["a_var"], 1)
                if has(j, inside) or has(j - 1, inside) or has(j - 3, inside):
                    pool.wait_ge(s["a_y0"], j + 1)
                    nc.gpsimd.tensor_tensor(g_y2[:, :], g_y0[:, :], g_y0[:, :], ALU.mult)
                    nc.gpsimd.tensor_scalar(g_half[:, :], g_y0[:, :], -0.5, None, ALU.mult).then_inc(s["a_n1"], 1)
                    pool.wait_ge(s["a_n1"], j + 1)
                    nc.gpsimd.tensor_tensor(g_vy[:, :], g_y2[:, :], g_var[:, :], ALU.mult).then_inc(s["a_n2"], 1)
                    pool.wait_ge(s["a_n2"], j + 1)
                    nc.gpsimd.tensor_tensor(g_r[:, :], g_vy[:, :], three2[:, :], ALU.subtract).then_inc(s["a_n3"], 1)
                    pool.wait_ge(s["a_n3"], j + 1)
                    after(pool, "tb_done", j - 3, inside)
                    after(pool, "ta_done", j - 2, inside)
                    after(pool, "cols_done", j - 5, inside)
                    nc.gpsimd.tensor_tensor(g_rstd[:, par, :], g_r[:, :], g_half[:, :], ALU.mult).then_inc(s["a_rs"], 1)
                if has(j - 3, inside):
                    after(pool, "tc_done", j - 4, inside)
                    pool.wait_ge(s["a_rs"], j + 1)
                    nc.gpsimd.tensor_tensor(c_cent[:, :, :], grp(x_res, j - 3),
                                            stat[:, par, 2 * G:L, 0:1].to_broadcast([P, G, D]), ALU.subtract).then_inc(s["cc_done"], 1)
                    after(pool, "cc_done", j - 3, inside)
                    after(pool, "tcT_done", j - 4, inside)
                    nc.gpsimd.tensor_tensor(t_c[:, :, :], c_cent[:, :, :],
                                            g_rstd[:, par, 2 * G:L].unsqueeze(2).to_broadcast([P, G, D]), ALU.mult).then_inc(s["tc_done"], 1)
                if has(j, inside):
                    after(pool, "x2_done", j - 1, inside)
                    nc.gpsimd.tensor_tensor(xb[:, :, :], grp(x_res, j),
                                            bias_b[:, :].unsqueeze(1).to_broadcast([P, G, D]), ALU.add).then_inc(s["xb2_done"], 1)

            rounds(run, pool)

        @block.vector
        def _(dve):
            dve.wait_ge(s["ld"], 96)
            nc.vector.tensor_copy(wq_f[:, :], wq_raw[:, :]).then_inc(s["setup_v"], 1)
            nc.vector.tensor_copy(ident_bf[:, :], ident[:, :]).then_inc(s["setup_v"], 1)
            nc.vector.memset(stat[:, :, :, :], 1.0).then_inc(s["setup_v"], 1)
            dve.wait_ge(s["setup_v"], 3)

            def run(j, par, inside=False):
                kinds = [(n, g) for n, g in ((0, j), (1, j - 1), (2, j - 3)) if has(g, inside)]
                live = bool(kinds)
                if live:
                    after(dve, "a_aggr", j - 1, inside)
                    after(dve, "x2_done", j - 1, inside)
                    after(dve, "x3_done", j - 3, inside)
                    for n, g in kinds:
                        for i in range(G):
                            last = nc.vector.bn_stats(bn[:, n * G + i, :], one(x_res, g, i))
                    last.then_inc(s["a_stats"], 1)
                if live:
                    after(dve, "tc_done", j - 5, inside)
                    after(dve, "cols_done", j - 5, inside)
                    after(dve, "a_var", j - 2, inside)
                    dve.wait_ge(s["a_stats"], j + 1)
                if has(j - 2, inside):
                    after(dve, "vs_done", j - 3, inside)
                    after(dve, "pr_done", j - 2, inside)
                    nc.vector.reciprocal(sinv[:, :], ssum[:, :]).then_inc(s["sinv_done"], 1)
                if live:
                    for n, g in kinds:
                        for i in range(G):
                            last = nc.vector.bn_aggr(stat[:, par, n * G + i, :], bn[:, n * G + i, :])
                    last.then_inc(s["a_aggr"], 1)
                if has(j - 4, inside):
                    after(dve, "lg_done", j - 4, inside)
                    nc.vector.tensor_copy(logits[:, bass.ds(G * (j - 4), G), :],
                                          ps_lg.rearrange("p (g e) -> p g e", e=E)).then_inc(s["lg_copied"], 1)
                if has(j - 1, inside):
                    after(dve, "ctxT_done", j - 2, inside)
                    nc.vector.tensor_copy(ctx_now[:, :, :], grp(ctx_res, j - 1)).then_inc(s["ctx_taken"], 1)
                if live:
                    dve.wait_ge(s["a_rs"], j + 1)
                if has(j - 1, inside):
                    after(dve, "tbT_done", j - 2, inside)
                    for i in range(G):
                        last = nc.vector.tensor_scalar(t_b[:, i, :], one(x_res, j - 1, i), stat[:, par, G + i, 0:1],
                                                       g_rstd[:, par, G + i:G + i + 1], ALU.subtract, ALU.mult)
                    last.then_inc(s["tb_done"], 1)
                if has(j, inside):
                    after(dve, "q1_done", j - 1, inside)
                    for i in range(G):
                        last = nc.vector.tensor_scalar(t_a[:, i, :], one(x_res, j, i), stat[:, par, i, 0:1],
                                                       g_rstd[:, par, i:i + 1], ALU.subtract, ALU.mult)
                    last.then_inc(s["ta_done"], 1)
                    after(dve, "ta_done", j, inside)
                    nc.vector.tensor_reduce(amax[:, :], t_a[:, :, :], AX, ALU.max, apply_absolute_value=True).then_inc(s["amax_done"], 1)
                if has(j - 2, inside):
                    after(dve, "out_done", j - 2, inside)
                    nc.vector.tensor_tensor(grp(x_res, j - 2), grp(x_res, j - 2), ps_o, ALU.add).then_inc(s["x3_done"], 1)
                if has(j, inside):
                    after(dve, "amax_done", j, inside)
                    after(dve, "ya_done", j - 1, inside)
                    nc.vector.tensor_scalar(q_step[:, :], amax[:, :], Q_EPS, 1.0 / Q_MAX, ALU.max, ALU.mult).then_inc(s["step_done"], 1)
                    after(dve, "step_done", j, inside)
                    nc.vector.reciprocal(q_inv[:, :], q_step[:, :]).then_inc(s["inv_done"], 1)
                if has(j - 3, inside):
                    nc.vector.tensor_copy(grp(x_res, j - 3, slice(D, D + 1)), stat[:, par, 2 * G:L, 0:1])
                    nc.vector.tensor_copy(grp(x_res, j - 3, slice(D + 1, D + 2)),
                                          g_rstd[:, par, 2 * G:L].unsqueeze(2)).then_inc(s["cols_done"], 1)
                if has(j, inside):
                    after(dve, "inv_done", j, inside)
                    after(dve, "q2_done", j - 1, inside)
                    for i in range(G):
                        last = nc.vector.tensor_scalar(q_round[:, i, :], t_a[:, i, :], q_inv[:, i:i + 1], ROUND,
                                                       ALU.mult, ALU.add)
                    last.then_inc(s["q1_done"], 1)
                    after(dve, "q1_done", j, inside)
                    after(dve, "qT_done", j - 1, inside)
                    nc.vector.tensor_scalar(q_bf[:, :, :], q_round[:, :, :], ROUND, Q_MAX, ALU.subtract,
                                            ALU.min).then_inc(s["q2_done"], 1)
                if has(j - 1, inside):
                    after(dve, "sc_done", j - 1, inside)
                    nc.vector.reduce_max(smax[:, :], ps_s, AX).then_inc(s["smax_done"], 1)
                    after(dve, "smax_done", j - 1, inside)
                    after(dve, "pr_done", j - 2, inside)
                    nc.vector.tensor_scalar(nmax[:, :], smax[:, :], -1.0, None, ALU.mult).then_inc(s["nmax_done"], 1)
                if has(j, inside):
                    after(dve, "acc_done", j, inside)
                    after(dve, "x2_done", j - 1, inside)
                    for i in range(G):
                        last = nc.vector.scalar_tensor_tensor(y_a[:, i, :], ps_acc[:, i, :], q_step[:, i:i + 1],
                                                              ws_b[:, :], ALU.mult, ALU.mult)
                    last.then_inc(s["ya_done"], 1)
                    after(dve, "ya_done", j, inside)
                    after(dve, "xb2_done", j, inside)
                    nc.vector.tensor_tensor(grp(x_res, j), y_a[:, :, :], xb[:, :, :], ALU.add).then_inc(s["x2_done"], 1)

            rounds(run, dve)

        @block.tensor
        def _(pe):
            pe.wait_ge(s["setup_v"], 2)
            pe.wait_ge(s["ld"], 96)
            nc.tensor.transpose(ps_ctx[:, 0, :], wq_f[:, :], ident[:, :])
            nc.tensor.transpose(ps_ctx[:, 1, :], we_raw[:, :], ident[:, :])
            nc.tensor.transpose(ps_ctx[:, 2, :], w2_raw[:, :], ident[:, :]).then_inc(s["setup_t"], 1)
            pe.wait_ge(s["setup_c"], 3)

            def run(j, par, inside=False):
                if has(j - 2, inside):
                    after(pe, "vs_done", j - 2, inside)
                    after(pe, "x3_done", j - 3, inside)
                    for i in range(G):
                        last = nc.tensor.matmul(ps_o[:, i, :], probs[:, i, :], v_s[:, i, :], start=True, stop=True)
                    last.then_inc(s["out_done"], 1)
                if has(j - 1, inside):
                    after(pe, "ctx_taken", j - 1, inside)
                    after(pe, "ctx_copied", j - 2, inside)
                    for i in range(G):
                        last = nc.tensor.transpose(ps_ctx[:, i, :], ctx_now[:, i, :], ident[:, :])
                    last.then_inc(s["ctxT_done"], 1)
                if has(j - 1, inside):
                    after(pe, "tb_done", j - 1, inside)
                    after(pe, "tc_copied", j - 4, inside)
                    for i in range(G):
                        last = nc.tensor.transpose(ps_t[:, i, :], t_b[:, i, :], ident[:, :])
                    last.then_inc(s["tbT_done"], 1)
                if has(j - 1, inside):
                    after(pe, "ctx_copied", j - 1, inside)
                    after(pe, "ke_copied", j - 2, inside)
                    nc.tensor.matmul(ps[:, 1, :], we_t[:, :], ctx_t[:, :, :].rearrange("p g m -> p (g m)"),
                                     start=True, stop=True).then_inc(s["ke_done"], 1)
                if has(j - 1, inside):
                    after(pe, "tb_copied", j - 1, inside)
                    after(pe, "ke_copied", j - 1, inside)
                    after(pe, "pr_done", j - 2, inside)
                    for i in range(G):
                        last = nc.tensor.matmul(ps_s[:, i, :], ke_t[:, i, :], tb_t[:, i, :], start=True, stop=True)
                    last.then_inc(s["sc_done"], 1)
                if has(j, inside):
                    after(pe, "q2_done", j, inside)
                    after(pe, "lg_copied", j - 4, inside)
                    for i in range(G):
                        last = nc.tensor.transpose(ps_qt[:, i, :], q_bf[:, i, :], ident_bf[:, :])
                    last.then_inc(s["qT_done"], 1)
                if has(j, inside):
                    after(pe, "qt_copied", j, inside)
                    for i in range(G):
                        last = nc.tensor.matmul(ps_acc[:, i, :], q_t[:, i, :], wq_t[:, :], start=True, stop=True)
                    last.then_inc(s["acc_done"], 1)
                if has(j - 1, inside):
                    after(pe, "vs_done", j - 2, inside)
                    for i in range(G):
                        last = nc.tensor.matmul(ps_v[:, i, :], ctx_t[:, i, :], w2_t[:, :], start=True, stop=True)
                    last.then_inc(s["v2_done"], 1)
                if has(j - 3, inside):
                    after(pe, "tc_done", j - 3, inside)
                    after(pe, "tb_copied", j - 1, inside)
                    for i in range(G):
                        last = nc.tensor.transpose(ps_t[:, i, :], t_c[:, i, :], ident[:, :])
                    last.then_inc(s["tcT_done"], 1)
                    after(pe, "tc_copied", j - 3, inside)
                    after(pe, "lg_copied", j - 4, inside)
                    for i in range(G):
                        last = nc.tensor.matmul(ps_lg[:, i * E:(i + 1) * E], tc_t[:, i, :], wr_t[:, :],
                                                start=True, stop=True)
                    last.then_inc(s["lg_done"], 1)

            rounds(run, pe)


def experts_program(nc, x_res, ident, logits, sorted_rows, br, W1, b1, W2, b2, out):
    E, F, D = W1.shape
    B = x_res.shape[1]
    XW = x_res.shape[2]
    C = F // P
    TOK = B * P
    T = sorted_rows.shape[0] // P
    W1C = F + C
    W2C = F + D
    assert T % LOT == 0
    out_rows = out.rearrange("b s d -> (b s) d")
    with ExitStack() as stack:
        def sb(name, shape, dt=F32):
            return stack.enter_context(nc.sbuf_tensor(name, shape, dt))

        def sem(name):
            return stack.enter_context(nc.semaphore(name))

        w1_raw = sb("w1_raw", [P, 2, C, D])
        w2_raw = sb("w2e_raw", [P, 2, F])
        w1_all = sb("w1_all", [P, E, W1C])
        w2_all = sb("w2_all", [P, E, W2C])
        upper = sb("upper", [P, P])
        ones_pp = sb("ones_pp", [P, P])
        br_b = sb("br_b", [P, E])
        iota_i = sb("iota_i", [P, T], I32)
        iota_f = sb("iota_f", [P, T])
        rev_i = sb("rev_i", [P, E], I32)
        rev_f = sb("rev_f", [P, E])
        zeros = sb("zeros", [P, 1])
        tick = sb("tick", [P, 1])
        lmax = sb("lmax", [P, B])
        onehot = sb("onehot", [P, B, E])
        cand = sb("cand", [P, B, E])
        cnt = sb("cnt", [P, B, E])
        scan = sb("scan", [P, 2, B * E])
        ntile = sb("ntile", [P, E])
        tend = sb("tend", [P, 2, E])
        tstart = sb("tstart", [P, E])
        pos = sb("pos", [P, B, E])
        slot = sb("slot", [P, B])
        texp = sb("texp", [P, 2, T])
        texp_i = sb("texp_i", [P, T], I32)
        stage = sb("stage", [P, 2, G, XW])
        idx = sb("idx", [P, 2, G], U32)
        rows = sb("rows", [P, T, XW])
        w1_now = sb("w1_now", [P, 2, W1C])
        w2_now = sb("w2_now", [P, 2, W2C])
        t_now = sb("t_now", [P, 2, D])
        t_t = sb("t_t", [P, 2, P])
        h_t = sb("h_t", [P, 2, C, P])
        xb2 = sb("xb2", [P, 2, D])
        o_now = sb("o_now", [P, 2, D])
        o_idx = sb("o_idx", [P, 2, 1], U32)

        ps = stack.enter_context(nc.psum_tensor("ps3", [P, 8, 512], F32))
        ps_h = (ps[:, 0, :], ps[:, 1, :])
        ps_t = (ps[:, 2, 0:P], ps[:, 3, 0:P])
        ps_y = (ps[:, 4, 0:P], ps[:, 5, 0:P])

        names = ("ld1", "raw_in", "raw_used", "setup_g", "wT_done", "w_copied", "b_in", "r", "rank_done", "staged", "ticked", 
                 "scattered0", "scattered1", "rows_in", "ld_rows", "w1_set", "w2_set", "t_set", "T_done", "t_copied",
                 "h_done", "relu_done", "y_done", "xb_set", "fin", "oidx_set", "out_sent0", "out_sent1")
        s = {n: sem("e_" + n) for n in names}
        ld_lot = [sem(f"e_lot{n}") for n in range(T // LOT)]
        ld_raw = [sem(f"e_raw{n}") for n in range(2)]

        FIRST = 4

        def rounds(run, eng):
            for j in range(-2, FIRST):
                run(j, j % 2, j // 2)
            with eng.Fori(0, (T - 2 - FIRST) // 2) as turn:
                run(FIRST + 2 * turn, 0, FIRST // 2 + turn, True)
                run(FIRST + 1 + 2 * turn, 1, FIRST // 2 + turn, True)
            for j in range(T - 2, T + 1):
                run(j, j % 2, j // 2)

        def has(k, inside):
            return inside or 0 <= k < T

        def after(eng, name, k, inside, n=1):
            if inside or k >= 0:
                eng.wait_ge(s[name], (k + 1) * n)

        def flat(ap):
            return ap.rearrange("p a d -> p (a d)")

        block = stack.enter_context(nc.Block())

        @block.sync
        def _(sp):
            sp.dma_start(br_b[:, :], br.partition_broadcast(P)).then_inc(s["b_in"], 16)
            for e in range(E):
                sp.dma_start(w1_all[:, e, F:F + C], b1[e].rearrange("(c p) -> p c", p=P),
                             allow_slow_non_contiguous=True).then_inc(s["b_in"], 16)
                sp.dma_start(w2_all[:, e, F:F + D], b2[e].partition_broadcast(P)).then_inc(s["b_in"], 16)
            for e in range(E):
                if e > 1:
                    sp.wait_ge(s["wT_done"], 2 * (e - 1))
                sp.dma_start(w1_raw[:, e % 2], W1[e].rearrange("(c p) d -> p c d", p=P)).then_inc(ld_raw[e % 2], 16)
                sp.dma_start(w2_raw[:, e % 2], W2[e]).then_inc(ld_raw[e % 2], 16)
            sp.wait_ge(s["scattered0"], 8 * B)
            sp.wait_ge(s["scattered1"], 8 * B)
            for n in range(T // LOT):
                sp.dma_start(rows[:, n * LOT:(n + 1) * LOT, :],
                             sorted_rows[n * LOT * P:(n + 1) * LOT * P, :].rearrange("(t p) w -> p t w", p=P)
                             ).then_inc(ld_lot[n], 16)
            for n in range(T // LOT):
                sp.wait_ge(ld_lot[n], 16)
                sp.sem_inc(s["rows_in"], LOT)
            sp.wait_ge(s["out_sent0"], 8 * T)
            sp.wait_ge(s["out_sent1"], 8 * T)

        @block.scalar
        def _(act):
            for e in range(E):
                act.wait_ge(s["wT_done"], 2 * e + 1)
                nc.scalar.activation(w1_all[:, e, 0:F], ps[:, 0, :], ACT.Copy).then_inc(s["w_copied"], 1)
                act.wait_ge(s["wT_done"], 2 * e + 2)
                nc.scalar.activation(w2_all[:, e, 0:F], ps[:, 1, :], ACT.Copy).then_inc(s["w_copied"], 1)

            def run(j, par, half, inside=False):
                if has(j + 1, inside):
                    after(act, "h_done", j - 1, inside)
                    after(act, "T_done", j + 1, inside)
                    nc.scalar.activation(t_t[:, 1 - par, :], ps_t[1 - par], ACT.Copy).then_inc(s["t_copied"], 1)
                if has(j, inside):
                    after(act, "y_done", j - 2, inside)
                    after(act, "h_done", j, inside)
                    for c in range(C):
                        last = nc.scalar.activation(h_t[:, par, c, :], ps_h[par][:, c * P:(c + 1) * P], ACT.Relu,
                                                    bias=w1_now[:, par, F + c:F + c + 1])
                    last.then_inc(s["relu_done"], 1)

            rounds(run, act)

        @block.gpsimd
        def _(pool):
            nc.gpsimd.memset(upper[:, :], 1.0).then_inc(s["setup_g"], 1)
            nc.gpsimd.memset(ones_pp[:, :], 1.0).then_inc(s["setup_g"], 1)
            nc.gpsimd.memset(zeros[:, :], 0.0).then_inc(s["setup_g"], 1)
            nc.gpsimd.iota(iota_i[:, :], pattern=[[1, T]], base=0, channel_multiplier=0).then_inc(s["setup_g"], 1)
            nc.gpsimd.iota(rev_i[:, :], pattern=[[-1, E]], base=E, channel_multiplier=0).then_inc(s["setup_g"], 1)
            pool.wait_ge(s["setup_g"], 5)
            nc.gpsimd.affine_select(out=upper[:, :], in_=upper[:, :], compare_op=ALU.is_gt, fill=0.0,
                                    base=0, pattern=[[1, P]], channel_multiplier=-1).then_inc(s["setup_g"], 1)
            pool.wait_ge(s["setup_g"], 6)

            def send(g, par, inside=False):
                if inside or g > 0:
                    pool.wait_ge(s["ticked"], g)
                pool.wait_ge(s["staged"], g + 1)
                nc.gpsimd.tensor_tensor(tick[:, :], zeros[:, :], zeros[:, :], ALU.add).then_inc(s["ticked"], 1)
                for i in range(G):
                    nc.gpsimd.indirect_dma_start(
                        out=sorted_rows, out_offset=bass.IndirectOffsetOnAxis(ap=idx[:, par, i:i + 1], axis=0),
                        in_=stage[:, par, i, :], in_offset=None).then_inc(s[f"scattered{par}"], 16)

            send(0, 0)
            send(1, 1)
            with pool.Fori(0, B // G // 2 - 2) as turn:
                send(2 + 2 * turn, 0, True)
                send(3 + 2 * turn, 1, True)
            send(B // G - 2, 0)
            send(B // G - 1, 1)

            def run(j, par, half, inside=False):
                if has(j - 1, inside):
                    after(pool, "fin", j - 1, inside)
                if has(j, inside):
                    if not has(j - 1, inside):
                        pool.wait_ge(s["rows_in"], 1)
                    after(pool, "fin", j - 2, inside)
                    after(pool, "w2_set", j, inside)
                    nc.gpsimd.tensor_tensor(xb2[:, par, :], flat(rows[:, bass.ds(j, 1), 0:D]), w2_now[:, par, F:W2C],
                                            ALU.add).then_inc(s["xb_set"], 1)
                if has(j - 1, inside):
                    nc.gpsimd.indirect_dma_start(
                        out=out_rows, out_offset=bass.IndirectOffsetOnAxis(ap=o_idx[:, 1 - par, :], axis=0),
                        in_=o_now[:, 1 - par, :], in_offset=None, bounds_check=TOK - 1,
                        oob_is_err=False).then_inc(s[f"out_sent{1 - par}"], 16)

            rounds(run, pool)

        @block.vector
        def _(dve):
            dve.wait_ge(s["setup_g"], 6)
            dve.wait_ge(s["b_in"], 16 * (2 * E + 1))
            n_r = [0]

            def step(ins):
                ins.then_inc(s["r"], 1)
                n_r[0] += 1
                dve.wait_ge(s["r"], n_r[0])

            flat_e = [P, B, E]
            nc.vector.tensor_copy(iota_f[:, :], iota_i[:, :])
            nc.vector.memset(texp[:, 0, :], 0.0)
            nc.vector.tensor_copy(rev_f[:, :], rev_i[:, :])
            step(nc.vector.tensor_tensor(logits[:, :, :], logits[:, :, :], br_b[:, :].unsqueeze(1).to_broadcast(flat_e), ALU.add))
            step(nc.vector.reduce_max(lmax[:, :], logits[:, :, :], AX))
            step(nc.vector.tensor_tensor(cand[:, :, :], logits[:, :, :], lmax[:, :].unsqueeze(2).to_broadcast(flat_e), ALU.is_ge))
            step(nc.vector.tensor_tensor(cand[:, :, :], cand[:, :, :], rev_f[:, :].unsqueeze(1).to_broadcast(flat_e), ALU.mult))
            step(nc.vector.reduce_max(lmax[:, :], cand[:, :, :], AX))
            step(nc.vector.tensor_tensor(onehot[:, :, :], cand[:, :, :], lmax[:, :].unsqueeze(2).to_broadcast(flat_e), ALU.is_equal))
            dve.wait_ge(s["rank_done"], 1)
            step(nc.vector.tensor_copy(cnt[:, :, :].rearrange("p b e -> p (b e)"), ps[:, 3, :]))
            src, k, n = cnt[:, :, :].rearrange("p b e -> p (b e)"), E, 0
            while k < B * E:
                dst = scan[:, n % 2, :]
                nc.vector.tensor_copy(dst[:, 0:k], src[:, 0:k])
                step(nc.vector.tensor_tensor(dst[:, k:], src[:, k:], src[:, 0:B * E - k], ALU.add))
                src, k, n = dst, 2 * k, n + 1
            total = src[:, (B - 1) * E:]
            step(nc.vector.tensor_scalar(ntile[:, :], total, 1.0 / P, (P - 1.0) / P - 0.5 + 0.5 / P, ALU.mult, ALU.add))
            step(nc.vector.tensor_scalar(ntile[:, :], ntile[:, :], ROUND, None, ALU.add))
            step(nc.vector.tensor_scalar(ntile[:, :], ntile[:, :], ROUND, None, ALU.subtract))
            s2, k, n = ntile[:, :], 1, 0
            while k < E:
                dst = tend[:, n % 2, :]
                nc.vector.tensor_copy(dst[:, 0:k], s2[:, 0:k])
                step(nc.vector.tensor_tensor(dst[:, k:], s2[:, k:], s2[:, 0:E - k], ALU.add))
                s2, k, n = dst, 2 * k, n + 1
            step(nc.vector.tensor_tensor(tstart[:, :], s2, ntile[:, :], ALU.subtract))
            step(nc.vector.tensor_scalar(tstart[:, :], tstart[:, :], float(P), None, ALU.mult))
            step(nc.vector.tensor_tensor(pos[:, :, :].rearrange("p b e -> p (b e)"), src,
                                         cnt[:, :, :].rearrange("p b e -> p (b e)"), ALU.subtract))
            step(nc.vector.tensor_tensor(pos[:, :, :].rearrange("p b e -> p (b e)"),
                                         pos[:, :, :].rearrange("p b e -> p (b e)"), ps[:, 2, :], ALU.add))
            step(nc.vector.tensor_tensor(pos[:, :, :], pos[:, :, :], tstart[:, :].unsqueeze(1).to_broadcast(flat_e), ALU.add))
            step(nc.vector.tensor_tensor(pos[:, :, :], pos[:, :, :], onehot[:, :, :], ALU.mult))
            step(nc.vector.reduce_sum(slot[:, :], pos[:, :, :], AX))
            assert n_r[0] == SLOT_R

            def take(g, par, pairs, inside=False):
                if inside or g > 1:
                    dve.wait_ge(s[f"scattered{par}"], 16 * G * pairs)
                nc.vector.tensor_copy(idx[:, par, :], flat(slot[:, bass.ds(G * g, G)].unsqueeze(1)))
                nc.vector.tensor_copy(stage[:, par, :, :], x_res[:, bass.ds(G * g, G), :]).then_inc(s["staged"], 1)

            for g in range(4):
                take(g, g % 2, g // 2)
            for e in range(E):
                step(nc.vector.scalar_tensor_tensor(texp[:, (e + 1) % 2, :], iota_f[:, :], s2[:, e:e + 1],
                                                    texp[:, e % 2, :], ALU.is_ge, ALU.add))
            step(nc.vector.tensor_scalar(texp_i[:, :], texp[:, E % 2, :], float(E - 1), None, ALU.min))
            with dve.Fori(0, B // G // 2 - 2) as turn:
                take(4 + 2 * turn, 0, 2 + turn, True)
                take(5 + 2 * turn, 1, 2 + turn, True)
            dve.wait_ge(s["w_copied"], 2 * E)

            def run(j, par, half, inside=False):
                if has(j + 1, inside):
                    e = dve.value_load(texp_i[0:1, bass.ds(j + 1, 1)], min_val=0, max_val=E - 1)
                    after(dve, "h_done", j - 1, inside)
                    after(dve, "relu_done", j - 1, inside)
                    nc.vector.tensor_copy(w1_now[:, 1 - par, :], flat(w1_all[:, bass.ds(e, 1), :])).then_inc(s["w1_set"], 1)
                if has(j + 2, inside):
                    after(dve, "rows_in", j + 2, inside)
                    after(dve, "T_done", j, inside)
                    row = rows[:, bass.ds(j + 2, 1), :]
                    nc.vector.tensor_scalar(t_now[:, par, :], flat(row[:, :, 0:D]), flat(row[:, :, D:D + 1]),
                                            flat(row[:, :, D + 1:D + 2]), ALU.subtract, ALU.mult).then_inc(s["t_set"], 1)
                if has(j - 1, inside):
                    if inside or j > 2:
                        dve.wait_ge(s[f"out_sent{1 - par}"], 16 * (half - 1 + par))
                    after(dve, "xb_set", j - 1, inside)
                    after(dve, "y_done", j - 1, inside)
                    nc.vector.tensor_copy(o_idx[:, 1 - par, :], flat(rows[:, bass.ds(j - 1, 1), D + 2:D + 3]))
                    nc.vector.tensor_tensor(o_now[:, 1 - par, :], ps_y[1 - par], xb2[:, 1 - par, :],
                                            ALU.add).then_inc(s["fin"], 1)
                if has(j + 1, inside):
                    after(dve, "y_done", j - 1, inside)
                    after(dve, "xb_set", j - 1, inside)
                    nc.vector.tensor_copy(w2_now[:, 1 - par, :], flat(w2_all[:, bass.ds(e, 1), :])).then_inc(s["w2_set"], 1)

            rounds(run, dve)

        @block.tensor
        def _(pe):
            for e in range(E):
                pe.wait_ge(ld_raw[e % 2], 32 * (e // 2 + 1))
                if e > 0:
                    pe.wait_ge(s["w_copied"], 2 * e)
                for c in range(C):
                    last = nc.tensor.transpose(ps[:, 0, c * P:(c + 1) * P], w1_raw[:, e % 2, c, :], ident[:, :])
                last.then_inc(s["wT_done"], 1)
                for c in range(C):
                    last = nc.tensor.transpose(ps[:, 1, c * P:(c + 1) * P], w2_raw[:, e % 2, c * P:(c + 1) * P], ident[:, :])
                last.then_inc(s["wT_done"], 1)
            pe.wait_ge(s["r"], 6)
            nc.tensor.matmul(ps[:, 2, :], upper[:, :], onehot[:, :, :].rearrange("p b e -> p (b e)"), start=True, stop=True)
            nc.tensor.matmul(ps[:, 3, :], ones_pp[:, :], onehot[:, :, :].rearrange("p b e -> p (b e)"), start=True,
                             stop=True).then_inc(s["rank_done"], 1)
            pe.wait_ge(s["r"], SLOT_R)

            def run(j, par, half, inside=False):
                if has(j + 1, inside):
                    after(pe, "t_set", j + 1, inside)
                    after(pe, "t_copied", j - 1, inside)
                    nc.tensor.transpose(ps_t[1 - par], t_now[:, 1 - par, :], ident[:, :]).then_inc(s["T_done"], 1)
                if has(j, inside):
                    after(pe, "t_copied", j, inside)
                    after(pe, "w1_set", j, inside)
                    after(pe, "relu_done", j - 2, inside)
                    for c in range(C):
                        last = nc.tensor.matmul(ps_h[par][:, c * P:(c + 1) * P], w1_now[:, par, c * P:(c + 1) * P],
                                                t_t[:, par, :], start=True, stop=True)
                    last.then_inc(s["h_done"], 1)
                if has(j - 1, inside):
                    after(pe, "relu_done", j - 1, inside)
                    after(pe, "w2_set", j - 1, inside)
                    after(pe, "fin", j - 3, inside)
                    for c in range(C):
                        last = nc.tensor.matmul(ps_y[1 - par], h_t[:, 1 - par, c, :],
                                                w2_now[:, 1 - par, c * P:(c + 1) * P], start=c == 0, stop=c == C - 1)
                    last.then_inc(s["y_done"], 1)

            rounds(run, pe)



def layers(nc, x, ctx, mask, ln_x_w, ln_x_b, ln_l_w, ln_l_b, Wq, Wkv, q_scale, k_scale, Wo, ln_o_w, ln_o_b,
           weight_q, weight_scale, bias, We, W2, Wr, br, F1, b1, F2, b2, out):
    B, S, D = x.shape
    M = ctx.shape[1]
    E = Wr.shape[0]
    mask = mask.bitcast(U8).rearrange("(b m) -> b m", m=M)
    weight_q = weight_q.bitcast(I8).rearrange("(o i) -> o i", i=D)
    tiles = -(-(B * S // P + E - 1) // LOT) * LOT
    sorted_rows = nc.dram_tensor("sorted_rows", (tiles * P, D + 3), F32, kind="Internal").ap()
    with ExitStack() as stack:
        x_res = stack.enter_context(nc.sbuf_tensor("x_res", [P, B, D + 3], F32))
        ident = stack.enter_context(nc.sbuf_tensor("ident", [P, P], F32))
        logits = stack.enter_context(nc.sbuf_tensor("logits", [P, B, E], F32))
        with ExitStack() as inner:
            ctx_res = inner.enter_context(nc.sbuf_tensor("ctx_res", [P, B, D], F32))
            latent_attention(nc, x_res, ctx_res, ident, sorted_rows, x, ctx, mask, ln_x_w, ln_x_b, ln_l_w, ln_l_b,
                             Wq, Wkv, q_scale, k_scale, Wo, ln_o_w, ln_o_b)
            ffn_xattn_route(nc, x_res, ctx_res, ident, logits, weight_q, weight_scale, bias, We, W2, Wr, B, D, E)
        experts_program(nc, x_res, ident, logits, sorted_rows, br, F1, b1, F2, b2, out)


INPUTS = ['x', 'ctx_1024', 'mask_BxS2_bk0', 'L0_xattn_ln_x_w', 'L0_xattn_ln_x_b', 'L0_xattn_ln_l_w', 'L0_xattn_ln_l_b',
          'L0_xattn_Wq', 'L0_xattn_Wkv', 'L0_xattn_q_scale', 'L0_xattn_k_scale', 'L0_xattn_Wo', 'L0_xattn_ln_o_w',
          'L0_xattn_ln_o_b', 'L0_ffn_weight_q', 'L0_ffn_weight_scale', 'L0_ffn_bias', 'L1_xattn_We', 'L1_xattn_W2',
          'L1_ffn_Wr', 'L1_ffn_br', 'L1_ffn_W1', 'L1_ffn_b1', 'L1_ffn_W2', 'L1_ffn_b2']


def kernel(**inputs):
    import numpy as np
    import concourse.bacc as bacc
    from concourse.bass_utils import run_bass_kernel_spmd

    nc = bacc.Bacc("TRN2", target_bir_lowering=False, num_devices=1)
    arrays, args = {}, []
    for name in INPUTS:
        a = np.ascontiguousarray(inputs[name])
        if a.dtype.itemsize == 1:
            a = a.reshape(-1).view(np.int32)
        arrays[f"in_{name}_dram"] = a
        args.append(nc.dram_tensor(f"in_{name}_dram", a.shape, mybir.dt.from_np(a.dtype), kind="ExternalInput").ap())
    out = nc.dram_tensor("out_dram", arrays["in_x_dram"].shape, F32, kind="ExternalOutput").ap()
    layers(nc, *args, out)
    r = run_bass_kernel_spmd(nc, [arrays], core_ids=[0])
    return r.results[0]["out_dram"]
```

```python
import math
from contextlib import ExitStack

import concourse.bass as bass
from concourse import mybir

F32 = mybir.dt.float32
F32R = mybir.dt.float32r
BF16 = mybir.dt.bfloat16
I32 = mybir.dt.int32
U32 = mybir.dt.uint32
I8 = mybir.dt.int8
U8 = mybir.dt.uint8
ALU = mybir.AluOpType
ACT = mybir.ActivationFunctionType
AX = mybir.AxisListType.X

P = 128
LN_EPS = 1e-5
L2_EPS = 1e-12
SIM_SCALE = 8.0
EXP_ROOM = 80.0
MASKED = -1e30
LN_LIFT = 20
LN2 = math.log(2.0)
VW = 96
Q_EPS = 1e-6
Q_MAX = 127.0
ROUND = 1.5 * 2.0 ** 23
G = 4
FILL = 20000.0
DEEP = 4
PAD_R = 3
TABLE_R = PAD_R + 3 + 3 + 1 + 6


def latent_attention(nc, x_res, ctx_res, ident, sorted_rows, x, ctx, mask, ln_x_w, ln_x_b, ln_l_w, ln_l_b, Wq, Wkv,
                     q_scale, k_scale, Wo, ln_o_w, ln_o_b, E):
    B, S, D = x.shape
    M = ctx.shape[1]
    DH = q_scale.shape[0]
    INNER = Wq.shape[1]
    H = INNER // DH
    PAIRS = H // 2
    assert S == P and D == P and INNER == PAIRS * P and 2 * DH == P

    with ExitStack() as stack:
        def sb(name, shape, dt=F32):
            return stack.enter_context(nc.sbuf_tensor(name, shape, dt))

        def sem(name):
            return stack.enter_context(nc.semaphore(name))

        fill = sb("fill", [P, 1, D + 3])
        ids = sb("ids", [P, B], I32)
        zero_col = sb("zero_col", [P, 1])
        mask_raw = sb("mask_raw", [P, P], U8)
        mask_f = sb("mask_f", [P, P])
        mask_bias = sb("mask_bias", [P, P])
        neg_shift = sb("neg_shift", [P, 1])
        qs_b = sb("qs_b", [P, DH])
        ks_b = sb("ks_b", [P, DH])
        qk_prod = sb("qk_prod", [P, DH])
        qk_max = sb("qk_max", [P, 1])
        scale_col = sb("scale_col", [P, 4])
        ln_cols = sb("ln_cols", [P, 4])
        lno_w = sb("lno_w", [P, D])
        lno_b = sb("lno_b", [P, D])
        w_raw = sb("w_raw", [P, 3 * INNER])
        w_hi = sb("w_hi", [P, 3 * INNER], F32R)
        w_lo = sb("w_lo", [P, 3 * INNER], F32R)
        wo_sb = sb("wo_sb", [P, PAIRS, D])

        bn6 = sb("bn6", [P, 2, 6])
        xc_stat = sb("xc_stat", [P, 2, 2, 2])
        lift_bias = sb("lift_bias", [P, 1])
        var_in = sb("var_in", [P, 32])
        rs_ln = sb("rs_ln", [P, 32])
        rs_y0 = sb("rs_y0", [P, 32])
        rs_t1 = sb("rs_t1", [P, 32])
        rs_t2 = sb("rs_t2", [P, 32])
        rs_t3 = sb("rs_t3", [P, 32])
        rs_t4 = sb("rs_t4", [P, 32])
        rstd = sb("rstd", [P, 2, 32])
        xc_hat = sb("xc_hat", [P, 2, 2, D])
        xc_t = sb("xc_t", [P, 2, 2, P])
        xc_hi = sb("xc_hi", [P, 2, 2, P], F32R)
        xc_lo = sb("xc_lo", [P, 2, 2, P], F32R)
        mask_now = sb("mask_now", [P, 2])
        sq = sb("sq", [P, 3 * INNER])
        sumsq = sb("sumsq", [P, 3 * H])
        three = sb("three", [P, 32])
        var_mul = sb("var_mul", [P, 2])
        var_add = sb("var_add", [P, 3])
        var_tmp = sb("var_tmp", [P, 2])
        qk_hat = sb("qk_hat", [P, 3 * INNER])
        q_hi = sb("q_hi", [P, PAIRS, 2, P], F32R)
        q_lo = sb("q_lo", [P, PAIRS, 2, P], F32R)
        k_hi = sb("k_hi", [P, 2, INNER], F32R)
        k_lo = sb("k_lo", [P, 2, INNER], F32R)
        prob = sb("prob", [P, 2, H * P])
        v_sb = sb("v_sb", [P, 2, 2, H, VW])
        rden = sb("rden", [P, H])
        o_n = sb("o_n", [P, INNER])
        o_t = sb("o_t", [P, INNER])
        o6 = sb("o6", [P, 6])
        o_stat = sb("o_stat", [P, 2, 2])
        o_c = sb("o_c", [P, 2, D])
        x_b = sb("x_b", [P, 2, D])

        ps = stack.enter_context(nc.psum_tensor("ps", [P, 8, 512], F32))
        ps_qk = ps[:, 0:3, :]
        ps_v, ps_ot = (ps[:, 4, :], ps[:, 5, :]), ps[:, 3, :]
        ps_s = (ps[:, 4, :], ps[:, 5, :], ps[:, 3, :], ps[:, 4, :])
        ps_pv = ps[:, 6, 0:(H - 1) * (DH + 1)].rearrange("p (h e) -> p h e", e=DH + 1)
        ps_xc = ps[:, 7, 0:2 * P]
        ps_o = ps[:, 7, 2 * P:3 * P]
        ps_pv7 = ps[:, 3, 0:DH + 1]

        lots = [slice(0, 4)] + [slice(n, min(n + 12, B)) for n in range(4, B, 12)]
        ld_lot = [sem(f"ld_lot{n}") for n in range(len(lots))]
        tokens_in = sem("tokens_in")
        ld_w = sem("ld_w")
        ctx_zeroed = sem("ctx_zeroed")
        const_ready = sem("const_ready")
        setup_v = sem("setup_v")
        setup_p = sem("setup_p")
        setup_g = sem("setup_g")
        s_maskT = sem("s_maskT")
        xc_bn = sem("xc_bn")
        xc_mv = sem("xc_mv")
        var_t = sem("var_t")
        ss_raw = sem("ss_raw")
        ss_done = sem("ss_done")
        var_ready = sem("var_ready")
        ln_done = sem("ln_done")
        y0_done = sem("y0_done")
        nwt = sem("nwt")
        rs_ready = sem("rs_ready")
        hat_ready = sem("hat_ready")
        xct_sb = sem("xct_sb")
        hi_done = sem("hi_done")
        lo_done = sem("lo_done")
        qk_done = sem("qk_done")
        sq_done = sem("sq_done")
        scaled = sem("scaled")
        qkT_done = sem("qkT_done")
        qhi_done = sem("qhi_done")
        khi_done = sem("khi_done")
        klo_done = sem("klo_done")
        qlo_done = sem("qlo_done")
        sim_done = sem("sim_done")
        exp_done = sem("exp_done")
        v_done = sem("v_done")
        v_copied = sem("v_copied")
        pv_done = sem("pv_done")
        rl_done = sem("rl_done")
        on_done = sem("on_done")
        onT_done = sem("onT_done")
        ot_done = sem("ot_done")
        wo_done = sem("wo_done")
        xcT_done = sem("xcT_done")
        o_bn = sem("o_bn")
        o_mv = sem("o_mv")
        o_cent = sem("o_cent")
        xb_done = sem("xb_done")
        mask_set = sem("mask_set")
        x1_done = sem("x1_done")
        fill_out = sem("fill_out")

        N_W = 16 * 16

        SETUP_V, SETUP_G = 14, 9

        def rounds(run, eng):
            for j in range(-3, 5):
                run(j, j % 2)
            with eng.Fori(0, (B - 8) // 2) as turn:
                run(5 + 2 * turn, 1, True)
                run(6 + 2 * turn, 0, True)
            for j in range(B - 3, B + 2):
                run(j, j % 2)

        def has(b, inside):
            return inside or 0 <= b < B

        block = stack.enter_context(nc.Block())

        @block.sync
        def _(sp):
            for n, lot in enumerate(lots):
                sp.dma_start(x_res[:, lot, 0:D], x[lot].rearrange("b s d -> s b d")).then_inc(ld_lot[n], 16)
                if n == 0:
                    sp.wait_ge(ctx_zeroed, 1)
                sp.dma_start(ctx_res[0:M, lot, :], ctx[lot].rearrange("b m d -> m b d")).then_inc(ld_lot[n], 16)
            for n, lot in enumerate(lots):
                sp.wait_ge(ld_lot[n], 32)
                sp.sem_inc(tokens_in, lot.stop - lot.start)
            sp.wait_ge(setup_v, SETUP_V)
            sp.dma_start(sorted_rows[sorted_rows.shape[0] - E * P:, :].rearrange("(t p) w -> p t w", p=P),
                         fill[:, :, :].to_broadcast([P, E, D + 3])).then_inc(fill_out, 16)
            sp.wait_ge(fill_out, 16)

        @block.scalar
        def _(act):
            act.dma_start(w_raw[:, 0:INNER], Wq).then_inc(ld_w, 16)
            act.dma_start(w_raw[:, INNER:3 * INNER], Wkv).then_inc(ld_w, 16)
            act.dma_start(wo_sb[:, :, :], Wo.rearrange("(t p) d -> p t d", p=P)).then_inc(ld_w, 16)
            act.dma_start(mask_raw[0:B, 0:M], mask).then_inc(ld_w, 16)
            for n, v in enumerate((ln_l_w, ln_l_b, ln_x_w, ln_x_b)):
                act.dma_start(ln_cols[:, n:n + 1], v.rearrange("(p a) -> p a", a=1)).then_inc(ld_w, 16)
            act.dma_start(qs_b[:, :], q_scale.partition_broadcast(P)).then_inc(ld_w, 16)
            act.dma_start(ks_b[:, :], k_scale.partition_broadcast(P)).then_inc(ld_w, 16)
            act.dma_start(lno_w[:, :], ln_o_w.partition_broadcast(P)).then_inc(ld_w, 16)
            act.dma_start(lno_b[:, :], ln_o_b.partition_broadcast(P)).then_inc(ld_w, 16)
            for n, v in enumerate((q_scale, k_scale)):
                for half in (0, 1):
                    act.dma_start(scale_col[half * DH:(half + 1) * DH, n:n + 1],
                                  v.rearrange("(p a) -> p a", a=1)).then_inc(ld_w, 16)
            act.wait_ge(setup_v, SETUP_V)
            act.wait_ge(setup_g, SETUP_G)
            nc.scalar.preload_act_table_set("natural_log_exp_and_others")

            def run(j, par, inside=False):
                if has(j, inside):
                    act.wait_ge(qkT_done, 3 * j + 1)
                    if inside or j > 0:
                        act.wait_ge(sim_done, 4 * j)
                    for half in (0, 1):
                        rows = slice(half * DH, (half + 1) * DH)
                        last = nc.scalar.activation(q_hi[rows, :, half, :],
                                                    ps_qk[rows, 0, :].rearrange("p (t q) -> p t q", q=P),
                                                    ACT.Copy, scale=scale_col[rows, 2:3])
                    last.then_inc(qhi_done, 1)
                    for kt in (0, 1):
                        act.wait_ge(qkT_done, 3 * j + 2 + kt)
                        nc.scalar.activation(k_hi[:, kt, :], ps_qk[:, 1 + kt, :], ACT.Copy).then_inc(khi_done, 1)
                if has(j + 1, inside):
                    act.wait_ge(xct_sb, j + 2)
                    if inside or j > 0:
                        act.wait_ge(v_done, 2 * j)
                    nc.scalar.activation(xc_hi[:, 1 - par, :, :], xc_t[:, 1 - par, :, :], ACT.Copy).then_inc(hi_done, 1)
                if has(j, inside):
                    if inside or j > 1:
                        act.wait_ge(pv_done, j - 1)
                    for kt in (0, 1):
                        act.wait_ge(v_done, 2 * j + kt + 1)
                        nc.scalar.activation(v_sb[:, par, kt, :, 0:DH], ps_v[kt].rearrange("p (h d) -> p h d", d=DH),
                                             ACT.Copy).then_inc(v_copied, 1)
                if has(j + 1, inside):
                    if inside or j >= 0:
                        act.wait_ge(ss_raw, 3 * j + 3)
                    for n in range(3):
                        act.wait_ge(qk_done, 3 * j + 4 + n)
                        nc.scalar.activation(sq[:, n * INNER:(n + 1) * INNER], ps_qk[:, n, :],
                                             ACT.Square).then_inc(sq_done, 1)
                def exps(before, units):
                    for done, n in enumerate(units, before):
                        if n == 3:
                            act.wait_ge(mask_set, j + 1)
                        act.wait_ge(sim_done, 4 * j + done + 1)
                        nc.scalar.activation(prob[:, n // 2, n % 2 * INNER:(n % 2 + 1) * INNER], ps_s[n], ACT.Exp,
                                             bias=(mask_now[:, par:par + 1] if n > 1 else
                                                   neg_shift[:, 0:1])).then_inc(exp_done, 1)

                act.wait_ge(var_ready, j + 4)
                if has(j + 1, inside):
                    act.wait_ge(ss_done, j + 2)
                if inside or j > -3:
                    act.wait_ge(rs_ready, j + 3)
                nc.scalar.activation(rs_ln[:, :], var_in[:, :], ACT.Ln, scale=float(2 ** LN_LIFT)).then_inc(ln_done, 1)
                act.wait_ge(ln_done, j + 4)
                nc.scalar.activation(rs_y0[:, :], rs_ln[:, :], ACT.Exp, scale=-0.5,
                                     bias=lift_bias[:, 0:1]).then_inc(y0_done, 1)
                if has(j, inside):
                    if inside or j > 0:
                        act.wait_ge(pv_done, j)
                    exps(0, (0,))
                if has(j - 1, inside):
                    act.wait_ge(onT_done, j)
                    if inside or j > 1:
                        act.wait_ge(wo_done, j - 1)
                    nc.scalar.activation(o_t[:, :], ps_ot, ACT.Copy).then_inc(ot_done, 1)
                if has(j, inside):
                    exps(1, (1, 3, 2))

            rounds(run, act)

        @block.gpsimd
        def _(pool):
            nc.gpsimd.memset(ctx_res[:, :, :], 0.0).then_inc(ctx_zeroed, 1)
            nc.gpsimd.memset(mask_f[:, :], 0.0).then_inc(setup_p, 1)
            nc.gpsimd.memset(ident[:, :], 0.0).then_inc(setup_p, 1)
            nc.gpsimd.memset(var_in[:, :], 1.0).then_inc(setup_p, 1)
            nc.gpsimd.memset(fill[:, :, :], FILL).then_inc(setup_p, 1)
            nc.gpsimd.iota(ids[:, :], pattern=[[P, B]], base=0, channel_multiplier=1).then_inc(setup_p, 1)
            nc.gpsimd.memset(zero_col[:, :], 0.0).then_inc(setup_p, 1)
            pool.wait_ge(setup_p, 6)
            nc.gpsimd.affine_select(out=ident[:, :], in_=ident[:, :], compare_op=ALU.not_equal, fill=1.0,
                                    base=0, pattern=[[-1, P]], channel_multiplier=1).then_inc(setup_g, 1)
            nc.gpsimd.memset(v_sb[:, :, :, :, DH + 1:VW], 0.0).then_inc(setup_g, 1)
            nc.gpsimd.memset(v_sb[:, :, :, :, DH:DH + 1], 1.0).then_inc(setup_g, 1)
            nc.gpsimd.memset(three[:, :], 3.0).then_inc(setup_g, 1)
            nc.gpsimd.memset(var_mul[:, 0:1], 1.0 + LN_EPS).then_inc(setup_g, 1)
            nc.gpsimd.memset(var_mul[:, 1:2], 1.0).then_inc(setup_g, 1)
            nc.gpsimd.memset(var_add[:, 0:1], LN_EPS * LN_EPS).then_inc(setup_g, 1)
            nc.gpsimd.memset(var_add[:, 1:3], LN_EPS).then_inc(setup_g, 1)
            nc.gpsimd.memset(lift_bias[:, :], 0.5 * LN_LIFT * LN2).then_inc(setup_g, 1)
            pool.wait_ge(ld_w, N_W)
            pool.wait_ge(setup_g, SETUP_G)

            def run(j, par, inside=False):
                if has(j + 1, inside):
                    pool.wait_ge(hi_done, j + 2)
                    nc.gpsimd.tensor_tensor(xc_lo[:, 1 - par, :, :], xc_t[:, 1 - par, :, :],
                                            xc_hi[:, 1 - par, :, :].bitcast(F32), ALU.subtract).then_inc(lo_done, 1)
                if inside or j > -3:
                    pool.wait_ge(rs_ready, j + 3)
                if has(j + 3, inside):
                    pool.wait_ge(xc_mv, j + 4)
                    nc.gpsimd.tensor_tensor(var_tmp[:, :], xc_stat[:, 1 - par, :, 1], var_mul[:, :],
                                            ALU.mult).then_inc(var_t, 1)
                    pool.wait_ge(var_t, j + 4)
                    last = nc.gpsimd.tensor_tensor(var_in[:, 24:26], var_tmp[:, :], var_add[:, 0:2], ALU.add)
                if has(j - 2, inside):
                    pool.wait_ge(o_mv, j - 1)
                    last = nc.gpsimd.tensor_tensor(var_in[:, 26:27], o_stat[:, par, 1:2], var_add[:, 2:3], ALU.add)
                last.then_inc(var_ready, 1)
                pool.wait_ge(y0_done, j + 4)
                nc.gpsimd.tensor_tensor(rs_t1[:, :], rs_y0[:, :], rs_y0[:, :], ALU.mult).then_inc(nwt, 1)
                nc.gpsimd.tensor_scalar(rs_t3[:, :], rs_y0[:, :], -0.5, None, ALU.mult).then_inc(nwt, 1)
                pool.wait_ge(nwt, 4 * (j + 3) + 1)
                nc.gpsimd.tensor_tensor(rs_t2[:, :], rs_t1[:, :], var_in[:, :], ALU.mult).then_inc(nwt, 1)
                if has(j - 1, inside):
                    pool.wait_ge(scaled, j)
                if inside or -1 <= j < B - 1:
                    pool.wait_ge(hat_ready, j + 2)
                if inside or j > 3:
                    pool.wait_ge(x1_done, j - 3)
                pool.wait_ge(nwt, 4 * (j + 3) + 3)
                nc.gpsimd.tensor_tensor(rs_t4[:, :], rs_t2[:, :], three[:, :], ALU.subtract).then_inc(nwt, 1)
                pool.wait_ge(nwt, 4 * (j + 3) + 4)
                nc.gpsimd.tensor_tensor(rstd[:, par, :], rs_t4[:, :], rs_t3[:, :], ALU.mult).then_inc(rs_ready, 1)
                if has(j, inside):
                    if inside or j > 0:
                        pool.wait_ge(exp_done, 4 * j)
                    if inside or j > 1:
                        pool.wait_ge(x1_done, j - 1)
                    nc.gpsimd.tensor_tensor(x_b[:, par, :], x_res[:, bass.ds(j, 1), 0:D].rearrange("p a d -> p (a d)"),
                                            lno_b[:, :], ALU.add).then_inc(xb_done, 1)
                if has(j + 1, inside):
                    if not has(j, inside):
                        pool.wait_ge(setup_v, SETUP_V)
                    nc.gpsimd.tensor_copy(mask_now[:, 1 - par:2 - par], mask_bias[:, bass.ds(j + 1, 1)]).then_inc(mask_set, 1)

            rounds(run, pool)

        @block.vector
        def _(dve):
            dve.wait_ge(ld_w, N_W)
            nc.vector.tensor_copy(w_hi[:, :], w_raw[:, :]).then_inc(setup_v, 1)
            nc.vector.tensor_tensor(qk_prod[:, :], qs_b[:, :], ks_b[:, :], ALU.mult).then_inc(setup_v, 1)
            dve.wait_ge(setup_p, 6)
            nc.vector.tensor_copy(mask_f[0:B, 0:M], mask_raw[0:B, 0:M]).then_inc(setup_v, 1)
            dve.wait_ge(setup_v, 3)
            nc.vector.tensor_tensor(w_lo[:, :], w_raw[:, :], w_hi[:, :].bitcast(F32), ALU.subtract).then_inc(setup_v, 1)
            nc.vector.tensor_reduce(qk_max[:, :], qk_prod[:, :], AX, ALU.max,
                                    apply_absolute_value=True).then_inc(setup_v, 1)
            nc.vector.tensor_tensor(scale_col[:, 3:4], scale_col[:, 0:1], scale_col[:, 1:2],
                                    ALU.mult).then_inc(setup_v, 1)
            dve.wait_ge(setup_v, 6)
            nc.vector.tensor_scalar(scale_col[:, 2:3], scale_col[:, 3:4], SIM_SCALE, None, ALU.mult).then_inc(setup_v, 1)
            nc.vector.tensor_scalar(neg_shift[:, :], qk_max[:, :], -SIM_SCALE, EXP_ROOM, ALU.mult,
                                    ALU.add).then_inc(setup_v, 1)
            dve.wait_ge(setup_v, 8)
            nc.vector.tensor_scalar(neg_shift[:, :], neg_shift[:, :], 0.0, None, ALU.min).then_inc(setup_v, 1)
            dve.wait_ge(s_maskT, 1)
            nc.vector.tensor_scalar(mask_bias[:, :], ps[:, 7, 0:P], 1.0, -MASKED, ALU.subtract,
                                    ALU.mult).then_inc(setup_v, 1)
            dve.wait_ge(setup_v, 10)
            for part in (q_hi, q_lo):
                nc.vector.tensor_copy(part[:, :, :, :].rearrange("p t a q -> p (t a q)"),
                                      zero_col[:, :].to_broadcast([P, 2 * INNER])).then_inc(setup_v, 1)
            nc.vector.tensor_copy(x_res[:, :, D + 2:D + 3], ids[:, :].unsqueeze(2)).then_inc(setup_v, 1)
            nc.vector.tensor_scalar(mask_bias[:, :], mask_bias[:, :], neg_shift[:, 0:1], None,
                                    ALU.add).then_inc(setup_v, 1)

            def run(j, par, inside=False):
                if has(j + 1, inside):
                    if inside or j > 0:
                        dve.wait_ge(lo_done, j)
                    dve.wait_ge(xcT_done, j + 2)
                    if has(j - 2, inside):
                        dve.wait_ge(wo_done, j - 1)
                    for n in (0, 1):
                        last = nc.vector.tensor_scalar(xc_t[:, 1 - par, n, :], ps_xc[:, n * P:(n + 1) * P],
                                                       ln_cols[:, 2 * n:2 * n + 1], ln_cols[:, 2 * n + 1:2 * n + 2],
                                                       ALU.mult, ALU.add)
                    last.then_inc(xct_sb, 1)
                if has(j, inside):
                    if inside or j > 0:
                        dve.wait_ge(sim_done, 4 * j)
                    dve.wait_ge(qhi_done, j + 1)
                    for half in (0, 1):
                        rows = slice(half * DH, (half + 1) * DH)
                        last = nc.vector.scalar_tensor_tensor(q_lo[rows, :, half, :],
                                                              ps_qk[rows, 0, :].rearrange("p (t q) -> p t q", q=P),
                                                              scale_col[rows, 2:3], q_hi[rows, :, half, :].bitcast(F32),
                                                              ALU.mult, ALU.subtract)
                    last.then_inc(qlo_done, 1)
                    for kt in (0, 1):
                        dve.wait_ge(khi_done, 2 * j + 1 + kt)
                        nc.vector.tensor_tensor(k_lo[:, kt, :], ps_qk[:, 1 + kt, :], k_hi[:, kt, :].bitcast(F32),
                                                ALU.subtract).then_inc(klo_done, 1)
                if has(j - 2, inside):
                    dve.wait_ge(wo_done, j - 1)
                    if has(j + 1, inside):
                        dve.wait_ge(xcT_done, j + 2)
                    if inside or j > 2:
                        dve.wait_ge(o_mv, j - 2)
                    nc.vector.bn_stats(o6[:, :], ps_o).then_inc(o_bn, 1)
                    if inside or j > 3:
                        dve.wait_ge(var_ready, j + 2)
                        dve.wait_ge(x1_done, j - 3)
                    dve.wait_ge(o_bn, j - 1)
                if has(j + 3, inside):
                    dve.wait_ge(tokens_in, j + 4)
                    if inside or j > -3:
                        dve.wait_ge(xc_mv, j + 3)
                    if inside or j > -2:
                        dve.wait_ge(hat_ready, j + 2)
                        dve.wait_ge(var_ready, j + 3)
                    for n, res in enumerate((x_res, ctx_res)):
                        last = nc.vector.bn_stats(bn6[:, n, :], res[:, bass.ds(j + 3, 1), 0:D].rearrange("p a d -> p (a d)"))
                    last.then_inc(xc_bn, 1)
                if has(j - 2, inside):
                    nc.vector.bn_aggr(o_stat[:, par, :], o6[:, :]).then_inc(o_mv, 1)
                    dve.wait_ge(o_mv, j - 1)
                    if has(j + 3, inside):
                        dve.wait_ge(xc_bn, j + 4)
                    nc.vector.scalar_tensor_tensor(o_c[:, par, :], ps_o, o_stat[:, par, 0:1],
                                                   lno_w[:, :], ALU.subtract, ALU.mult).then_inc(o_cent, 1)
                elif has(j + 3, inside):
                    dve.wait_ge(xc_bn, j + 4)
                if has(j + 3, inside):
                    for n in (0, 1):
                        last = nc.vector.bn_aggr(xc_stat[:, 1 - par, n, :], bn6[:, n, :])
                    last.then_inc(xc_mv, 1)
                if has(j + 1, inside):
                    if inside or j > -1:
                        dve.wait_ge(ss_done, j + 1)
                    for n in range(3):
                        dve.wait_ge(sq_done, 3 * j + 4 + n)
                        nc.vector.reduce_sum(sumsq[:, n * H:(n + 1) * H],
                                             sq[:, n * INNER:(n + 1) * INNER].rearrange("p (h d) -> p h d", d=DH),
                                             AX).then_inc(ss_raw, 1)
                    dve.wait_ge(ss_raw, 3 * j + 6)
                    if inside or j > -3:
                        dve.wait_ge(rs_ready, j + 3)
                    nc.vector.tensor_scalar(var_in[:, 0:3 * H], sumsq[:, :], L2_EPS * L2_EPS, None,
                                            ALU.max).then_inc(ss_done, 1)
                if has(j - 1, inside):
                    if inside or j > 1:
                        dve.wait_ge(onT_done, j - 1)
                    dve.wait_ge(pv_done, j)
                    nc.vector.reciprocal(rden[:, 0:H - 1], ps_pv[:, :, DH])
                    nc.vector.reciprocal(rden[:, H - 1:H], ps_pv7[:, DH:DH + 1]).then_inc(rl_done, 1)
                    dve.wait_ge(rl_done, j)
                    nc.vector.tensor_tensor(o_n[:, 0:(H - 1) * DH].rearrange("p (h d) -> p h d", d=DH),
                                            ps_pv[:, :, 0:DH],
                                            rden[:, 0:H - 1].unsqueeze(2).to_broadcast([P, H - 1, DH]), ALU.mult)
                    nc.vector.tensor_scalar(o_n[:, (H - 1) * DH:INNER], ps_pv7[:, 0:DH], rden[:, H - 1:H], None,
                                            ALU.mult).then_inc(on_done, 1)
                dve.wait_ge(rs_ready, j + 4)
                if has(j + 1, inside):
                    if inside or j > -1:
                        dve.wait_ge(qkT_done, 3 * j + 3)
                    for n in range(3):
                        nc.vector.tensor_tensor(qk_hat[:, n * INNER:(n + 1) * INNER].rearrange("p (h d) -> p h d", d=DH),
                                                ps_qk[:, n, :].rearrange("p (h d) -> p h d", d=DH),
                                                rstd[:, par, n * H:(n + 1) * H].unsqueeze(2).to_broadcast([P, H, DH]),
                                                ALU.mult).then_inc(scaled, 1)
                if has(j + 3, inside):
                    if inside or j > -2:
                        dve.wait_ge(xcT_done, j + 2)
                    for n, res in enumerate((x_res, ctx_res)):
                        last = nc.vector.tensor_scalar(xc_hat[:, 1 - par, n, :],
                                                       res[:, bass.ds(j + 3, 1), 0:D].rearrange("p a d -> p (a d)"),
                                                       xc_stat[:, 1 - par, n, 0:1], rstd[:, par, 24 + n:25 + n],
                                                       ALU.subtract, ALU.mult)
                    last.then_inc(hat_ready, 1)
                if has(j - 2, inside):
                    dve.wait_ge(o_cent, j - 1)
                    dve.wait_ge(xb_done, j - 1)
                    nc.vector.scalar_tensor_tensor(x_res[:, bass.ds(j - 2, 1), 0:D].rearrange("p a d -> p (a d)"),
                                                   o_c[:, par, :], rstd[:, par, 26:27], x_b[:, par, :],
                                                   ALU.mult, ALU.add).then_inc(x1_done, 1)

            rounds(run, dve)

        @block.tensor
        def _(pe):
            pe.wait_ge(setup_g, SETUP_G)
            pe.wait_ge(setup_v, 3)
            nc.tensor.transpose(ps[:, 7, 0:P], mask_f[:, :], ident[:, :]).then_inc(s_maskT, 1)
            pe.wait_ge(setup_v, SETUP_V)

            def product(dst, tok_hi, tok_lo, w):
                nc.tensor.matmul(dst, tok_hi, w_hi[:, w:w + INNER], start=True, stop=False)
                nc.tensor.matmul(dst, tok_hi, w_lo[:, w:w + INNER], start=False, stop=False)
                return nc.tensor.matmul(dst, tok_lo, w_hi[:, w:w + INNER], start=False, stop=True)

            def run(j, par, inside=False):
                if has(j, inside):
                    for n in range(3):
                        pe.wait_ge(scaled, 3 * j + 1 + n)
                        for t in range(PAIRS):
                            last = nc.tensor.transpose(ps_qk[:, n, t * P:(t + 1) * P],
                                                       qk_hat[:, n * INNER + t * P:n * INNER + (t + 1) * P], ident[:, :])
                        last.then_inc(qkT_done, 1)
                if has(j, inside):
                    if inside or j > 0:
                        pe.wait_ge(exp_done, 4 * j)
                    for kt in (0, 1):
                        last = product(ps_v[kt], xc_hi[:, par, kt, :], xc_lo[:, par, kt, :], 2 * INNER)
                        last.then_inc(v_done, 1)
                def weighted(heads):
                    for h in heads:
                        dst = ps[:, 6, h * (DH + 1):h * (DH + 1) + VW] if h < H - 1 else ps[:, 3, 0:VW]
                        for kt in (0, 1):
                            last = nc.tensor.matmul(dst, prob[:, kt, h * P:(h + 1) * P], v_sb[:, 1 - par, kt, h, :],
                                                    start=kt == 0, stop=kt == 1)
                    return last

                if has(j - 1, inside):
                    pe.wait_ge(v_copied, 2 * j)
                    pe.wait_ge(exp_done, 4 * j)
                    if inside or j > 1:
                        pe.wait_ge(on_done, j - 1)
                    weighted(range(H // 2))
                if has(j + 1, inside):
                    pe.wait_ge(hi_done, j + 2)
                    pe.wait_ge(lo_done, j + 2)
                    for n, (src, w) in enumerate(((0, 0), (0, INNER), (1, INNER))):
                        if has(j, inside):
                            if n == 0:
                                pe.wait_ge(qlo_done, j + 1)
                            else:
                                pe.wait_ge(klo_done, 2 * j + n)
                        last = product(ps_qk[:, n, :], xc_hi[:, 1 - par, src, :], xc_lo[:, 1 - par, src, :], w)
                        last.then_inc(qk_done, 1)
                if has(j - 1, inside):
                    weighted(range(H // 2, H)).then_inc(pv_done, 1)
                if has(j + 2, inside):
                    pe.wait_ge(hat_ready, j + 3)
                    if has(j + 1, inside):
                        pe.wait_ge(xct_sb, j + 2)
                    if has(j - 2, inside):
                        pe.wait_ge(o_cent, j - 1)
                    for n in (0, 1):
                        last = nc.tensor.transpose(ps_xc[:, n * P:(n + 1) * P], xc_hat[:, par, n, :], ident[:, :])
                    last.then_inc(xcT_done, 1)
                def scores(units):
                    for n in units:
                        if n < 2:
                            pe.wait_ge(v_copied, 2 * j + n + 1)
                        elif n == 2:
                            if inside or j > 0:
                                pe.wait_ge(ot_done, j)
                        else:
                            pe.wait_ge(exp_done, 4 * j + 1)
                        for t in (0, 1):
                            pair = n % 2 * 2 + t
                            keys = slice(pair * P, (pair + 1) * P)
                            for m, (k, q) in enumerate(((k_hi, q_hi), (k_hi, q_lo), (k_lo, q_hi))):
                                last = nc.tensor.matmul(ps_s[n][:, t * 2 * P:(t + 1) * 2 * P], k[:, n // 2, keys],
                                                        q[:, pair, :, :].rearrange("p a q -> p (a q)"),
                                                        start=m == 0, stop=m == 2)
                        last.then_inc(sim_done, 1)

                if has(j, inside):
                    pe.wait_ge(qlo_done, j + 1)
                    pe.wait_ge(klo_done, 2 * j + 2)
                    scores((0, 1))
                if has(j - 1, inside):
                    pe.wait_ge(on_done, j)
                    for t in range(PAIRS):
                        last = nc.tensor.transpose(ps_ot[:, t * P:(t + 1) * P], o_n[:, t * P:(t + 1) * P], ident[:, :])
                    last.then_inc(onT_done, 1)
                if has(j, inside):
                    scores((3,))
                if has(j - 1, inside):
                    pe.wait_ge(ot_done, j)
                    if not has(j + 2, inside) and has(j - 2, inside):
                        pe.wait_ge(o_cent, j - 1)
                    if not has(j + 2, inside) and has(j + 1, inside):
                        pe.wait_ge(xct_sb, j + 2)
                    for t in range(PAIRS):
                        last = nc.tensor.matmul(ps_o, o_t[:, t * P:(t + 1) * P], wo_sb[:, t, :],
                                                start=t == 0, stop=t == PAIRS - 1)
                    last.then_inc(wo_done, 1)
                if has(j, inside):
                    scores((2,))

            rounds(run, pe)


def part_rows(B):
    return B * P + P


def ffn_xattn_route(nc, x_res, ctx_res, ident, w1_all, w2_all, total, sorted_rows, weight_q, weight_scale, bias, We, W2,
                    Wr, br, F1, F2):
    B = ctx_res.shape[1]
    D = ctx_res.shape[2]
    E, F = F1.shape[0], F1.shape[1]
    C = F // P
    XW = x_res.shape[2]
    PART = part_rows(B)
    NG = B // G
    L = 3 * G
    with ExitStack() as stack:
        def sb(name, shape, dt=F32):
            return stack.enter_context(nc.sbuf_tensor(name, shape, dt))

        def sem(name):
            return stack.enter_context(nc.semaphore(name))

        wq_raw = sb("wq_raw", [P, D], I8)
        wq_f = sb("wq_f", [P, D])
        wq_t = sb("wq_t", [P, D], BF16)
        we_raw = sb("we_raw", [P, D])
        w2_raw = sb("w2_raw", [P, D])
        we_t = sb("we_t", [P, D])
        w2_t = sb("w2_t", [P, D])
        wr_t = sb("wr_t", [P, E])
        ws_b = sb("ws_b", [P, D])
        bias_b = sb("bias_b", [P, D])
        ident_bf = sb("ident_bf", [P, P], BF16)
        eps_t = sb("eps_t", [P, L])
        lift2 = sb("lift2", [P, 1])
        three2 = sb("three2", [P, L])
        upper = sb("upper", [P, P])
        ones_pp = sb("ones_pp", [P, P])
        br_b = sb("br_b", [P, E])
        rev_i = sb("rev_i", [P, E], I32)
        rev_f = sb("rev_f", [P, E])
        part_i = sb("part_i", [P, E], I32)
        part_f = sb("part_f", [P, E])
        w1_raw = sb("w1_raw", [P, 4, C, D])
        w2e_raw = sb("w2e_raw", [P, 4, F])
        lg = sb("lg", [P, G, E])
        lmax = sb("lmax", [P, G])
        cand = sb("cand", [P, G, E])
        cmax = sb("cmax", [P, G])
        onehot = sb("onehot", [P, G, E])
        before = sb("before", [P, E])
        gsum = sb("gsum", [P, E])
        place = sb("place", [P, G, E])
        own = sb("own", [P, G, E])
        slot = sb("slot", [P, G])
        stage = sb("stage", [P, 2, G, XW])
        idx = sb("idx", [P, 2, G], U32)
        bn = sb("bn", [P, L, 6])
        stat = sb("stat", [P, 2, L, 2])
        g_var = sb("g_var", [P, L])
        g_ln = sb("g_ln", [P, L])
        g_y0 = sb("g_y0", [P, L])
        g_y2 = sb("g_y2", [P, L])
        g_half = sb("g_half", [P, L])
        g_vy = sb("g_vy", [P, L])
        g_r = sb("g_r", [P, L])
        g_rstd = sb("g_rstd", [P, 2, L])
        t_a = sb("t_a", [P, G, D])
        amax = sb("amax", [P, G])
        q_step = sb("q_step", [P, G])
        q_inv = sb("q_inv", [P, G])
        q_round = sb("q_round", [P, G, D])
        q_bf = sb("q_bf", [P, G, D], BF16)
        q_t = sb("q_t", [P, G, P], BF16)
        xb = sb("xb", [P, G, D])
        y_a = sb("y_a", [P, G, D])
        t_b = sb("t_b", [P, G, D])
        tb_t = sb("tb_t", [P, G, P])
        ctx_now = sb("ctx_now", [P, G, D])
        ctx_t = sb("ctx_t", [P, G, P])
        ke_t = sb("ke_t", [P, G, P])
        smax = sb("smax", [P, G])
        nmax = sb("nmax", [P, G])
        probs = sb("probs", [P, G, P])
        ssum = sb("ssum", [P, G])
        sinv = sb("sinv", [P, G])
        v_s = sb("v_s", [P, G, D])
        c_cent = sb("c_cent", [P, G, D])
        t_c = sb("t_c", [P, G, D])
        tc_t = sb("tc_t", [P, G, P])

        ps = stack.enter_context(nc.psum_tensor("ps2", [P, 7, 512], F32))
        ps_q = stack.enter_context(nc.psum_tensor("ps_q", [P, 1024], BF16))
        ps_ctx, ps_ke, ps_v, ps_acc, ps_t, ps_s, ps_o = (
            ps[:, n, :].rearrange("p (g d) -> p g d", d=D) for n in range(7))
        ps_qt = ps_q[:, 0:G * P].rearrange("p (g d) -> p g d", d=P)
        ps_lg = ps_q[:, 512:512 + 2 * G * E].bitcast(F32)
        ps_rank = ps_q[:, 640:640 + 2 * G * E].bitcast(F32)

        names = ("ld", "setup_g", "setup_v", "setup_t", "setup_c", "a_stats", "a_aggr", "a_var", "a_ln", "a_y0",
                 "a_n1", "a_n2", "a_n3", "a_rs", "ta_done", "amax_done", "step_done", "inv_done", "q1_done", "q2_done", "qT_done",
                 "qt_copied", "acc_done", "ya_done", "xb2_done", "x2_done", "tb_done", "tbT_done", "tb_copied",
                 "ctxT_done", "ctx_copied", "ke_done", "ke_copied", "v2_done", "sc_done", "smax_done",
                 "nmax_done", "pr_done", "sinv_done", "vs_done", "out_done", "x3_done", "cc_done", "tc_done",
                 "tcT_done", "tc_copied", "lg_done", "lg_copied", "cols_done", "ctx_taken",
                 "lmax_done", "ge_done", "cand_done", "cmax_done", "oh_done", "rank_done", "place_done", "gsum_done",
                 "own_done", "before_done", "slot_done", "staged", "sent0", "sent1", "wT_done", "w_copied", "tot_done")
        s = {n: sem("m_" + n) for n in names}
        ld_raw = [sem(f"m_raw{n}") for n in range(4)]

        FIRST = 6

        def rounds(run, eng):
            for j in range(FIRST):
                run(j, j % 2, j // 2)
            with eng.Fori(0, (NG - FIRST) // 2) as turn:
                run(FIRST + 2 * turn, 0, FIRST // 2 + turn, True)
                run(FIRST + 1 + 2 * turn, 1, FIRST // 2 + turn, True)
            for j in range(NG, NG + 5):
                run(j, j % 2, j // 2)

        def has(g, inside):
            return inside or 0 <= g < NG

        def after(eng, name, g, inside):
            if inside or g >= 0:
                eng.wait_ge(s[name], (g if inside else min(g, NG - 1)) + 1)

        def grp(res, g, w=slice(0, D)):
            return res[:, bass.ds(G * g, G), w]

        def one(res, g, i):
            return res[:, bass.ds(G * g + i, 1), 0:D].rearrange("p a d -> p (a d)")

        block = stack.enter_context(nc.Block())

        @block.sync
        def _(sp):
            sp.dma_start(wq_raw[:, :], weight_q).then_inc(s["ld"], 16)
            sp.dma_start(we_raw[:, :], We).then_inc(s["ld"], 16)
            sp.dma_start(w2_raw[:, :], W2).then_inc(s["ld"], 16)
            sp.dma_start(wr_t[:, :], Wr.rearrange("e d -> d e"), allow_slow_non_contiguous=True).then_inc(s["ld"], 16)
            sp.dma_start(ws_b[:, :], weight_scale.partition_broadcast(P)).then_inc(s["ld"], 16)
            sp.dma_start(bias_b[:, :], bias.partition_broadcast(P)).then_inc(s["ld"], 16)
            sp.dma_start(br_b[:, :], br.partition_broadcast(P)).then_inc(s["ld"], 16)
            for e in range(E):
                if e > 3:
                    sp.wait_ge(s["wT_done"], 2 * (e - 3))
                sp.dma_start(w1_raw[:, e % 4], F1[e].rearrange("(c p) d -> p c d", p=P)).then_inc(ld_raw[e % 4], 16)
                sp.dma_start(w2e_raw[:, e % 4], F2[e]).then_inc(ld_raw[e % 4], 16)
            sp.wait_ge(s["sent0"], 8 * B)
            sp.wait_ge(s["sent1"], 8 * B)

        @block.scalar
        def _(act):
            act.wait_ge(s["setup_t"], 1)
            nc.scalar.activation(wq_t[:, :], ps_ctx[:, 0, :], ACT.Copy).then_inc(s["setup_c"], 1)
            nc.scalar.activation(we_t[:, :], ps_ctx[:, 1, :], ACT.Copy).then_inc(s["setup_c"], 1)
            nc.scalar.activation(w2_t[:, :], ps_ctx[:, 2, :], ACT.Copy).then_inc(s["setup_c"], 1)
            act.wait_ge(s["setup_g"], 3)
            nc.scalar.preload_act_table_set("natural_log_exp_and_others")

            def run(j, par, half, inside=False):
                if has(j - 2, inside):
                    after(act, "sinv_done", j - 2, inside)
                    after(act, "v2_done", j - 2, inside)
                    after(act, "out_done", j - 3, inside)
                    for i in range(G):
                        last = nc.scalar.activation(v_s[:, i, :], ps_v[:, i, :], ACT.Copy, scale=sinv[:, i:i + 1])
                    last.then_inc(s["vs_done"], 1)
                if has(j, inside) or has(j - 1, inside) or has(j - 3, inside):
                    act.wait_ge(s["a_var"], j + 1)
                    after(act, "a_rs", j - 1, inside)
                    nc.scalar.activation(g_ln[:, :], g_var[:, :], ACT.Ln, scale=float(2 ** LN_LIFT)).then_inc(s["a_ln"], 1)
                    act.wait_ge(s["a_ln"], j + 1)
                    nc.scalar.activation(g_y0[:, :], g_ln[:, :], ACT.Exp, scale=-0.5, bias=lift2[:, 0:1]).then_inc(s["a_y0"], 1)
                if has(j - 1, inside):
                    after(act, "ctxT_done", j - 1, inside)
                    after(act, "v2_done", j - 2, inside)
                    nc.scalar.activation(ctx_t[:, :, :], ps_ctx, ACT.Copy).then_inc(s["ctx_copied"], 1)
                if has(j - 1, inside):
                    after(act, "tbT_done", j - 1, inside)
                    after(act, "sc_done", j - 2, inside)
                    nc.scalar.activation(tb_t[:, :, :], ps_t, ACT.Copy).then_inc(s["tb_copied"], 1)
                if has(j - 1, inside):
                    after(act, "ke_done", j - 1, inside)
                    after(act, "sc_done", j - 2, inside)
                    nc.scalar.activation(ke_t[:, :, :], ps_ke, ACT.Copy).then_inc(s["ke_copied"], 1)
                if has(j, inside):
                    after(act, "qT_done", j, inside)
                    after(act, "acc_done", j - 1, inside)
                    nc.scalar.activation(q_t[:, :, :], ps_qt, ACT.Copy).then_inc(s["qt_copied"], 1)
                if has(j - 3, inside):
                    after(act, "tcT_done", j - 3, inside)
                    after(act, "lg_done", j - 4, inside)
                    nc.scalar.activation(tc_t[:, :, :], ps_t, ACT.Copy).then_inc(s["tc_copied"], 1)
                if has(j - 1, inside):
                    after(act, "nmax_done", j - 1, inside)
                    after(act, "out_done", j - 2, inside)
                    after(act, "sinv_done", j - 2, inside)
                    for i in range(G):
                        last = nc.scalar.activation(probs[:, i, :], ps_s[:, i, :], ACT.Exp, bias=nmax[:, i:i + 1],
                                                    accum_out=ssum[:, i:i + 1])
                    last.then_inc(s["pr_done"], 1)

                if not inside and j > NG:
                    for e in (2 * (j - NG - 1), 2 * (j - NG - 1) + 1):
                        act.wait_ge(s["wT_done"], 2 * e + 1)
                        nc.scalar.activation(w1_all[:, e, 0:F], ps[:, 3, :], ACT.Copy).then_inc(s["w_copied"], 1)
                        act.wait_ge(s["wT_done"], 2 * e + 2)
                        nc.scalar.activation(w2_all[:, e, 0:F], ps[:, 1, :], ACT.Copy).then_inc(s["w_copied"], 1)

            rounds(run, act)

        @block.gpsimd
        def _(pool):
            nc.gpsimd.memset(eps_t[:, :], LN_EPS).then_inc(s["setup_g"], 1)
            nc.gpsimd.memset(three2[:, :], 3.0).then_inc(s["setup_g"], 1)
            nc.gpsimd.memset(lift2[:, :], 0.5 * LN_LIFT * LN2).then_inc(s["setup_g"], 1)
            nc.gpsimd.memset(upper[:, :], 1.0).then_inc(s["setup_g"], 1)
            nc.gpsimd.memset(ones_pp[:, :], 1.0).then_inc(s["setup_g"], 1)
            nc.gpsimd.memset(before[:, :], 0.0).then_inc(s["setup_g"], 1)
            nc.gpsimd.iota(rev_i[:, :], pattern=[[-1, E]], base=E, channel_multiplier=0).then_inc(s["setup_g"], 1)
            nc.gpsimd.iota(part_i[:, :], pattern=[[PART, E]], base=0, channel_multiplier=0).then_inc(s["setup_g"], 1)
            pool.wait_ge(s["setup_g"], 8)
            nc.gpsimd.affine_select(out=upper[:, :], in_=upper[:, :], compare_op=ALU.is_gt, fill=0.0,
                                    base=0, pattern=[[1, P]], channel_multiplier=-1).then_inc(s["setup_g"], 1)
            pool.wait_ge(s["setup_g"], 9)
            pool.wait_ge(s["ld"], 112)
            pool.wait_ge(s["setup_v"], 5)

            def run(j, par, half, inside=False):
                if has(j, inside) or has(j - 1, inside) or has(j - 3, inside):
                    after(pool, "a_rs", j - 1, inside)
                    pool.wait_ge(s["a_aggr"], j + 1)
                    nc.gpsimd.tensor_tensor(g_var[:, :], stat[:, par, :, 1], eps_t[:, :], ALU.add).then_inc(s["a_var"], 1)
                if has(j, inside) or has(j - 1, inside) or has(j - 3, inside):
                    pool.wait_ge(s["a_y0"], j + 1)
                    nc.gpsimd.tensor_tensor(g_y2[:, :], g_y0[:, :], g_y0[:, :], ALU.mult)
                    nc.gpsimd.tensor_scalar(g_half[:, :], g_y0[:, :], -0.5, None, ALU.mult).then_inc(s["a_n1"], 1)
                    pool.wait_ge(s["a_n1"], j + 1)
                    nc.gpsimd.tensor_tensor(g_vy[:, :], g_y2[:, :], g_var[:, :], ALU.mult).then_inc(s["a_n2"], 1)
                    pool.wait_ge(s["a_n2"], j + 1)
                    nc.gpsimd.tensor_tensor(g_r[:, :], g_vy[:, :], three2[:, :], ALU.subtract).then_inc(s["a_n3"], 1)
                    pool.wait_ge(s["a_n3"], j + 1)
                    after(pool, "tb_done", j - 3, inside)
                    after(pool, "ta_done", j - 2, inside)
                    after(pool, "cols_done", j - 5, inside)
                    nc.gpsimd.tensor_tensor(g_rstd[:, par, :], g_r[:, :], g_half[:, :], ALU.mult).then_inc(s["a_rs"], 1)
                if has(j - 3, inside):
                    after(pool, "tc_done", j - 4, inside)
                    if has(j - 5, inside):
                        after(pool, "staged", j - 5, inside)
                    pool.wait_ge(s["a_rs"], j + 1)
                    nc.gpsimd.tensor_tensor(c_cent[:, :, :], grp(x_res, j - 3),
                                            stat[:, par, 2 * G:L, 0:1].to_broadcast([P, G, D]), ALU.subtract).then_inc(s["cc_done"], 1)
                    after(pool, "cc_done", j - 3, inside)
                    after(pool, "tcT_done", j - 4, inside)
                    nc.gpsimd.tensor_tensor(t_c[:, :, :], c_cent[:, :, :],
                                            g_rstd[:, par, 2 * G:L].unsqueeze(2).to_broadcast([P, G, D]), ALU.mult).then_inc(s["tc_done"], 1)
                if has(j, inside):
                    after(pool, "x2_done", j - 1, inside)
                    nc.gpsimd.tensor_tensor(xb[:, :, :], grp(x_res, j),
                                            bias_b[:, :].unsqueeze(1).to_broadcast([P, G, D]), ALU.add).then_inc(s["xb2_done"], 1)

                if has(j - 5, inside):
                    if not has(j - 3, inside):
                        after(pool, "staged", j - 5, inside)
                    for i in range(G):
                        nc.gpsimd.indirect_dma_start(
                            out=sorted_rows, out_offset=bass.IndirectOffsetOnAxis(ap=idx[:, 1 - par, i:i + 1], axis=0),
                            in_=stage[:, 1 - par, i, :], in_offset=None).then_inc(s[f"sent{1 - par}"], 16)

            rounds(run, pool)

        @block.vector
        def _(dve):
            dve.wait_ge(s["ld"], 112)
            nc.vector.tensor_copy(wq_f[:, :], wq_raw[:, :]).then_inc(s["setup_v"], 1)
            nc.vector.tensor_copy(ident_bf[:, :], ident[:, :]).then_inc(s["setup_v"], 1)
            nc.vector.memset(stat[:, :, :, :], 1.0).then_inc(s["setup_v"], 1)
            dve.wait_ge(s["setup_g"], 9)
            nc.vector.tensor_copy(rev_f[:, :], rev_i[:, :]).then_inc(s["setup_v"], 1)
            nc.vector.tensor_copy(part_f[:, :], part_i[:, :]).then_inc(s["setup_v"], 1)
            dve.wait_ge(s["setup_v"], 5)

            def run(j, par, half, inside=False):
                kinds = [(n, g) for n, g in ((0, j), (1, j - 1), (2, j - 3)) if has(g, inside)]
                live = bool(kinds)
                if live:
                    after(dve, "a_aggr", j - 1, inside)
                    after(dve, "x2_done", j - 1, inside)
                    after(dve, "x3_done", j - 3, inside)
                    for n, g in kinds:
                        for i in range(G):
                            last = nc.vector.bn_stats(bn[:, n * G + i, :], one(x_res, g, i))
                    last.then_inc(s["a_stats"], 1)
                if live:
                    after(dve, "tc_done", j - 5, inside)
                    after(dve, "cols_done", j - 5, inside)
                    after(dve, "a_var", j - 2, inside)
                    dve.wait_ge(s["a_stats"], j + 1)
                if has(j - 2, inside):
                    after(dve, "vs_done", j - 3, inside)
                    after(dve, "pr_done", j - 2, inside)
                    nc.vector.reciprocal(sinv[:, :], ssum[:, :]).then_inc(s["sinv_done"], 1)
                if live:
                    for n, g in kinds:
                        for i in range(G):
                            last = nc.vector.bn_aggr(stat[:, par, n * G + i, :], bn[:, n * G + i, :])
                    last.then_inc(s["a_aggr"], 1)
                if has(j - 4, inside):
                    after(dve, "lg_done", j - 4, inside)
                    after(dve, "ge_done", j - 5, inside)
                    bias_all = br_b[:, :].unsqueeze(1).to_broadcast([P, G, E])
                    nc.vector.tensor_tensor(lg[:, :, :], ps_lg.rearrange("p (g e) -> p g e", e=E), bias_all,
                                            ALU.add).then_inc(s["lg_copied"], 1)
                    after(dve, "lg_copied", j - 4, inside)
                    nc.vector.reduce_max(lmax[:, :], lg[:, :, :], AX).then_inc(s["lmax_done"], 1)
                    after(dve, "lmax_done", j - 4, inside)
                    after(dve, "oh_done", j - 5, inside)
                    nc.vector.tensor_tensor(cand[:, :, :], lg[:, :, :], lmax[:, :].unsqueeze(2).to_broadcast([P, G, E]),
                                            ALU.is_ge).then_inc(s["ge_done"], 1)
                if has(j - 1, inside):
                    after(dve, "ctxT_done", j - 2, inside)
                    nc.vector.tensor_copy(ctx_now[:, :, :], grp(ctx_res, j - 1)).then_inc(s["ctx_taken"], 1)
                if has(j - 4, inside):
                    after(dve, "ge_done", j - 4, inside)
                    nc.vector.tensor_tensor(cand[:, :, :], cand[:, :, :], rev_f[:, :].unsqueeze(1).to_broadcast([P, G, E]),
                                            ALU.mult).then_inc(s["cand_done"], 1)
                    after(dve, "cand_done", j - 4, inside)
                    nc.vector.reduce_max(cmax[:, :], cand[:, :, :], AX).then_inc(s["cmax_done"], 1)
                    after(dve, "cmax_done", j - 4, inside)
                    after(dve, "own_done", j - 5, inside)
                    after(dve, "gsum_done", j - 5, inside)
                    nc.vector.tensor_tensor(onehot[:, :, :], cand[:, :, :],
                                            cmax[:, :].unsqueeze(2).to_broadcast([P, G, E]),
                                            ALU.is_equal).then_inc(s["oh_done"], 1)
                if live:
                    dve.wait_ge(s["a_rs"], j + 1)
                if has(j - 1, inside):
                    after(dve, "tbT_done", j - 2, inside)
                    for i in range(G):
                        last = nc.vector.tensor_scalar(t_b[:, i, :], one(x_res, j - 1, i), stat[:, par, G + i, 0:1],
                                                       g_rstd[:, par, G + i:G + i + 1], ALU.subtract, ALU.mult)
                    last.then_inc(s["tb_done"], 1)
                if has(j, inside):
                    after(dve, "q1_done", j - 1, inside)
                    for i in range(G):
                        last = nc.vector.tensor_scalar(t_a[:, i, :], one(x_res, j, i), stat[:, par, i, 0:1],
                                                       g_rstd[:, par, i:i + 1], ALU.subtract, ALU.mult)
                    last.then_inc(s["ta_done"], 1)
                    after(dve, "ta_done", j, inside)
                    nc.vector.tensor_reduce(amax[:, :], t_a[:, :, :], AX, ALU.max, apply_absolute_value=True).then_inc(s["amax_done"], 1)
                if has(j - 2, inside):
                    after(dve, "out_done", j - 2, inside)
                    nc.vector.tensor_tensor(grp(x_res, j - 2), grp(x_res, j - 2), ps_o, ALU.add).then_inc(s["x3_done"], 1)
                if has(j, inside):
                    after(dve, "amax_done", j, inside)
                    after(dve, "ya_done", j - 1, inside)
                    nc.vector.tensor_scalar(q_step[:, :], amax[:, :], Q_EPS, 1.0 / Q_MAX, ALU.max, ALU.mult).then_inc(s["step_done"], 1)
                    after(dve, "step_done", j, inside)
                    nc.vector.reciprocal(q_inv[:, :], q_step[:, :]).then_inc(s["inv_done"], 1)
                if has(j - 3, inside):
                    nc.vector.tensor_copy(grp(x_res, j - 3, slice(D, D + 1)), stat[:, par, 2 * G:L, 0:1])
                    nc.vector.tensor_copy(grp(x_res, j - 3, slice(D + 1, D + 2)),
                                          g_rstd[:, par, 2 * G:L].unsqueeze(2)).then_inc(s["cols_done"], 1)
                if has(j, inside):
                    after(dve, "inv_done", j, inside)
                    after(dve, "q2_done", j - 1, inside)
                    for i in range(G):
                        last = nc.vector.tensor_scalar(q_round[:, i, :], t_a[:, i, :], q_inv[:, i:i + 1], ROUND,
                                                       ALU.mult, ALU.add)
                    last.then_inc(s["q1_done"], 1)
                    after(dve, "q1_done", j, inside)
                    after(dve, "qT_done", j - 1, inside)
                    nc.vector.tensor_scalar(q_bf[:, :, :], q_round[:, :, :], ROUND, Q_MAX, ALU.subtract,
                                            ALU.min).then_inc(s["q2_done"], 1)
                if has(j - 1, inside):
                    after(dve, "sc_done", j - 1, inside)
                    nc.vector.reduce_max(smax[:, :], ps_s, AX).then_inc(s["smax_done"], 1)
                    after(dve, "smax_done", j - 1, inside)
                    after(dve, "pr_done", j - 2, inside)
                    nc.vector.tensor_scalar(nmax[:, :], smax[:, :], -1.0, None, ALU.mult).then_inc(s["nmax_done"], 1)
                if has(j, inside):
                    after(dve, "acc_done", j, inside)
                    after(dve, "x2_done", j - 1, inside)
                    for i in range(G):
                        last = nc.vector.scalar_tensor_tensor(y_a[:, i, :], ps_acc[:, i, :], q_step[:, i:i + 1],
                                                              ws_b[:, :], ALU.mult, ALU.mult)
                    last.then_inc(s["ya_done"], 1)
                if has(j - 4, inside):
                    after(dve, "rank_done", j - 4, inside)
                    after(dve, "own_done", j - 5, inside)
                    nc.vector.tensor_tensor(place[:, :, :], ps_rank.rearrange("p (g e) -> p g e", e=E),
                                            part_f[:, :].unsqueeze(1).to_broadcast([P, G, E]), ALU.add).then_inc(s["place_done"], 1)
                    after(dve, "before_done", j - 5, inside)
                    nc.vector.reduce_sum(gsum[:, :], onehot[:, :, :].rearrange("p g e -> p e g"), AX).then_inc(s["gsum_done"], 1)
                if has(j, inside):
                    after(dve, "ya_done", j, inside)
                    after(dve, "xb2_done", j, inside)
                    nc.vector.tensor_tensor(grp(x_res, j), y_a[:, :, :], xb[:, :, :], ALU.add).then_inc(s["x2_done"], 1)

                if has(j - 4, inside):
                    after(dve, "place_done", j - 4, inside)
                    after(dve, "slot_done", j - 5, inside)
                    nc.vector.tensor_tensor(own[:, :, :], place[:, :, :], onehot[:, :, :], ALU.mult).then_inc(s["own_done"], 1)
                    after(dve, "gsum_done", j - 4, inside)
                    nc.vector.tensor_tensor(before[:, :], before[:, :], gsum[:, :], ALU.add).then_inc(s["before_done"], 1)
                    after(dve, "own_done", j - 4, inside)
                    after(dve, "staged", j - 5, inside)
                    nc.vector.reduce_sum(slot[:, :], own[:, :, :], AX).then_inc(s["slot_done"], 1)
                    after(dve, "slot_done", j - 4, inside)
                    if inside or j > 5:
                        dve.wait_ge(s[f"sent{par}"], 16 * G * (half - 2))
                    nc.vector.tensor_copy(idx[:, par, :], slot[:, :])
                    nc.vector.tensor_copy(stage[:, par, :, :], grp(x_res, j - 4, slice(0, XW))).then_inc(s["staged"], 1)

            rounds(run, dve)
            dve.wait_ge(s["tot_done"], 1)
            nc.vector.tensor_copy(total[:, :], ps[:, 0, 0:E])

        @block.tensor
        def _(pe):
            pe.wait_ge(s["setup_v"], 2)
            pe.wait_ge(s["ld"], 112)
            nc.tensor.transpose(ps_ctx[:, 0, :], wq_f[:, :], ident[:, :])
            nc.tensor.transpose(ps_ctx[:, 1, :], we_raw[:, :], ident[:, :])
            nc.tensor.transpose(ps_ctx[:, 2, :], w2_raw[:, :], ident[:, :]).then_inc(s["setup_t"], 1)
            pe.wait_ge(s["setup_c"], 3)

            def run(j, par, half, inside=False):
                if has(j - 2, inside):
                    after(pe, "vs_done", j - 2, inside)
                    after(pe, "x3_done", j - 3, inside)
                    for i in range(G):
                        last = nc.tensor.matmul(ps_o[:, i, :], probs[:, i, :], v_s[:, i, :], start=True, stop=True)
                    last.then_inc(s["out_done"], 1)
                if has(j - 1, inside):
                    after(pe, "ctx_taken", j - 1, inside)
                    after(pe, "ctx_copied", j - 2, inside)
                    for i in range(G):
                        last = nc.tensor.transpose(ps_ctx[:, i, :], ctx_now[:, i, :], ident[:, :])
                    last.then_inc(s["ctxT_done"], 1)
                if has(j - 1, inside):
                    after(pe, "tb_done", j - 1, inside)
                    after(pe, "tc_copied", j - 4, inside)
                    for i in range(G):
                        last = nc.tensor.transpose(ps_t[:, i, :], t_b[:, i, :], ident[:, :])
                    last.then_inc(s["tbT_done"], 1)
                if has(j - 1, inside):
                    after(pe, "ctx_copied", j - 1, inside)
                    after(pe, "ke_copied", j - 2, inside)
                    nc.tensor.matmul(ps[:, 1, :], we_t[:, :], ctx_t[:, :, :].rearrange("p g m -> p (g m)"),
                                     start=True, stop=True).then_inc(s["ke_done"], 1)
                if has(j - 1, inside):
                    after(pe, "tb_copied", j - 1, inside)
                    after(pe, "ke_copied", j - 1, inside)
                    after(pe, "pr_done", j - 2, inside)
                    for i in range(G):
                        last = nc.tensor.matmul(ps_s[:, i, :], ke_t[:, i, :], tb_t[:, i, :], start=True, stop=True)
                    last.then_inc(s["sc_done"], 1)
                if has(j, inside):
                    after(pe, "q2_done", j, inside)
                    after(pe, "place_done", j - 5, inside)
                    after(pe, "lg_copied", j - 4, inside)
                    for i in range(G):
                        last = nc.tensor.transpose(ps_qt[:, i, :], q_bf[:, i, :], ident_bf[:, :])
                    last.then_inc(s["qT_done"], 1)
                if has(j, inside):
                    after(pe, "qt_copied", j, inside)
                    for i in range(G):
                        last = nc.tensor.matmul(ps_acc[:, i, :], q_t[:, i, :], wq_t[:, :], start=True, stop=True)
                    last.then_inc(s["acc_done"], 1)
                if has(j - 4, inside):
                    after(pe, "oh_done", j - 4, inside)
                    after(pe, "before_done", j - 5, inside)
                    if not has(j, inside):
                        after(pe, "qt_copied", NG - 1, inside)
                    nc.tensor.matmul(ps_rank, upper[:, :], onehot[:, :, :].rearrange("p g e -> p (g e)"),
                                     start=True, stop=False)
                    for i in range(G - 1):
                        nc.tensor.matmul(ps_rank[:, (i + 1) * E:], ones_pp[:, :],
                                         onehot[:, i:i + 1, :].to_broadcast([P, G - 1 - i, E]), start=False, stop=False)
                    nc.tensor.matmul(ps_rank, ones_pp[:, :], before[:, :].unsqueeze(1).to_broadcast([P, G, E]),
                                     start=False, stop=True).then_inc(s["rank_done"], 1)
                if has(j - 1, inside):
                    after(pe, "vs_done", j - 2, inside)
                    for i in range(G):
                        last = nc.tensor.matmul(ps_v[:, i, :], ctx_t[:, i, :], w2_t[:, :], start=True, stop=True)
                    last.then_inc(s["v2_done"], 1)
                if has(j - 3, inside):
                    after(pe, "tc_done", j - 3, inside)
                    after(pe, "tb_copied", j - 1, inside)
                    for i in range(G):
                        last = nc.tensor.transpose(ps_t[:, i, :], t_c[:, i, :], ident[:, :])
                    last.then_inc(s["tcT_done"], 1)
                    after(pe, "tc_copied", j - 3, inside)
                    after(pe, "lg_copied", j - 4, inside)
                    after(pe, "place_done", j - 4, inside)
                    for i in range(G):
                        last = nc.tensor.matmul(ps_lg[:, i * E:(i + 1) * E], tc_t[:, i, :], wr_t[:, :],
                                                start=True, stop=True)
                    last.then_inc(s["lg_done"], 1)

                if not inside and j > NG:
                    if j == NG + 1:
                        after(pe, "ya_done", NG - 1, inside)
                        after(pe, "ke_copied", NG - 1, inside)
                    for e in (2 * (j - NG - 1), 2 * (j - NG - 1) + 1):
                        pe.wait_ge(ld_raw[e % 4], 32 * (e // 4 + 1))
                        for half_n, (raw, bank) in enumerate(((w1_raw[:, e % 4].rearrange("p c d -> p (c d)"), 3),
                                                              (w2e_raw[:, e % 4, :], 1))):
                            if 2 * e + half_n > 1:
                                pe.wait_ge(s["w_copied"], 2 * e + half_n - 1)
                            for c in range(C):
                                last = nc.tensor.transpose(ps[:, bank, c * P:(c + 1) * P], raw[:, c * P:(c + 1) * P],
                                                           ident[:, :])
                            last.then_inc(s["wT_done"], 1)

            rounds(run, pe)
            after(pe, "before_done", NG - 1, False)
            nc.tensor.matmul(ps[:, 0, 0:E], ones_pp[:, :], before[:, :], start=True, stop=True).then_inc(s["tot_done"], 1)


def experts_program(nc, B, T, ident, w1_all, w2_all, total, sorted_rows, F1, b1, b2, out):
    E, F, D = F1.shape
    XW = sorted_rows.shape[1]
    PART = part_rows(B)
    C = F // P
    TOK = B * P
    W1C = F + C
    W2C = F + D
    assert T % DEEP == 0
    out_rows = out.rearrange("b s d -> (b s) d")
    with ExitStack() as stack:
        def sb(name, shape, dt=F32):
            return stack.enter_context(nc.sbuf_tensor(name, shape, dt))

        def sem(name):
            return stack.enter_context(nc.semaphore(name))

        iota_i = sb("iota_i", [P, T], I32)
        iota_f = sb("iota_f", [P, T])
        base_i = sb("base_i", [P, E], I32)
        base_f = sb("base_f", [P, E])
        fill = sb("fill2", [P, XW])
        ntile = sb("ntile", [P, E])
        tend = sb("tend", [P, 2, E])
        skip = sb("skip", [P, E])
        pad_f = sb("pad_f", [P, E])
        pad_idx = sb("pad_idx", [P, E], U32)
        ended = sb("ended", [P, T, E])
        skipped = sb("skipped", [P, T, E])
        texp = sb("texp", [P, T])
        trow = sb("trow", [P, T])
        texp_i = sb("texp_i", [P, T], I32)
        trow_i = sb("trow_i", [P, T], I32)
        rows = sb("rows", [P, T, XW])
        w1_now = sb("w1_now", [P, 2, W1C])
        w2_now = sb("w2_now", [P, 2, W2C])
        t_now = sb("t_now", [P, 2, D])
        t_t = sb("t_t", [P, 2, P])
        h_t = sb("h_t", [P, 2, C, P])
        xb2 = sb("xb2", [P, 2, D])
        o_now = sb("o_now", [P, 2, D])
        o_idx = sb("o_idx", [P, 2, 1], U32)

        ps = stack.enter_context(nc.psum_tensor("ps3", [P, 8, 512], F32))
        ps_h = (ps[:, 0, :], ps[:, 1, :])
        ps_t = (ps[:, 2, 0:P], ps[:, 3, 0:P])
        ps_y = (ps[:, 4, 0:P], ps[:, 5, 0:P])

        names = ("setup_g", "b_in", "r", "padded", "rows_in", "w1_set", "w2_set", "t_set", "T_done", "t_copied",
                 "h_done", "relu_done", "y_done", "xb_set", "fin", "out_sent0", "out_sent1")
        s = {n: sem("e_" + n) for n in names}
        ld = [sem(f"e_ld{n}") for n in range(DEEP)]

        FIRST = 4

        def rounds(run, eng):
            for j in range(-2, FIRST):
                run(j, j % 2, j // 2)
            with eng.Fori(0, (T - 2 - FIRST) // 2) as turn:
                run(FIRST + 2 * turn, 0, FIRST // 2 + turn, True)
                run(FIRST + 1 + 2 * turn, 1, FIRST // 2 + turn, True)
            for j in range(T - 2, T + 1):
                run(j, j % 2, j // 2)

        def has(k, inside):
            return inside or 0 <= k < T

        def after(eng, name, k, inside, n=1):
            if inside or k >= 0:
                eng.wait_ge(s[name], (k + 1) * n)

        def flat(ap):
            return ap.rearrange("p a d -> p (a d)")

        block = stack.enter_context(nc.Block())

        @block.sync
        def _(sp):
            for e in range(E):
                sp.dma_start(w1_all[:, e, F:F + C], b1[e].rearrange("(c p) -> p c", p=P),
                             allow_slow_non_contiguous=True).then_inc(s["b_in"], 16)
                sp.dma_start(w2_all[:, e, F:F + D], b2[e].partition_broadcast(P)).then_inc(s["b_in"], 16)
            sp.wait_ge(s["r"], TABLE_R)
            sp.wait_ge(s["padded"], 16 * E)

            def load(i, n):
                row = sp.value_load(trow_i[0:1, bass.ds(i, 1)], min_val=0, max_val=E * PART + (E - 1) * P)
                sp.dma_start(rows[:, bass.ds(i, 1), :].rearrange("p a w -> p (a w)"),
                             sorted_rows[bass.ds(row, P), :]).then_inc(ld[n], 16)

            for n in range(DEEP):
                load(n, n)
            with sp.Fori(1, T // DEEP) as turn:
                for n in range(DEEP):
                    sp.wait_ge(ld[n], 16 * turn)
                    sp.sem_inc(s["rows_in"], 1)
                    load(DEEP * turn + n, n)
            for n in range(DEEP):
                sp.wait_ge(ld[n], 16 * (T // DEEP))
                sp.sem_inc(s["rows_in"], 1)
            sp.wait_ge(s["out_sent0"], 8 * T)
            sp.wait_ge(s["out_sent1"], 8 * T)

        @block.scalar
        def _(act):
            def run(j, par, half, inside=False):
                if has(j + 1, inside):
                    after(act, "h_done", j - 1, inside)
                    after(act, "T_done", j + 1, inside)
                    nc.scalar.activation(t_t[:, 1 - par, :], ps_t[1 - par], ACT.Copy).then_inc(s["t_copied"], 1)
                if has(j, inside):
                    after(act, "y_done", j - 2, inside)
                    after(act, "h_done", j, inside)
                    for c in range(C):
                        last = nc.scalar.activation(h_t[:, par, c, :], ps_h[par][:, c * P:(c + 1) * P], ACT.Relu,
                                                    bias=w1_now[:, par, F + c:F + c + 1])
                    last.then_inc(s["relu_done"], 1)

            rounds(run, act)

        @block.gpsimd
        def _(pool):
            nc.gpsimd.iota(iota_i[:, :], pattern=[[1, T]], base=0, channel_multiplier=0).then_inc(s["setup_g"], 1)
            nc.gpsimd.iota(base_i[:, :], pattern=[[PART, E]], base=0, channel_multiplier=1).then_inc(s["setup_g"], 1)
            nc.gpsimd.memset(fill[:, :], FILL).then_inc(s["setup_g"], 1)
            pool.wait_ge(s["setup_g"], 3)
            pool.wait_ge(s["r"], PAD_R)
            for e in range(E):
                nc.gpsimd.indirect_dma_start(
                    out=sorted_rows, out_offset=bass.IndirectOffsetOnAxis(ap=pad_idx[:, e:e + 1], axis=0),
                    in_=fill[:, :], in_offset=None).then_inc(s["padded"], 16)

            def run(j, par, half, inside=False):
                if has(j - 1, inside):
                    after(pool, "fin", j - 1, inside)
                if has(j, inside):
                    if not has(j - 1, inside):
                        pool.wait_ge(s["rows_in"], 1)
                    after(pool, "fin", j - 2, inside)
                    after(pool, "w2_set", j, inside)
                    nc.gpsimd.tensor_tensor(xb2[:, par, :], flat(rows[:, bass.ds(j, 1), 0:D]), w2_now[:, par, F:W2C],
                                            ALU.add).then_inc(s["xb_set"], 1)
                if has(j - 1, inside):
                    nc.gpsimd.indirect_dma_start(
                        out=out_rows, out_offset=bass.IndirectOffsetOnAxis(ap=o_idx[:, 1 - par, :], axis=0),
                        in_=o_now[:, 1 - par, :], in_offset=None, bounds_check=TOK - 1,
                        oob_is_err=False).then_inc(s[f"out_sent{1 - par}"], 16)

            rounds(run, pool)

        @block.vector
        def _(dve):
            dve.wait_ge(s["setup_g"], 3)
            n_r = [0]

            def step(ins):
                ins.then_inc(s["r"], 1)
                n_r[0] += 1
                dve.wait_ge(s["r"], n_r[0])

            nc.vector.tensor_copy(iota_f[:, :], iota_i[:, :])
            step(nc.vector.tensor_copy(base_f[:, :], base_i[:, :]))
            step(nc.vector.tensor_tensor(pad_f[:, :], base_f[:, :], total[:, :], ALU.add))
            step(nc.vector.tensor_copy(pad_idx[:, :], pad_f[:, :]))
            assert n_r[0] == PAD_R
            step(nc.vector.tensor_scalar(ntile[:, :], total[:, :], 1.0 / P, (P - 1.0) / P - 0.5 + 0.5 / P, ALU.mult, ALU.add))
            step(nc.vector.tensor_scalar(ntile[:, :], ntile[:, :], ROUND, None, ALU.add))
            step(nc.vector.tensor_scalar(ntile[:, :], ntile[:, :], ROUND, None, ALU.subtract))
            end, k, n = ntile[:, :], 1, 0
            while k < E:
                dst = tend[:, n % 2, :]
                nc.vector.tensor_copy(dst[:, 0:k], end[:, 0:k])
                step(nc.vector.tensor_tensor(dst[:, k:], end[:, k:], end[:, 0:E - k], ALU.add))
                end, k, n = dst, 2 * k, n + 1
            step(nc.vector.tensor_scalar(skip[:, :], ntile[:, :], -float(P), float(PART), ALU.mult, ALU.add))
            wide = [P, T, E]
            step(nc.vector.tensor_tensor(ended[:, :, :], iota_f[:, :].unsqueeze(2).to_broadcast(wide),
                                         end.unsqueeze(1).to_broadcast(wide), ALU.is_ge))
            step(nc.vector.tensor_tensor(skipped[:, :, :], ended[:, :, :], skip[:, :].unsqueeze(1).to_broadcast(wide), ALU.mult))
            step(nc.vector.reduce_sum(texp[:, :], ended[:, :, :], AX))
            step(nc.vector.reduce_sum(trow[:, :], skipped[:, :, :], AX))
            step(nc.vector.tensor_scalar(texp_i[:, :], texp[:, :], float(E - 1), None, ALU.min))
            step(nc.vector.scalar_tensor_tensor(trow_i[:, :], iota_f[:, :], float(P), trow[:, :], ALU.mult, ALU.add))
            assert n_r[0] == TABLE_R
            dve.wait_ge(s["b_in"], 16 * 2 * E)

            def run(j, par, half, inside=False):
                if has(j + 1, inside):
                    e = dve.value_load(texp_i[0:1, bass.ds(j + 1, 1)], min_val=0, max_val=E - 1)
                    after(dve, "h_done", j - 1, inside)
                    after(dve, "relu_done", j - 1, inside)
                    nc.vector.tensor_copy(w1_now[:, 1 - par, :], flat(w1_all[:, bass.ds(e, 1), :])).then_inc(s["w1_set"], 1)
                if has(j + 2, inside):
                    after(dve, "rows_in", j + 2, inside)
                    after(dve, "T_done", j, inside)
                    row = rows[:, bass.ds(j + 2, 1), :]
                    nc.vector.tensor_scalar(t_now[:, par, :], flat(row[:, :, 0:D]), flat(row[:, :, D:D + 1]),
                                            flat(row[:, :, D + 1:D + 2]), ALU.subtract, ALU.mult).then_inc(s["t_set"], 1)
                if has(j - 1, inside):
                    if inside or j > 2:
                        dve.wait_ge(s[f"out_sent{1 - par}"], 16 * (half - 1 + par))
                    after(dve, "xb_set", j - 1, inside)
                    after(dve, "y_done", j - 1, inside)
                    nc.vector.tensor_copy(o_idx[:, 1 - par, :], flat(rows[:, bass.ds(j - 1, 1), D + 2:D + 3]))
                    nc.vector.tensor_tensor(o_now[:, 1 - par, :], ps_y[1 - par], xb2[:, 1 - par, :],
                                            ALU.add).then_inc(s["fin"], 1)
                if has(j + 1, inside):
                    after(dve, "y_done", j - 1, inside)
                    after(dve, "xb_set", j - 1, inside)
                    nc.vector.tensor_copy(w2_now[:, 1 - par, :], flat(w2_all[:, bass.ds(e, 1), :])).then_inc(s["w2_set"], 1)

            rounds(run, dve)

        @block.tensor
        def _(pe):
            def run(j, par, half, inside=False):
                if has(j + 1, inside):
                    after(pe, "t_set", j + 1, inside)
                    after(pe, "t_copied", j - 1, inside)
                    nc.tensor.transpose(ps_t[1 - par], t_now[:, 1 - par, :], ident[:, :]).then_inc(s["T_done"], 1)
                if has(j, inside):
                    after(pe, "t_copied", j, inside)
                    after(pe, "w1_set", j, inside)
                    after(pe, "relu_done", j - 2, inside)
                    for c in range(C):
                        last = nc.tensor.matmul(ps_h[par][:, c * P:(c + 1) * P], w1_now[:, par, c * P:(c + 1) * P],
                                                t_t[:, par, :], start=True, stop=True)
                    last.then_inc(s["h_done"], 1)
                if has(j - 1, inside):
                    after(pe, "relu_done", j - 1, inside)
                    after(pe, "w2_set", j - 1, inside)
                    after(pe, "fin", j - 3, inside)
                    for c in range(C):
                        last = nc.tensor.matmul(ps_y[1 - par], h_t[:, 1 - par, c, :],
                                                w2_now[:, 1 - par, c * P:(c + 1) * P], start=c == 0, stop=c == C - 1)
                    last.then_inc(s["y_done"], 1)

            rounds(run, pe)


def layers(nc, x, ctx, mask, ln_x_w, ln_x_b, ln_l_w, ln_l_b, Wq, Wkv, q_scale, k_scale, Wo, ln_o_w, ln_o_b,
           weight_q, weight_scale, bias, We, W2, Wr, br, F1, b1, F2, b2, out):
    B, S, D = x.shape
    M = ctx.shape[1]
    E = Wr.shape[0]
    mask = mask.bitcast(U8).rearrange("(b m) -> b m", m=M)
    weight_q = weight_q.bitcast(I8).rearrange("(o i) -> o i", i=D)
    tiles = -(-(B * S // P + E - 1) // DEEP) * DEEP
    sorted_rows = nc.dram_tensor("sorted_rows", (E * part_rows(B) + E * P, D + 3), F32, kind="Internal").ap()
    F = F1.shape[1]
    with ExitStack() as stack:
        def sb(name, shape):
            return stack.enter_context(nc.sbuf_tensor(name, shape, F32))

        x_res = sb("x_res", [P, B, D + 3])
        ctx_res = sb("ctx_res", [P, B, D])
        ident = sb("ident", [P, P])
        latent_attention(nc, x_res, ctx_res, ident, sorted_rows, x, ctx, mask, ln_x_w, ln_x_b, ln_l_w, ln_l_b,
                         Wq, Wkv, q_scale, k_scale, Wo, ln_o_w, ln_o_b, E)
        w1_all = sb("w1_all", [P, E, F + F // P])
        w2_all = sb("w2_all", [P, E, F + D])
        total = sb("total", [P, E])
        ffn_xattn_route(nc, x_res, ctx_res, ident, w1_all, w2_all, total, sorted_rows, weight_q, weight_scale, bias,
                        We, W2, Wr, br, F1, F2)
        experts_program(nc, B, tiles, ident, w1_all, w2_all, total, sorted_rows, F1, b1, b2, out)


INPUTS = ['x', 'ctx_1024', 'mask_BxS2_bk0', 'L0_xattn_ln_x_w', 'L0_xattn_ln_x_b', 'L0_xattn_ln_l_w', 'L0_xattn_ln_l_b',
          'L0_xattn_Wq', 'L0_xattn_Wkv', 'L0_xattn_q_scale', 'L0_xattn_k_scale', 'L0_xattn_Wo', 'L0_xattn_ln_o_w',
          'L0_xattn_ln_o_b', 'L0_ffn_weight_q', 'L0_ffn_weight_scale', 'L0_ffn_bias', 'L1_xattn_We', 'L1_xattn_W2',
          'L1_ffn_Wr', 'L1_ffn_br', 'L1_ffn_W1', 'L1_ffn_b1', 'L1_ffn_W2', 'L1_ffn_b2']


def kernel(**inputs):
    import numpy as np
    import concourse.bacc as bacc
    from concourse.bass_utils import run_bass_kernel_spmd

    nc = bacc.Bacc("TRN2", target_bir_lowering=False, num_devices=1)
    arrays, args = {}, []
    for name in INPUTS:
        a = np.ascontiguousarray(inputs[name])
        if a.dtype.itemsize == 1:
            a = a.reshape(-1).view(np.int32)
        arrays[f"in_{name}_dram"] = a
        args.append(nc.dram_tensor(f"in_{name}_dram", a.shape, mybir.dt.from_np(a.dtype), kind="ExternalInput").ap())
    out = nc.dram_tensor("out_dram", arrays["in_x_dram"].shape, F32, kind="ExternalOutput").ap()
    layers(nc, *args, out)
    r = run_bass_kernel_spmd(nc, [arrays], core_ids=[0])
    return r.results[0]["out_dram"]
```

```python
import math
from contextlib import ExitStack

import concourse.bass as bass
from concourse import mybir

F32 = mybir.dt.float32
F32R = mybir.dt.float32r
BF16 = mybir.dt.bfloat16
I32 = mybir.dt.int32
U32 = mybir.dt.uint32
I8 = mybir.dt.int8
U8 = mybir.dt.uint8
ALU = mybir.AluOpType
ACT = mybir.ActivationFunctionType
AX = mybir.AxisListType.X

P = 128
LN_EPS = 1e-5
L2_EPS = 1e-12
SIM_SCALE = 8.0
EXP_ROOM = 80.0
MASKED = -1e30
LN_LIFT = 20
LN2 = math.log(2.0)
VW = 96
Q_EPS = 1e-6
Q_MAX = 127.0
ROUND = 1.5 * 2.0 ** 23
G = 4
FILL = 20000.0
DEEP = 3
PAD_R = 3
TABLE_R = PAD_R + 3 + 3 + 1 + 6


def latent_attention(nc, x_res, ctx_res, ident, sorted_rows, x, ctx, mask, ln_x_w, ln_x_b, ln_l_w, ln_l_b, Wq, Wkv,
                     q_scale, k_scale, Wo, ln_o_w, ln_o_b, E, second):
    B, S, D = x.shape
    M = ctx.shape[1]
    DH = q_scale.shape[0]
    INNER = Wq.shape[1]
    H = INNER // DH
    PAIRS = H // 2
    assert S == P and D == P and INNER == PAIRS * P and 2 * DH == P

    with ExitStack() as stack:
        def sb(name, shape, dt=F32):
            return stack.enter_context(nc.sbuf_tensor(name, shape, dt))

        def sem(name):
            return stack.enter_context(nc.semaphore(name))

        fill = sb("fill", [P, 1, D + 3])
        ids = sb("ids", [P, B], I32)
        zero_col = sb("zero_col", [P, 1])
        mask_raw = sb("mask_raw", [P, P], U8)
        mask_f = sb("mask_f", [P, P])
        mask_bias = sb("mask_bias", [P, P])
        neg_shift = sb("neg_shift", [P, 1])
        qs_b = sb("qs_b", [P, DH])
        ks_b = sb("ks_b", [P, DH])
        qk_prod = sb("qk_prod", [P, DH])
        qk_max = sb("qk_max", [P, 1])
        scale_col = sb("scale_col", [P, 4])
        ln_cols = sb("ln_cols", [P, 4])
        lno_w = sb("lno_w", [P, D])
        lno_b = sb("lno_b", [P, D])
        w_raw = sb("w_raw", [P, 3 * INNER])
        w_hi = sb("w_hi", [P, 3 * INNER], F32R)
        w_lo = sb("w_lo", [P, 3 * INNER], F32R)
        wo_sb = sb("wo_sb", [P, PAIRS, D])

        bn6 = sb("bn6", [P, 2, 6])
        xc_stat = sb("xc_stat", [P, 2, 2, 2])
        lift_bias = sb("lift_bias", [P, 1])
        var_in = sb("var_in", [P, 32])
        rs_ln = sb("rs_ln", [P, 32])
        rs_y0 = sb("rs_y0", [P, 32])
        rs_t1 = sb("rs_t1", [P, 32])
        rs_t2 = sb("rs_t2", [P, 32])
        rs_t3 = sb("rs_t3", [P, 32])
        rs_t4 = sb("rs_t4", [P, 32])
        rstd = sb("rstd", [P, 2, 32])
        xc_hat = sb("xc_hat", [P, 2, 2, D])
        xc_t = sb("xc_t", [P, 2, 2, P])
        xc_hi = sb("xc_hi", [P, 2, 2, P], F32R)
        xc_lo = sb("xc_lo", [P, 2, 2, P], F32R)
        mask_now = sb("mask_now", [P, 2])
        sq = sb("sq", [P, 3 * INNER])
        sumsq = sb("sumsq", [P, 3 * H])
        three = sb("three", [P, 32])
        var_mul = sb("var_mul", [P, 2])
        var_add = sb("var_add", [P, 3])
        var_tmp = sb("var_tmp", [P, 2])
        qk_hat = sb("qk_hat", [P, 3 * INNER])
        q_hi = sb("q_hi", [P, PAIRS, 2, P], F32R)
        q_lo = sb("q_lo", [P, PAIRS, 2, P], F32R)
        k_hi = sb("k_hi", [P, 2, INNER], F32R)
        k_lo = sb("k_lo", [P, 2, INNER], F32R)
        prob = sb("prob", [P, 2, H * P])
        v_sb = sb("v_sb", [P, 2, 2, H, VW])
        rden = sb("rden", [P, H])
        o_n = sb("o_n", [P, INNER])
        o_t = sb("o_t", [P, INNER])
        o6 = sb("o6", [P, 6])
        o_stat = sb("o_stat", [P, 2, 2])
        o_c = sb("o_c", [P, 2, D])
        x_b = sb("x_b", [P, 2, D])

        ps = stack.enter_context(nc.psum_tensor("ps", [P, 8, 512], F32))
        ps_qk = ps[:, 0:3, :]
        ps_v, ps_ot = (ps[:, 4, :], ps[:, 5, :]), ps[:, 3, :]
        ps_s = (ps[:, 4, :], ps[:, 5, :], ps[:, 3, :], ps[:, 4, :])
        ps_pv = ps[:, 6, 0:(H - 1) * (DH + 1)].rearrange("p (h e) -> p h e", e=DH + 1)
        ps_xc = ps[:, 7, 0:2 * P]
        ps_o = ps[:, 7, 2 * P:3 * P]
        ps_pv7 = ps[:, 3, 0:DH + 1]

        lots = [slice(0, 4)] + [slice(n, min(n + 12, B)) for n in range(4, B, 12)]
        ld_lot = [sem(f"ld_lot{n}") for n in range(len(lots))]
        tokens_in = sem("tokens_in")
        ld_qkv = sem("ld_qkv")
        ld_w = sem("ld_w")
        ctx_zeroed = sem("ctx_zeroed")
        const_ready = sem("const_ready")
        setup_v = sem("setup_v")
        setup_p = sem("setup_p")
        setup_g = sem("setup_g")
        s_maskT = sem("s_maskT")
        xc_bn = sem("xc_bn")
        xc_mv = sem("xc_mv")
        var_t = sem("var_t")
        ss_raw = sem("ss_raw")
        ss_done = sem("ss_done")
        var_ready = sem("var_ready")
        ln_done = sem("ln_done")
        y0_done = sem("y0_done")
        nwt = sem("nwt")
        rs_ready = sem("rs_ready")
        hat_ready = sem("hat_ready")
        xct_sb = sem("xct_sb")
        hi_done = sem("hi_done")
        lo_done = sem("lo_done")
        qk_done = sem("qk_done")
        sq_done = sem("sq_done")
        scaled = sem("scaled")
        qkT_done = sem("qkT_done")
        qhi_done = sem("qhi_done")
        khi_done = sem("khi_done")
        klo_done = sem("klo_done")
        qlo_done = sem("qlo_done")
        sim_done = sem("sim_done")
        exp_done = sem("exp_done")
        v_done = sem("v_done")
        v_copied = sem("v_copied")
        pv_done = sem("pv_done")
        rl_done = sem("rl_done")
        on_done = sem("on_done")
        onT_done = sem("onT_done")
        ot_done = sem("ot_done")
        wo_done = sem("wo_done")
        xcT_done = sem("xcT_done")
        o_bn = sem("o_bn")
        o_mv = sem("o_mv")
        o_cent = sem("o_cent")
        xb_done = sem("xb_done")
        mask_set = sem("mask_set")
        x1_done = sem("x1_done")
        fill_out = sem("fill_out")
        second_in = sem("second_in")

        N_W = 14 * 16

        SETUP_V, SETUP_G, FIRST_G = 14, 9, 7

        def rounds(run, eng):
            for j in range(-1, 5):
                run(j, j % 2)
            with eng.Fori(0, (B - 8) // 2) as turn:
                run(5 + 2 * turn, 1, True)
                run(6 + 2 * turn, 0, True)
            for j in range(B - 3, B + 2):
                run(j, j % 2)

        def has(b, inside):
            return inside or 0 <= b < B

        block = stack.enter_context(nc.Block())

        @block.sync
        def _(sp):
            for n, lot in enumerate(lots):
                sp.dma_start(x_res[:, lot, 0:D], x[lot].rearrange("b s d -> s b d")).then_inc(ld_lot[n], 16)
                sp.wait_ge(ctx_zeroed, n + 1)
                sp.dma_start(ctx_res[0:M, lot, :], ctx[lot].rearrange("b m d -> m b d")).then_inc(ld_lot[n], 16)
                if n == 0:
                    sp.dma_start(mask_raw[0:B, 0:M], mask).then_inc(ld_w, 16)
                    for col, v in enumerate((ln_l_w, ln_l_b, ln_x_w, ln_x_b)):
                        sp.dma_start(ln_cols[:, col:col + 1], v.rearrange("(p a) -> p a", a=1)).then_inc(ld_w, 16)
                sp.wait_ge(ld_lot[n], 32)
                sp.sem_inc(tokens_in, lot.stop - lot.start)
                if n == 0:
                    sp.dma_start(qs_b[:, :], q_scale.partition_broadcast(P)).then_inc(ld_w, 16)
                    sp.dma_start(ks_b[:, :], k_scale.partition_broadcast(P)).then_inc(ld_w, 16)
                    sp.dma_start(lno_w[:, :], ln_o_w.partition_broadcast(P)).then_inc(ld_w, 16)
                    sp.dma_start(lno_b[:, :], ln_o_b.partition_broadcast(P)).then_inc(ld_w, 16)
            for dst, src in second:
                sp.dma_start(dst, src, allow_slow_non_contiguous=True).then_inc(second_in, 16)
            sp.wait_ge(setup_v, SETUP_V)
            sp.dma_start(sorted_rows[sorted_rows.shape[0] - E * P:, :].rearrange("(t p) w -> p t w", p=P),
                         fill[:, :, :].to_broadcast([P, E, D + 3])).then_inc(fill_out, 16)
            sp.wait_ge(fill_out, 16)
            sp.wait_ge(second_in, 16 * len(second))

        @block.scalar
        def _(act):
            act.dma_start(w_raw[:, 0:INNER], Wq).then_inc(ld_qkv, 16)
            act.dma_start(w_raw[:, INNER:3 * INNER], Wkv).then_inc(ld_qkv, 16)
            act.dma_start(wo_sb[:, :, :], Wo.rearrange("(t p) d -> p t d", p=P)).then_inc(ld_w, 16)
            nc.scalar.preload_act_table_set("natural_log_exp_and_others")
            for col, v in enumerate((q_scale, k_scale)):
                for half in (0, 1):
                    act.dma_start(scale_col[half * DH:(half + 1) * DH, col:col + 1],
                                  v.rearrange("(p a) -> p a", a=1)).then_inc(ld_w, 16)

            def run(j, par, inside=False):
                if has(j, inside):
                    act.wait_ge(qkT_done, 3 * j + 1)
                    for half in (0, 1):
                        rows = slice(half * DH, (half + 1) * DH)
                        last = nc.scalar.activation(q_hi[rows, :, half, :],
                                                    ps_qk[rows, 0, :].rearrange("p (t q) -> p t q", q=P),
                                                    ACT.Copy, scale=scale_col[rows, 2:3])
                    last.then_inc(qhi_done, 1)
                    for kt in (0, 1):
                        act.wait_ge(qkT_done, 3 * j + 2 + kt)
                        nc.scalar.activation(k_hi[:, kt, :], ps_qk[:, 1 + kt, :], ACT.Copy).then_inc(khi_done, 1)
                if has(j + 1, inside):
                    act.wait_ge(xct_sb, j + 2)
                    nc.scalar.activation(xc_hi[:, 1 - par, :, :], xc_t[:, 1 - par, :, :], ACT.Copy).then_inc(hi_done, 1)
                if has(j, inside):
                    for kt in (0, 1):
                        act.wait_ge(v_done, 2 * j + kt + 1)
                        nc.scalar.activation(v_sb[:, par, kt, :, 0:DH], ps_v[kt].rearrange("p (h d) -> p h d", d=DH),
                                             ACT.Copy).then_inc(v_copied, 1)
                if has(j + 1, inside):
                    for n in range(3):
                        act.wait_ge(qk_done, 3 * j + 4 + n)
                        nc.scalar.activation(sq[:, n * INNER:(n + 1) * INNER], ps_qk[:, n, :],
                                             ACT.Square).then_inc(sq_done, 1)
                def exps(before, units):
                    for done, n in enumerate(units, before):
                        act.wait_ge(sim_done, 4 * j + done + 1)
                        nc.scalar.activation(prob[:, n // 2, n % 2 * INNER:(n % 2 + 1) * INNER], ps_s[n], ACT.Exp,
                                             bias=(mask_now[:, par:par + 1] if n > 1 else
                                                   neg_shift[:, 0:1])).then_inc(exp_done, 1)

                act.wait_ge(var_ready, j + 4)
                if has(j + 1, inside):
                    act.wait_ge(ss_done, j + 2)
                nc.scalar.activation(rs_ln[:, :], var_in[:, :], ACT.Ln, scale=float(2 ** LN_LIFT)).then_inc(ln_done, 1)
                act.wait_ge(ln_done, j + 4)
                nc.scalar.activation(rs_y0[:, :], rs_ln[:, :], ACT.Exp, scale=-0.5,
                                     bias=lift_bias[:, 0:1]).then_inc(y0_done, 1)
                if has(j, inside):
                    exps(0, (0,))
                if has(j - 1, inside):
                    act.wait_ge(onT_done, j)
                    nc.scalar.activation(o_t[:, :], ps_ot, ACT.Copy).then_inc(ot_done, 1)
                if has(j, inside):
                    exps(1, (1, 3, 2))

            act.wait_ge(setup_g, FIRST_G)
            run(-3, 1)
            run(-2, 0)
            act.wait_ge(setup_v, SETUP_V)
            rounds(run, act)

        @block.gpsimd
        def _(pool):
            nc.gpsimd.memset(ctx_res[:, lots[0], :], 0.0).then_inc(ctx_zeroed, 1)
            nc.gpsimd.memset(mask_f[:, :], 0.0).then_inc(setup_p, 1)
            nc.gpsimd.memset(ident[:, :], 0.0).then_inc(setup_p, 1)
            nc.gpsimd.memset(var_in[:, :], 1.0).then_inc(setup_p, 1)
            nc.gpsimd.memset(fill[:, :, :], FILL).then_inc(setup_p, 1)
            nc.gpsimd.iota(ids[:, :], pattern=[[P, B]], base=0, channel_multiplier=1).then_inc(setup_p, 1)
            nc.gpsimd.memset(zero_col[:, :], 0.0).then_inc(setup_p, 1)
            pool.wait_ge(setup_p, 6)
            nc.gpsimd.affine_select(out=ident[:, :], in_=ident[:, :], compare_op=ALU.not_equal, fill=1.0,
                                    base=0, pattern=[[-1, P]], channel_multiplier=1).then_inc(setup_g, 1)
            nc.gpsimd.memset(three[:, :], 3.0).then_inc(setup_g, 1)
            nc.gpsimd.memset(var_mul[:, 0:1], 1.0 + LN_EPS).then_inc(setup_g, 1)
            nc.gpsimd.memset(var_mul[:, 1:2], 1.0).then_inc(setup_g, 1)
            nc.gpsimd.memset(var_add[:, 0:1], LN_EPS * LN_EPS).then_inc(setup_g, 1)
            nc.gpsimd.memset(var_add[:, 1:3], LN_EPS).then_inc(setup_g, 1)
            nc.gpsimd.memset(lift_bias[:, :], 0.5 * LN_LIFT * LN2).then_inc(setup_g, 1)
            pool.wait_ge(setup_g, FIRST_G)

            def run(j, par, inside=False):
                if has(j + 1, inside):
                    pool.wait_ge(hi_done, j + 2)
                    nc.gpsimd.tensor_tensor(xc_lo[:, 1 - par, :, :], xc_t[:, 1 - par, :, :],
                                            xc_hi[:, 1 - par, :, :].bitcast(F32), ALU.subtract).then_inc(lo_done, 1)
                if has(j + 3, inside):
                    pool.wait_ge(xc_mv, j + 4)
                    nc.gpsimd.tensor_tensor(var_tmp[:, :], xc_stat[:, 1 - par, :, 1], var_mul[:, :],
                                            ALU.mult).then_inc(var_t, 1)
                    pool.wait_ge(var_t, j + 4)
                    last = nc.gpsimd.tensor_tensor(var_in[:, 24:26], var_tmp[:, :], var_add[:, 0:2], ALU.add)
                if has(j - 2, inside):
                    pool.wait_ge(o_mv, j - 1)
                    last = nc.gpsimd.tensor_tensor(var_in[:, 26:27], o_stat[:, par, 1:2], var_add[:, 2:3], ALU.add)
                last.then_inc(var_ready, 1)
                pool.wait_ge(y0_done, j + 4)
                nc.gpsimd.tensor_tensor(rs_t1[:, :], rs_y0[:, :], rs_y0[:, :], ALU.mult).then_inc(nwt, 1)
                nc.gpsimd.tensor_scalar(rs_t3[:, :], rs_y0[:, :], -0.5, None, ALU.mult).then_inc(nwt, 1)
                pool.wait_ge(nwt, 4 * (j + 3) + 1)
                nc.gpsimd.tensor_tensor(rs_t2[:, :], rs_t1[:, :], var_in[:, :], ALU.mult).then_inc(nwt, 1)
                pool.wait_ge(nwt, 4 * (j + 3) + 3)
                nc.gpsimd.tensor_tensor(rs_t4[:, :], rs_t2[:, :], three[:, :], ALU.subtract).then_inc(nwt, 1)
                pool.wait_ge(nwt, 4 * (j + 3) + 4)
                nc.gpsimd.tensor_tensor(rstd[:, par, :], rs_t4[:, :], rs_t3[:, :], ALU.mult).then_inc(rs_ready, 1)
                if has(j, inside):
                    if inside or j > 1:
                        pool.wait_ge(x1_done, j - 1)
                    nc.gpsimd.tensor_tensor(x_b[:, par, :], x_res[:, bass.ds(j, 1), 0:D].rearrange("p a d -> p (a d)"),
                                            lno_b[:, :], ALU.add).then_inc(xb_done, 1)
                if has(j + 1, inside):
                    nc.gpsimd.tensor_copy(mask_now[:, 1 - par:2 - par], mask_bias[:, bass.ds(j + 1, 1)]).then_inc(mask_set, 1)
                if not inside and 0 <= j < len(lots) - 2:
                    nc.gpsimd.memset(ctx_res[:, lots[j + 2], :], 0.0).then_inc(ctx_zeroed, 1)

            run(-3, 1)
            nc.gpsimd.memset(v_sb[:, :, :, :, DH + 1:VW], 0.0).then_inc(setup_g, 1)
            nc.gpsimd.memset(v_sb[:, :, :, :, DH:DH + 1], 1.0).then_inc(setup_g, 1)
            nc.gpsimd.memset(ctx_res[:, lots[1], :], 0.0).then_inc(ctx_zeroed, 1)
            run(-2, 0)
            pool.wait_ge(setup_v, SETUP_V)
            rounds(run, pool)

        @block.vector
        def _(dve):
            def run(j, par, inside=False):
                if has(j + 1, inside):
                    dve.wait_ge(xcT_done, j + 2)
                    if has(j - 2, inside):
                        dve.wait_ge(wo_done, j - 1)
                    for n in (0, 1):
                        last = nc.vector.tensor_scalar(xc_t[:, 1 - par, n, :], ps_xc[:, n * P:(n + 1) * P],
                                                       ln_cols[:, 2 * n:2 * n + 1], ln_cols[:, 2 * n + 1:2 * n + 2],
                                                       ALU.mult, ALU.add)
                    last.then_inc(xct_sb, 1)
                if has(j, inside):
                    dve.wait_ge(qhi_done, j + 1)
                    for half in (0, 1):
                        rows = slice(half * DH, (half + 1) * DH)
                        last = nc.vector.scalar_tensor_tensor(q_lo[rows, :, half, :],
                                                              ps_qk[rows, 0, :].rearrange("p (t q) -> p t q", q=P),
                                                              scale_col[rows, 2:3], q_hi[rows, :, half, :].bitcast(F32),
                                                              ALU.mult, ALU.subtract)
                    last.then_inc(qlo_done, 1)
                    for kt in (0, 1):
                        dve.wait_ge(khi_done, 2 * j + 1 + kt)
                        nc.vector.tensor_tensor(k_lo[:, kt, :], ps_qk[:, 1 + kt, :], k_hi[:, kt, :].bitcast(F32),
                                                ALU.subtract).then_inc(klo_done, 1)
                if has(j - 2, inside):
                    dve.wait_ge(wo_done, j - 1)
                    nc.vector.bn_stats(o6[:, :], ps_o).then_inc(o_bn, 1)
                    dve.wait_ge(o_bn, j - 1)
                if has(j + 3, inside):
                    dve.wait_ge(tokens_in, j + 4)
                    for n, res in enumerate((x_res, ctx_res)):
                        last = nc.vector.bn_stats(bn6[:, n, :], res[:, bass.ds(j + 3, 1), 0:D].rearrange("p a d -> p (a d)"))
                    last.then_inc(xc_bn, 1)
                if has(j - 2, inside):
                    nc.vector.bn_aggr(o_stat[:, par, :], o6[:, :]).then_inc(o_mv, 1)
                    dve.wait_ge(o_mv, j - 1)
                    nc.vector.scalar_tensor_tensor(o_c[:, par, :], ps_o, o_stat[:, par, 0:1],
                                                   lno_w[:, :], ALU.subtract, ALU.mult).then_inc(o_cent, 1)
                elif has(j + 3, inside):
                    dve.wait_ge(xc_bn, j + 4)
                if has(j + 3, inside):
                    for n in (0, 1):
                        last = nc.vector.bn_aggr(xc_stat[:, 1 - par, n, :], bn6[:, n, :])
                    last.then_inc(xc_mv, 1)
                if has(j + 1, inside):
                    for n in range(3):
                        dve.wait_ge(sq_done, 3 * j + 4 + n)
                        nc.vector.reduce_sum(sumsq[:, n * H:(n + 1) * H],
                                             sq[:, n * INNER:(n + 1) * INNER].rearrange("p (h d) -> p h d", d=DH),
                                             AX).then_inc(ss_raw, 1)
                    dve.wait_ge(ss_raw, 3 * j + 6)
                    nc.vector.tensor_scalar(var_in[:, 0:3 * H], sumsq[:, :], L2_EPS * L2_EPS, None,
                                            ALU.max).then_inc(ss_done, 1)
                if has(j - 1, inside):
                    dve.wait_ge(pv_done, j)
                    nc.vector.reciprocal(rden[:, 0:H - 1], ps_pv[:, :, DH])
                    nc.vector.reciprocal(rden[:, H - 1:H], ps_pv7[:, DH:DH + 1]).then_inc(rl_done, 1)
                    dve.wait_ge(rl_done, j)
                    nc.vector.tensor_tensor(o_n[:, 0:(H - 1) * DH].rearrange("p (h d) -> p h d", d=DH),
                                            ps_pv[:, :, 0:DH],
                                            rden[:, 0:H - 1].unsqueeze(2).to_broadcast([P, H - 1, DH]), ALU.mult)
                    nc.vector.tensor_scalar(o_n[:, (H - 1) * DH:INNER], ps_pv7[:, 0:DH], rden[:, H - 1:H], None,
                                            ALU.mult).then_inc(on_done, 1)
                dve.wait_ge(rs_ready, j + 4)
                if has(j + 1, inside):
                    for n in range(3):
                        nc.vector.tensor_tensor(qk_hat[:, n * INNER:(n + 1) * INNER].rearrange("p (h d) -> p h d", d=DH),
                                                ps_qk[:, n, :].rearrange("p (h d) -> p h d", d=DH),
                                                rstd[:, par, n * H:(n + 1) * H].unsqueeze(2).to_broadcast([P, H, DH]),
                                                ALU.mult).then_inc(scaled, 1)
                if has(j + 3, inside):
                    for n, res in enumerate((x_res, ctx_res)):
                        last = nc.vector.tensor_scalar(xc_hat[:, 1 - par, n, :],
                                                       res[:, bass.ds(j + 3, 1), 0:D].rearrange("p a d -> p (a d)"),
                                                       xc_stat[:, 1 - par, n, 0:1], rstd[:, par, 24 + n:25 + n],
                                                       ALU.subtract, ALU.mult)
                    last.then_inc(hat_ready, 1)
                if has(j - 2, inside):
                    dve.wait_ge(o_cent, j - 1)
                    nc.vector.scalar_tensor_tensor(x_res[:, bass.ds(j - 2, 1), 0:D].rearrange("p a d -> p (a d)"),
                                                   o_c[:, par, :], rstd[:, par, 26:27], x_b[:, par, :],
                                                   ALU.mult, ALU.add).then_inc(x1_done, 1)

            dve.wait_ge(setup_p, 6)
            for part in (q_hi, q_lo):
                nc.vector.tensor_copy(part[:, :, :, :].rearrange("p t a q -> p (t a q)"),
                                      zero_col[:, :].to_broadcast([P, 2 * INNER])).then_inc(setup_v, 1)
            nc.vector.tensor_copy(x_res[:, :, D + 2:D + 3], ids[:, :].unsqueeze(2)).then_inc(setup_v, 1)
            run(-3, 1)
            dve.wait_ge(ld_qkv, 32)
            nc.vector.tensor_copy(w_hi[:, :], w_raw[:, :]).then_inc(setup_v, 1)
            dve.wait_ge(setup_v, 4)
            nc.vector.tensor_tensor(w_lo[:, :], w_raw[:, :], w_hi[:, :].bitcast(F32), ALU.subtract).then_inc(setup_v, 1)
            run(-2, 0)
            dve.wait_ge(ld_w, N_W)
            nc.vector.tensor_copy(mask_f[0:B, 0:M], mask_raw[0:B, 0:M]).then_inc(setup_v, 1)
            nc.vector.tensor_tensor(qk_prod[:, :], qs_b[:, :], ks_b[:, :], ALU.mult).then_inc(setup_v, 1)
            nc.vector.tensor_tensor(scale_col[:, 3:4], scale_col[:, 0:1], scale_col[:, 1:2],
                                    ALU.mult).then_inc(setup_v, 1)
            dve.wait_ge(setup_v, 7)
            nc.vector.tensor_reduce(qk_max[:, :], qk_prod[:, :], AX, ALU.max,
                                    apply_absolute_value=True).then_inc(setup_v, 1)
            dve.wait_ge(setup_v, 9)
            nc.vector.tensor_scalar(scale_col[:, 2:3], scale_col[:, 3:4], SIM_SCALE, None, ALU.mult).then_inc(setup_v, 1)
            nc.vector.tensor_scalar(neg_shift[:, :], qk_max[:, :], -SIM_SCALE, EXP_ROOM, ALU.mult,
                                    ALU.add).then_inc(setup_v, 1)
            dve.wait_ge(setup_v, 11)
            nc.vector.tensor_scalar(neg_shift[:, :], neg_shift[:, :], 0.0, None, ALU.min).then_inc(setup_v, 1)
            dve.wait_ge(s_maskT, 1)
            nc.vector.tensor_scalar(mask_bias[:, :], ps[:, 6, 0:P], 1.0, -MASKED, ALU.subtract,
                                    ALU.mult).then_inc(setup_v, 1)
            dve.wait_ge(setup_v, 13)
            nc.vector.tensor_scalar(mask_bias[:, :], mask_bias[:, :], neg_shift[:, 0:1], None,
                                    ALU.add).then_inc(setup_v, 1)
            rounds(run, dve)

        @block.tensor
        def _(pe):
            def product(dst, tok_hi, tok_lo, w):
                nc.tensor.matmul(dst, tok_hi, w_hi[:, w:w + INNER], start=True, stop=False)
                nc.tensor.matmul(dst, tok_hi, w_lo[:, w:w + INNER], start=False, stop=False)
                return nc.tensor.matmul(dst, tok_lo, w_hi[:, w:w + INNER], start=False, stop=True)

            def run(j, par, inside=False):
                if has(j, inside):
                    for n in range(3):
                        pe.wait_ge(scaled, 3 * j + 1 + n)
                        for t in range(PAIRS):
                            last = nc.tensor.transpose(ps_qk[:, n, t * P:(t + 1) * P],
                                                       qk_hat[:, n * INNER + t * P:n * INNER + (t + 1) * P], ident[:, :])
                        last.then_inc(qkT_done, 1)
                if has(j, inside):
                    if inside or j > 0:
                        pe.wait_ge(exp_done, 4 * j)
                    for kt in (0, 1):
                        last = product(ps_v[kt], xc_hi[:, par, kt, :], xc_lo[:, par, kt, :], 2 * INNER)
                        last.then_inc(v_done, 1)
                def weighted(heads):
                    for h in heads:
                        dst = ps[:, 6, h * (DH + 1):h * (DH + 1) + VW] if h < H - 1 else ps[:, 3, 0:VW]
                        for kt in (0, 1):
                            last = nc.tensor.matmul(dst, prob[:, kt, h * P:(h + 1) * P], v_sb[:, 1 - par, kt, h, :],
                                                    start=kt == 0, stop=kt == 1)
                    return last

                if has(j - 1, inside):
                    pe.wait_ge(exp_done, 4 * j)
                    weighted(range(H // 2))
                if has(j + 1, inside):
                    pe.wait_ge(lo_done, j + 2)
                    for n, (src, w) in enumerate(((0, 0), (0, INNER), (1, INNER))):
                        if has(j, inside):
                            if n == 0:
                                pe.wait_ge(qlo_done, j + 1)
                            else:
                                pe.wait_ge(klo_done, 2 * j + n)
                        last = product(ps_qk[:, n, :], xc_hi[:, 1 - par, src, :], xc_lo[:, 1 - par, src, :], w)
                        last.then_inc(qk_done, 1)
                if has(j - 1, inside):
                    weighted(range(H // 2, H)).then_inc(pv_done, 1)
                if has(j + 2, inside):
                    pe.wait_ge(hat_ready, j + 3)
                    if has(j - 2, inside):
                        pe.wait_ge(o_cent, j - 1)
                    for n in (0, 1):
                        last = nc.tensor.transpose(ps_xc[:, n * P:(n + 1) * P], xc_hat[:, par, n, :], ident[:, :])
                    last.then_inc(xcT_done, 1)
                def scores(units):
                    for n in units:
                        if n < 2:
                            pe.wait_ge(v_copied, 2 * j + n + 1)
                        elif n == 2:
                            if inside or j > 0:
                                pe.wait_ge(ot_done, j)
                        else:
                            pe.wait_ge(exp_done, 4 * j + 1)
                        for t in (0, 1):
                            pair = n % 2 * 2 + t
                            keys = slice(pair * P, (pair + 1) * P)
                            for m, (k, q) in enumerate(((k_hi, q_hi), (k_hi, q_lo), (k_lo, q_hi))):
                                last = nc.tensor.matmul(ps_s[n][:, t * 2 * P:(t + 1) * 2 * P], k[:, n // 2, keys],
                                                        q[:, pair, :, :].rearrange("p a q -> p (a q)"),
                                                        start=m == 0, stop=m == 2)
                        last.then_inc(sim_done, 1)

                if has(j, inside):
                    pe.wait_ge(klo_done, 2 * j + 2)
                    scores((0, 1))
                if has(j - 1, inside):
                    pe.wait_ge(on_done, j)
                    for t in range(PAIRS):
                        last = nc.tensor.transpose(ps_ot[:, t * P:(t + 1) * P], o_n[:, t * P:(t + 1) * P], ident[:, :])
                    last.then_inc(onT_done, 1)
                if has(j, inside):
                    scores((3,))
                if has(j - 1, inside):
                    pe.wait_ge(ot_done, j)
                    if not has(j + 2, inside) and has(j - 2, inside):
                        pe.wait_ge(o_cent, j - 1)
                    if not has(j + 2, inside) and has(j + 1, inside):
                        pe.wait_ge(xct_sb, j + 2)
                    for t in range(PAIRS):
                        last = nc.tensor.matmul(ps_o, o_t[:, t * P:(t + 1) * P], wo_sb[:, t, :],
                                                start=t == 0, stop=t == PAIRS - 1)
                    last.then_inc(wo_done, 1)
                if has(j, inside):
                    scores((2,))

            pe.wait_ge(setup_g, FIRST_G)
            run(-3, 1)
            run(-2, 0)
            pe.wait_ge(setup_g, SETUP_G)
            pe.wait_ge(setup_v, 6)
            nc.tensor.transpose(ps[:, 6, 0:P], mask_f[:, :], ident[:, :]).then_inc(s_maskT, 1)
            pe.wait_ge(setup_v, SETUP_V)
            rounds(run, pe)


def tile_table(nc, dve, table, routed, E, T, PART):
    n_r = [0]

    def step(ins):
        ins.then_inc(routed, 1)
        n_r[0] += 1
        dve.wait_ge(routed, n_r[0])

    nc.vector.tensor_copy(table["iota_f"][:, :], table["iota_i"][:, :])
    step(nc.vector.tensor_copy(table["base_f"][:, :], table["base_i"][:, :]))
    step(nc.vector.tensor_tensor(table["pad_f"][:, :], table["base_f"][:, :], table["total"][:, :], ALU.add))
    step(nc.vector.tensor_copy(table["pad_i"][:, :], table["pad_f"][:, :]))
    assert n_r[0] == PAD_R
    step(nc.vector.tensor_scalar(table["ntile"][:, :], table["total"][:, :], 1.0 / P, (P - 1.0) / P - 0.5 + 0.5 / P, ALU.mult, ALU.add))
    step(nc.vector.tensor_scalar(table["ntile"][:, :], table["ntile"][:, :], ROUND, None, ALU.add))
    step(nc.vector.tensor_scalar(table["ntile"][:, :], table["ntile"][:, :], ROUND, None, ALU.subtract))
    end, k, n = table["ntile"][:, :], 1, 0
    while k < E:
        dst = table["tend"][:, n % 2, :]
        nc.vector.tensor_copy(dst[:, 0:k], end[:, 0:k])
        step(nc.vector.tensor_tensor(dst[:, k:], end[:, k:], end[:, 0:E - k], ALU.add))
        end, k, n = dst, 2 * k, n + 1
    step(nc.vector.tensor_scalar(table["skip"][:, :], table["ntile"][:, :], -float(P), float(PART), ALU.mult, ALU.add))
    wide = [P, T, E]
    step(nc.vector.tensor_tensor(table["ended"][:, :, :], table["iota_f"][:, :].unsqueeze(2).to_broadcast(wide),
                                 end.unsqueeze(1).to_broadcast(wide), ALU.is_ge))
    step(nc.vector.tensor_tensor(table["skipped"][:, :, :], table["ended"][:, :, :], table["skip"][:, :].unsqueeze(1).to_broadcast(wide), ALU.mult))
    step(nc.vector.reduce_sum(table["texp"][:, :], table["ended"][:, :, :], AX))
    step(nc.vector.reduce_sum(table["trow"][:, :], table["skipped"][:, :, :], AX))
    step(nc.vector.tensor_scalar(table["texp_i"][:, :], table["texp"][:, :], float(E - 1), None, ALU.min))
    step(nc.vector.scalar_tensor_tensor(table["trow_i"][:, :], table["iota_f"][:, :], float(P), table["trow"][:, :], ALU.mult, ALU.add))
    assert n_r[0] == TABLE_R


def part_rows(B):
    return B * P + P


def ffn_xattn_route(nc, x_res, ctx_res, ident, w1_all, w2_all, table, stage, idx, sent, padded, sorted_rows, wq_raw, we_raw, w2_raw,
                    wr_t, ws_b, bias_b, br_b, F1, b1, F2, b2):
    B = ctx_res.shape[1]
    D = ctx_res.shape[2]
    E, F = F1.shape[0], F1.shape[1]
    C = F // P
    XW = x_res.shape[2]
    PART = part_rows(B)
    NG = B // G
    L = 3 * G
    with ExitStack() as stack:
        def sb(name, shape, dt=F32):
            return stack.enter_context(nc.sbuf_tensor(name, shape, dt))

        def sem(name):
            return stack.enter_context(nc.semaphore(name))

        wq_f = sb("wq_f", [P, D])
        wq_t = sb("wq_t", [P, D], BF16)
        we_t = sb("we_t", [P, D])
        w2_t = sb("w2_t", [P, D])
        ident_bf = sb("ident_bf", [P, P], BF16)
        eps_t = sb("eps_t", [P, L])
        lift2 = sb("lift2", [P, 1])
        three2 = sb("three2", [P, L])
        upper = sb("upper", [P, P])
        ones_pp = sb("ones_pp", [P, P])
        rev_i = sb("rev_i", [P, E], I32)
        rev_f = sb("rev_f", [P, E])
        part_i = sb("part_i", [P, E], I32)
        part_f = sb("part_f", [P, E])
        w1_raw = sb("w1_raw", [P, 4, C, D])
        w2e_raw = sb("w2e_raw", [P, 4, F])
        lg = sb("lg", [P, G, E])
        lmax = sb("lmax", [P, G])
        cand = sb("cand", [P, G, E])
        cmax = sb("cmax", [P, G])
        onehot = sb("onehot", [P, G, E])
        before = sb("before", [P, E])
        gsum = sb("gsum", [P, E])
        place = sb("place", [P, G, E])
        own = sb("own", [P, G, E])
        slot = sb("slot", [P, G])
        bn = sb("bn", [P, L, 6])
        stat = sb("stat", [P, 2, L, 2])
        g_var = sb("g_var", [P, L])
        g_ln = sb("g_ln", [P, L])
        g_y0 = sb("g_y0", [P, L])
        g_y2 = sb("g_y2", [P, L])
        g_half = sb("g_half", [P, L])
        g_vy = sb("g_vy", [P, L])
        g_r = sb("g_r", [P, L])
        g_rstd = sb("g_rstd", [P, 2, L])
        t_a = sb("t_a", [P, G, D])
        amax = sb("amax", [P, G])
        q_step = sb("q_step", [P, G])
        q_inv = sb("q_inv", [P, G])
        q_round = sb("q_round", [P, G, D])
        q_bf = sb("q_bf", [P, G, D], BF16)
        q_t = sb("q_t", [P, G, P], BF16)
        xb = sb("xb", [P, G, D])
        y_a = sb("y_a", [P, G, D])
        t_b = sb("t_b", [P, G, D])
        tb_t = sb("tb_t", [P, G, P])
        ctx_now = sb("ctx_now", [P, 2, G, D])
        ctx_t = sb("ctx_t", [P, G, P])
        ke_t = sb("ke_t", [P, G, P])
        nmax = sb("nmax", [P, G])
        probs = sb("probs", [P, G, P])
        ssum = sb("ssum", [P, G])
        sinv = sb("sinv", [P, G])
        v_s = sb("v_s", [P, G, D])
        c_cent = sb("c_cent", [P, G, D])
        t_c = sb("t_c", [P, G, D])
        tc_t = sb("tc_t", [P, G, P])

        ps = stack.enter_context(nc.psum_tensor("ps2", [P, 7, 512], F32))
        ps_q = stack.enter_context(nc.psum_tensor("ps_q", [P, 1024], BF16))
        ps_ctx, ps_ke, ps_v, ps_acc, ps_t, ps_s, ps_o = (
            ps[:, n, :].rearrange("p (g d) -> p g d", d=D) for n in range(7))
        ps_qt = ps_q[:, 0:G * P].rearrange("p (g d) -> p g d", d=P)
        ps_lg = ps_q[:, 512:512 + 2 * G * E].bitcast(F32)
        ps_rank = ps_q[:, 640:640 + 2 * G * E].bitcast(F32)

        names = ("setup_g", "setup_v", "setup_t", "setup_c", "a_stats", "a_aggr", "a_var", "a_ln", "a_y0",
                 "a_n1", "a_n2", "a_n3", "a_rs", "ta_done", "amax_done", "step_done", "inv_done", "q1_done", "q2_done", "qT_done",
                 "qt_copied", "acc_done", "ya_done", "xb2_done", "x2_done", "tb_done", "tbT_done", "tb_copied",
                 "ctxT_done", "ctx_copied", "ke_done", "ke_copied", "v2_done", "sc_done", 
                 "nmax_done", "pr_done", "sinv_done", "vs_done", "out_done", "x3_done", "cc_done", "tc_done",
                 "tcT_done", "tc_copied", "lg_done", "lg_copied", "cols_done", "ctx_taken",
                 "lmax_done", "ge_done", "cand_done", "cmax_done", "oh_done", "rank_done", "place_done", "gsum_done",
                 "own_done", "before_done", "slot_done", "routed", "staged", "b_in", "wT_done", "w_copied", "tot_done")
        s = {n: sem("m_" + n) for n in names}
        ld_raw = [sem(f"m_raw{n}") for n in range(4)]

        FIRST = 6

        def rounds(run, eng):
            for j in range(FIRST):
                run(j, j % 2, j // 2)
            with eng.Fori(0, (NG - 2 - FIRST) // 2) as turn:
                run(FIRST + 2 * turn, 0, FIRST // 2 + turn, True)
                run(FIRST + 1 + 2 * turn, 1, FIRST // 2 + turn, True)
            for j in range(NG - 2, NG + 5):
                run(j, j % 2, j // 2)

        def has(g, inside):
            return inside or 0 <= g < NG

        def after(eng, name, g, inside):
            if inside or g >= 0:
                eng.wait_ge(s[name], (g if inside else min(g, NG - 1)) + 1)

        def grp(res, g, w=slice(0, D)):
            return res[:, bass.ds(G * g, G), w]

        def one(res, g, i):
            return res[:, bass.ds(G * g + i, 1), 0:D].rearrange("p a d -> p (a d)")

        SP_FILLS = (E + 2) // 2

        def fill_up(eng, experts):
            eng.wait_ge(s["routed"], PAD_R)
            for e in experts:
                row = eng.value_load(table["pad_i"][0:1, e:e + 1], min_val=0, max_val=(E - 1) * PART + B * P)
                eng.dma_start(sorted_rows[bass.ds(row, P), :], table["fill"][:, :]).then_inc(padded, 16)

        block = stack.enter_context(nc.Block())

        @block.sync
        def _(sp):
            for e in range(E):
                sp.dma_start(w1_all[:, e, F:F + C], b1[e].rearrange("(c p) -> p c", p=P),
                             allow_slow_non_contiguous=True).then_inc(s["b_in"], 16)
                sp.dma_start(w2_all[:, e, F:F + D], b2[e].partition_broadcast(P)).then_inc(s["b_in"], 16)
            for e in range(E):
                if e > 3:
                    sp.wait_ge(s["wT_done"], 2 * (e - 3))
                sp.dma_start(w1_raw[:, e % 4], F1[e].rearrange("(c p) d -> p c d", p=P)).then_inc(ld_raw[e % 4], 16)
                sp.dma_start(w2e_raw[:, e % 4], F2[e]).then_inc(ld_raw[e % 4], 16)
            sp.wait_ge(s["b_in"], 16 * 2 * E)
            fill_up(sp, range(SP_FILLS))

        @block.scalar
        def _(act):
            act.wait_ge(s["setup_t"], 1)
            nc.scalar.activation(wq_t[:, :], ps_ctx[:, 0, :], ACT.Copy).then_inc(s["setup_c"], 1)
            nc.scalar.activation(we_t[:, :], ps_ctx[:, 1, :], ACT.Copy).then_inc(s["setup_c"], 1)
            nc.scalar.activation(w2_t[:, :], ps_ctx[:, 2, :], ACT.Copy).then_inc(s["setup_c"], 1)
            act.wait_ge(s["setup_g"], 3)
            nc.scalar.preload_act_table_set("natural_log_exp_and_others")

            def run(j, par, half, inside=False):
                if has(j - 2, inside):
                    after(act, "sinv_done", j - 2, inside)
                    after(act, "v2_done", j - 2, inside)
                    for i in range(G):
                        last = nc.scalar.activation(v_s[:, i, :], ps_v[:, i, :], ACT.Copy, scale=sinv[:, i:i + 1])
                    last.then_inc(s["vs_done"], 1)
                if has(j, inside) or has(j - 1, inside) or has(j - 3, inside):
                    act.wait_ge(s["a_var"], j + 1)
                    nc.scalar.activation(g_ln[:, :], g_var[:, :], ACT.Ln, scale=float(2 ** LN_LIFT)).then_inc(s["a_ln"], 1)
                    act.wait_ge(s["a_ln"], j + 1)
                    nc.scalar.activation(g_y0[:, :], g_ln[:, :], ACT.Exp, scale=-0.5, bias=lift2[:, 0:1]).then_inc(s["a_y0"], 1)
                if has(j - 1, inside):
                    after(act, "ke_done", j - 1, inside)
                    after(act, "sc_done", j - 2, inside)
                    nc.scalar.activation(ke_t[:, :, :], ps_ke, ACT.Copy).then_inc(s["ke_copied"], 1)
                if has(j - 1, inside):
                    after(act, "tbT_done", j - 1, inside)
                    nc.scalar.activation(tb_t[:, :, :], ps_t, ACT.Copy).then_inc(s["tb_copied"], 1)
                if has(j, inside):
                    after(act, "qT_done", j, inside)
                    nc.scalar.activation(q_t[:, :, :], ps_qt, ACT.Copy).then_inc(s["qt_copied"], 1)
                if has(j - 1, inside):
                    after(act, "nmax_done", j - 1, inside)
                    for i in range(G):
                        last = nc.scalar.activation(probs[:, i, :], ps_s[:, i, :], ACT.Exp, bias=nmax[:, i:i + 1],
                                                    accum_out=ssum[:, i:i + 1])
                    last.then_inc(s["pr_done"], 1)

                if has(j - 3, inside):
                    after(act, "tcT_done", j - 3, inside)
                    nc.scalar.activation(tc_t[:, :, :], ps_t, ACT.Copy).then_inc(s["tc_copied"], 1)
                if has(j, inside):
                    after(act, "ctxT_done", j, inside)
                    after(act, "ke_done", j - 1, inside)
                    after(act, "v2_done", j - 1, inside)
                    nc.scalar.activation(ctx_t[:, :, :], ps_ctx, ACT.Copy).then_inc(s["ctx_copied"], 1)
                if not inside and j > NG:
                    for e in (2 * (j - NG - 1), 2 * (j - NG - 1) + 1):
                        act.wait_ge(s["wT_done"], 2 * e + 1)
                        nc.scalar.activation(w1_all[:, e, 0:F], ps[:, 3, :], ACT.Copy).then_inc(s["w_copied"], 1)
                        act.wait_ge(s["wT_done"], 2 * e + 2)
                        nc.scalar.activation(w2_all[:, e, 0:F], ps[:, 1, :], ACT.Copy).then_inc(s["w_copied"], 1)

            rounds(run, act)
            fill_up(act, range(SP_FILLS, E))

        @block.gpsimd
        def _(pool):
            nc.gpsimd.memset(eps_t[:, :], LN_EPS).then_inc(s["setup_g"], 1)
            nc.gpsimd.memset(three2[:, :], 3.0).then_inc(s["setup_g"], 1)
            nc.gpsimd.memset(lift2[:, :], 0.5 * LN_LIFT * LN2).then_inc(s["setup_g"], 1)
            nc.gpsimd.memset(upper[:, :], 1.0).then_inc(s["setup_g"], 1)
            nc.gpsimd.memset(ones_pp[:, :], 1.0).then_inc(s["setup_g"], 1)
            nc.gpsimd.memset(before[:, :], 0.0).then_inc(s["setup_g"], 1)
            nc.gpsimd.iota(rev_i[:, :], pattern=[[-1, E]], base=E, channel_multiplier=0).then_inc(s["setup_g"], 1)
            nc.gpsimd.iota(part_i[:, :], pattern=[[PART, E]], base=0, channel_multiplier=0).then_inc(s["setup_g"], 1)
            pool.wait_ge(s["setup_g"], 8)
            nc.gpsimd.affine_select(out=upper[:, :], in_=upper[:, :], compare_op=ALU.is_gt, fill=0.0,
                                    base=0, pattern=[[1, P]], channel_multiplier=-1).then_inc(s["setup_g"], 1)
            nc.gpsimd.iota(table["iota_i"][:, :], pattern=[[1, table["texp"].shape[1]]], base=0,
                           channel_multiplier=0).then_inc(s["setup_g"], 1)
            nc.gpsimd.iota(table["base_i"][:, :], pattern=[[PART, E]], base=0, channel_multiplier=0).then_inc(s["setup_g"], 1)
            nc.gpsimd.memset(table["fill"][:, :], FILL).then_inc(s["setup_g"], 1)
            pool.wait_ge(s["setup_g"], 12)
            nc.gpsimd.tensor_copy(ctx_now[:, 0, :, :], ctx_res[:, 0:G, :]).then_inc(s["ctx_taken"], 1)
            pool.wait_ge(s["setup_v"], 5)

            def run(j, par, half, inside=False):
                if has(j, inside) or has(j - 1, inside) or has(j - 3, inside):
                    pool.wait_ge(s["a_aggr"], j + 1)
                    nc.gpsimd.tensor_tensor(g_var[:, :], stat[:, par, :, 1], eps_t[:, :], ALU.add).then_inc(s["a_var"], 1)
                if has(j, inside) or has(j - 1, inside) or has(j - 3, inside):
                    pool.wait_ge(s["a_y0"], j + 1)
                    nc.gpsimd.tensor_tensor(g_y2[:, :], g_y0[:, :], g_y0[:, :], ALU.mult)
                    nc.gpsimd.tensor_scalar(g_half[:, :], g_y0[:, :], -0.5, None, ALU.mult).then_inc(s["a_n1"], 1)
                    pool.wait_ge(s["a_n1"], j + 1)
                    nc.gpsimd.tensor_tensor(g_vy[:, :], g_y2[:, :], g_var[:, :], ALU.mult).then_inc(s["a_n2"], 1)
                    pool.wait_ge(s["a_n2"], j + 1)
                    nc.gpsimd.tensor_tensor(g_r[:, :], g_vy[:, :], three2[:, :], ALU.subtract).then_inc(s["a_n3"], 1)
                    pool.wait_ge(s["a_n3"], j + 1)
                    nc.gpsimd.tensor_tensor(g_rstd[:, par, :], g_r[:, :], g_half[:, :], ALU.mult).then_inc(s["a_rs"], 1)
                if has(j - 3, inside):
                    if has(j - 5, inside):
                        after(pool, "staged", j - 5, inside)
                    pool.wait_ge(s["a_rs"], j + 1)
                    nc.gpsimd.tensor_tensor(c_cent[:, :, :], grp(x_res, j - 3),
                                            stat[:, par, 2 * G:L, 0:1].to_broadcast([P, G, D]), ALU.subtract).then_inc(s["cc_done"], 1)
                    after(pool, "cc_done", j - 3, inside)
                    nc.gpsimd.tensor_tensor(t_c[:, :, :], c_cent[:, :, :],
                                            g_rstd[:, par, 2 * G:L].unsqueeze(2).to_broadcast([P, G, D]), ALU.mult).then_inc(s["tc_done"], 1)
                if has(j, inside):
                    after(pool, "ctxT_done", j - 1, inside)
                    nc.gpsimd.tensor_tensor(xb[:, :, :], grp(x_res, j),
                                            bias_b[:, :].unsqueeze(1).to_broadcast([P, G, D]), ALU.add).then_inc(s["xb2_done"], 1)
                if has(j + 1, inside):
                    nc.gpsimd.tensor_copy(ctx_now[:, 1 - par, :, :], grp(ctx_res, j + 1)).then_inc(s["ctx_taken"], 1)

                if has(j - 5, inside):
                    if not has(j - 3, inside):
                        after(pool, "staged", j - 5, inside)
                    for i in range(G):
                        nc.gpsimd.indirect_dma_start(
                            out=sorted_rows, out_offset=bass.IndirectOffsetOnAxis(ap=idx[:, 1 - par, i:i + 1], axis=0),
                            in_=stage[:, 1 - par, i, :], in_offset=None).then_inc(sent[1 - par], 16)

            rounds(run, pool)

        @block.vector
        def _(dve):
            nc.vector.tensor_copy(wq_f[:, :], wq_raw[:, :]).then_inc(s["setup_v"], 1)
            nc.vector.tensor_copy(ident_bf[:, :], ident[:, :]).then_inc(s["setup_v"], 1)
            nc.vector.memset(stat[:, :, :, :], 1.0).then_inc(s["setup_v"], 1)
            dve.wait_ge(s["setup_g"], 12)
            nc.vector.tensor_copy(rev_f[:, :], rev_i[:, :]).then_inc(s["setup_v"], 1)
            nc.vector.tensor_copy(part_f[:, :], part_i[:, :]).then_inc(s["setup_v"], 1)
            dve.wait_ge(s["setup_v"], 5)

            def run(j, par, half, inside=False):
                kinds = [(n, g) for n, g in ((0, j), (1, j - 1), (2, j - 3)) if has(g, inside)]
                live = bool(kinds)
                if live:
                    after(dve, "x2_done", j - 1, inside)
                    for n, g in kinds:
                        for i in range(G):
                            last = nc.vector.bn_stats(bn[:, n * G + i, :], one(x_res, g, i))
                    last.then_inc(s["a_stats"], 1)
                if live:
                    dve.wait_ge(s["a_stats"], j + 1)
                if has(j - 2, inside):
                    after(dve, "pr_done", j - 2, inside)
                    nc.vector.reciprocal(sinv[:, :], ssum[:, :]).then_inc(s["sinv_done"], 1)
                if live:
                    for n, g in kinds:
                        for i in range(G):
                            last = nc.vector.bn_aggr(stat[:, par, n * G + i, :], bn[:, n * G + i, :])
                    last.then_inc(s["a_aggr"], 1)
                if has(j - 4, inside):
                    after(dve, "lg_done", j - 4, inside)
                    bias_all = br_b[:, :].unsqueeze(1).to_broadcast([P, G, E])
                    nc.vector.tensor_tensor(lg[:, :, :], ps_lg.rearrange("p (g e) -> p g e", e=E), bias_all,
                                            ALU.add).then_inc(s["lg_copied"], 1)
                    after(dve, "lg_copied", j - 4, inside)
                    nc.vector.reduce_max(lmax[:, :], lg[:, :, :], AX).then_inc(s["lmax_done"], 1)
                    after(dve, "lmax_done", j - 4, inside)
                    nc.vector.tensor_tensor(cand[:, :, :], lg[:, :, :], lmax[:, :].unsqueeze(2).to_broadcast([P, G, E]),
                                            ALU.is_ge).then_inc(s["ge_done"], 1)
                if has(j - 4, inside):
                    after(dve, "ge_done", j - 4, inside)
                    nc.vector.tensor_tensor(cand[:, :, :], cand[:, :, :], rev_f[:, :].unsqueeze(1).to_broadcast([P, G, E]),
                                            ALU.mult).then_inc(s["cand_done"], 1)
                    after(dve, "cand_done", j - 4, inside)
                    nc.vector.reduce_max(cmax[:, :], cand[:, :, :], AX).then_inc(s["cmax_done"], 1)
                    after(dve, "cmax_done", j - 4, inside)
                    nc.vector.tensor_tensor(onehot[:, :, :], cand[:, :, :],
                                            cmax[:, :].unsqueeze(2).to_broadcast([P, G, E]),
                                            ALU.is_equal).then_inc(s["oh_done"], 1)
                if live:
                    dve.wait_ge(s["a_rs"], j + 1)
                if has(j - 1, inside):
                    for i in range(G):
                        last = nc.vector.tensor_scalar(t_b[:, i, :], one(x_res, j - 1, i), stat[:, par, G + i, 0:1],
                                                       g_rstd[:, par, G + i:G + i + 1], ALU.subtract, ALU.mult)
                    last.then_inc(s["tb_done"], 1)
                if has(j, inside):
                    for i in range(G):
                        last = nc.vector.tensor_scalar(t_a[:, i, :], one(x_res, j, i), stat[:, par, i, 0:1],
                                                       g_rstd[:, par, i:i + 1], ALU.subtract, ALU.mult)
                    last.then_inc(s["ta_done"], 1)
                    after(dve, "ta_done", j, inside)
                    nc.vector.tensor_reduce(amax[:, :], t_a[:, :, :], AX, ALU.max, apply_absolute_value=True).then_inc(s["amax_done"], 1)
                if has(j - 2, inside):
                    after(dve, "out_done", j - 2, inside)
                    nc.vector.tensor_tensor(grp(x_res, j - 2), grp(x_res, j - 2), ps_o, ALU.add).then_inc(s["x3_done"], 1)
                if has(j, inside):
                    after(dve, "amax_done", j, inside)
                    nc.vector.tensor_scalar(q_step[:, :], amax[:, :], Q_EPS, 1.0 / Q_MAX, ALU.max, ALU.mult).then_inc(s["step_done"], 1)
                if has(j - 4, inside):
                    after(dve, "rank_done", j - 4, inside)
                    nc.vector.tensor_tensor(place[:, :, :], ps_rank.rearrange("p (g e) -> p g e", e=E),
                                            part_f[:, :].unsqueeze(1).to_broadcast([P, G, E]), ALU.add).then_inc(s["place_done"], 1)
                    nc.vector.reduce_sum(gsum[:, :], onehot[:, :, :].rearrange("p g e -> p e g"), AX).then_inc(s["gsum_done"], 1)
                if has(j, inside):
                    after(dve, "step_done", j, inside)
                    nc.vector.reciprocal(q_inv[:, :], q_step[:, :]).then_inc(s["inv_done"], 1)
                if has(j - 4, inside):
                    after(dve, "gsum_done", j - 4, inside)
                    nc.vector.tensor_tensor(own[:, :, :], place[:, :, :], onehot[:, :, :], ALU.mult).then_inc(s["own_done"], 1)
                    nc.vector.tensor_tensor(before[:, :], before[:, :], gsum[:, :], ALU.add).then_inc(s["before_done"], 1)
                if has(j - 3, inside):
                    nc.vector.tensor_copy(grp(x_res, j - 3, slice(D, D + 1)), stat[:, par, 2 * G:L, 0:1])
                    nc.vector.tensor_copy(grp(x_res, j - 3, slice(D + 1, D + 2)),
                                          g_rstd[:, par, 2 * G:L].unsqueeze(2)).then_inc(s["cols_done"], 1)
                if has(j, inside):
                    after(dve, "inv_done", j, inside)
                    for i in range(G):
                        last = nc.vector.tensor_scalar(q_round[:, i, :], t_a[:, i, :], q_inv[:, i:i + 1], ROUND,
                                                       ALU.mult, ALU.add)
                    last.then_inc(s["q1_done"], 1)
                if has(j - 4, inside):
                    after(dve, "own_done", j - 4, inside)
                    nc.vector.reduce_sum(slot[:, :], own[:, :, :], AX).then_inc(s["slot_done"], 1)
                if has(j, inside):
                    after(dve, "q1_done", j, inside)
                    nc.vector.tensor_scalar(q_bf[:, :, :], q_round[:, :, :], ROUND, Q_MAX, ALU.subtract,
                                            ALU.min).then_inc(s["q2_done"], 1)
                if has(j - 1, inside):
                    after(dve, "sc_done", j - 1, inside)
                    nc.vector.tensor_reduce(nmax[:, :], ps_s, AX, ALU.max, negate=True).then_inc(s["nmax_done"], 1)
                if has(j - 4, inside):
                    after(dve, "slot_done", j - 4, inside)
                    if inside or j > 5:
                        dve.wait_ge(sent[par], 16 * G * (half - 2))
                    nc.vector.tensor_copy(idx[:, par, :], slot[:, :])
                    nc.vector.tensor_copy(stage[:, par, :, :], grp(x_res, j - 4, slice(0, XW))).then_inc(s["staged"], 1)
                if has(j, inside):
                    after(dve, "acc_done", j, inside)
                    for i in range(G):
                        last = nc.vector.scalar_tensor_tensor(y_a[:, i, :], ps_acc[:, i, :], q_step[:, i:i + 1],
                                                              ws_b[:, :], ALU.mult, ALU.mult)
                    last.then_inc(s["ya_done"], 1)
                    after(dve, "ya_done", j, inside)
                    after(dve, "xb2_done", j, inside)
                    nc.vector.tensor_tensor(grp(x_res, j), y_a[:, :, :], xb[:, :, :], ALU.add).then_inc(s["x2_done"], 1)

            rounds(run, dve)
            dve.wait_ge(s["tot_done"], 1)
            nc.vector.tensor_copy(table["total"][:, :], ps[:, 0, 0:E])
            tile_table(nc, dve, table, s["routed"], E, table["texp"].shape[1], PART)

        @block.tensor
        def _(pe):
            pe.wait_ge(s["setup_v"], 2)
            nc.tensor.transpose(ps_ctx[:, 0, :], wq_f[:, :], ident[:, :])
            nc.tensor.transpose(ps_ctx[:, 1, :], we_raw[:, :], ident[:, :])
            nc.tensor.transpose(ps_ctx[:, 2, :], w2_raw[:, :], ident[:, :]).then_inc(s["setup_t"], 1)
            pe.wait_ge(s["setup_c"], 3)

            def run(j, par, half, inside=False):
                if has(j - 2, inside):
                    after(pe, "vs_done", j - 2, inside)
                    for i in range(G):
                        last = nc.tensor.matmul(ps_o[:, i, :], probs[:, i, :], v_s[:, i, :], start=True, stop=True)
                    last.then_inc(s["out_done"], 1)
                if has(j - 1, inside):
                    after(pe, "tb_done", j - 1, inside)
                    for i in range(G):
                        last = nc.tensor.transpose(ps_t[:, i, :], t_b[:, i, :], ident[:, :])
                    last.then_inc(s["tbT_done"], 1)
                if has(j - 4, inside):
                    after(pe, "oh_done", j - 4, inside)
                    nc.tensor.matmul(ps_rank, upper[:, :], onehot[:, :, :].rearrange("p g e -> p (g e)"),
                                     start=True, stop=False)
                    for i in range(G - 1):
                        nc.tensor.matmul(ps_rank[:, (i + 1) * E:], ones_pp[:, :],
                                         onehot[:, i:i + 1, :].to_broadcast([P, G - 1 - i, E]), start=False, stop=False)
                    nc.tensor.matmul(ps_rank, ones_pp[:, :], before[:, :].unsqueeze(1).to_broadcast([P, G, E]),
                                     start=False, stop=True).then_inc(s["rank_done"], 1)
                if has(j - 1, inside):
                    after(pe, "ke_copied", j - 1, inside)
                    after(pe, "tb_copied", j - 1, inside)
                    after(pe, "pr_done", j - 2, inside)
                    for i in range(G):
                        last = nc.tensor.matmul(ps_s[:, i, :], ke_t[:, i, :], tb_t[:, i, :], start=True, stop=True)
                    last.then_inc(s["sc_done"], 1)
                if has(j, inside):
                    after(pe, "q2_done", j, inside)
                    after(pe, "place_done", j - 4, inside)
                    for i in range(G):
                        last = nc.tensor.transpose(ps_qt[:, i, :], q_bf[:, i, :], ident_bf[:, :])
                    last.then_inc(s["qT_done"], 1)
                if has(j, inside):
                    after(pe, "qt_copied", j, inside)
                    for i in range(G):
                        last = nc.tensor.matmul(ps_acc[:, i, :], q_t[:, i, :], wq_t[:, :], start=True, stop=True)
                    last.then_inc(s["acc_done"], 1)
                if has(j - 3, inside):
                    after(pe, "tc_done", j - 3, inside)
                    for i in range(G):
                        last = nc.tensor.transpose(ps_t[:, i, :], t_c[:, i, :], ident[:, :])
                    last.then_inc(s["tcT_done"], 1)
                if has(j - 1, inside):
                    after(pe, "vs_done", j - 2, inside)
                    for i in range(G):
                        last = nc.tensor.matmul(ps_v[:, i, :], ctx_t[:, i, :], w2_t[:, :], start=True, stop=True)
                    last.then_inc(s["v2_done"], 1)
                if has(j, inside):
                    after(pe, "ctx_taken", j, inside)
                    after(pe, "ctx_copied", j - 1, inside)
                    for i in range(G):
                        last = nc.tensor.transpose(ps_ctx[:, i, :], ctx_now[:, par, i, :], ident[:, :])
                    last.then_inc(s["ctxT_done"], 1)
                if has(j - 3, inside):
                    after(pe, "tc_copied", j - 3, inside)
                    after(pe, "place_done", j - 4, inside)
                    for i in range(G):
                        last = nc.tensor.matmul(ps_lg[:, i * E:(i + 1) * E], tc_t[:, i, :], wr_t[:, :],
                                                start=True, stop=True)
                    last.then_inc(s["lg_done"], 1)
                if has(j, inside):
                    after(pe, "ctx_copied", j, inside)
                    after(pe, "ke_copied", j - 1, inside)
                    nc.tensor.matmul(ps[:, 1, :], we_t[:, :], ctx_t[:, :, :].rearrange("p g m -> p (g m)"),
                                     start=True, stop=True).then_inc(s["ke_done"], 1)

                if not inside and j == NG + 4:
                    after(pe, "before_done", NG - 1, False)
                    nc.tensor.matmul(ps[:, 0, 0:E], ones_pp[:, :], before[:, :], start=True,
                                     stop=True).then_inc(s["tot_done"], 1)
                if not inside and j > NG:
                    for e in (2 * (j - NG - 1), 2 * (j - NG - 1) + 1):
                        pe.wait_ge(ld_raw[e % 4], 32 * (e // 4 + 1))
                        for half_n, (raw, bank) in enumerate(((w1_raw[:, e % 4].rearrange("p c d -> p (c d)"), 3),
                                                              (w2e_raw[:, e % 4, :], 1))):
                            if 2 * e + half_n > 1:
                                pe.wait_ge(s["w_copied"], 2 * e + half_n - 1)
                            for c in range(C):
                                last = nc.tensor.transpose(ps[:, bank, c * P:(c + 1) * P], raw[:, c * P:(c + 1) * P],
                                                           ident[:, :])
                            last.then_inc(s["wT_done"], 1)

            rounds(run, pe)


def experts_program(nc, B, T, F, ident, w1_all, w2_all, table, sent, padded, sorted_rows, out):
    E, D = w1_all.shape[1], out.shape[2]
    XW = sorted_rows.shape[1]
    PART = part_rows(B)
    C = F // P
    TOK = B * P
    W1C = F + C
    W2C = F + D
    assert T % DEEP == 0
    out_rows = out.rearrange("b s d -> (b s) d")
    texp_i, trow_i = table["texp_i"], table["trow_i"]
    with ExitStack() as stack:
        def sb(name, shape, dt=F32):
            return stack.enter_context(nc.sbuf_tensor(name, shape, dt))

        def sem(name):
            return stack.enter_context(nc.semaphore(name))

        rows = sb("rows", [P, T, XW])
        w1_now = sb("w1_now", [P, 2, W1C])
        w2_now = sb("w2_now", [P, 2, W2C])
        t_now = sb("t_now", [P, 2, D])
        t_t = sb("t_t", [P, 2, P])
        h_t = sb("h_t", [P, 2, C, P])
        xb2 = sb("xb2", [P, 2, D])
        o_now = sb("o_now", [P, 2, D])
        o_idx = sb("o_idx", [P, 2, 1], U32)

        ps = stack.enter_context(nc.psum_tensor("ps3", [P, 8, 512], F32))
        ps_h = (ps[:, 0, :], ps[:, 1, :])
        ps_t = (ps[:, 2, 0:P], ps[:, 3, 0:P])
        ps_y = (ps[:, 4, 0:P], ps[:, 5, 0:P])

        names = ("rows_in", "w1_set", "w2_set", "t_set", "T_done", "t_copied",
                 "h_done", "relu_done", "y_done", "xb_set", "fin", "out_sent0", "out_sent1")
        s = {n: sem("e_" + n) for n in names}
        ld = [sem(f"e_ld{n}") for n in range(DEEP)]

        FIRST = 4

        def rounds(run, eng):
            for j in range(-2, FIRST):
                run(j, j % 2, j // 2)
            with eng.Fori(0, (T - 2 - FIRST) // 2) as turn:
                run(FIRST + 2 * turn, 0, FIRST // 2 + turn, True)
                run(FIRST + 1 + 2 * turn, 1, FIRST // 2 + turn, True)
            for j in range(T - 2, T + 1):
                run(j, j % 2, j // 2)

        def has(k, inside):
            return inside or 0 <= k < T

        def after(eng, name, k, inside, n=1):
            if inside or k >= 0:
                eng.wait_ge(s[name], (k + 1) * n)

        def flat(ap):
            return ap.rearrange("p a d -> p (a d)")

        block = stack.enter_context(nc.Block())

        @block.sync
        def _(sp):
            sp.wait_ge(padded, 16 * E)
            for half in (0, 1):
                sp.wait_ge(sent[half], 8 * B)

            def load(i, n):
                row = sp.value_load(trow_i[0:1, bass.ds(i, 1)], min_val=0, max_val=E * PART + (E - 1) * P)
                sp.dma_start(rows[:, bass.ds(i, 1), :].rearrange("p a w -> p (a w)"),
                             sorted_rows[bass.ds(row, P), :]).then_inc(ld[n], 16)

            for n in range(DEEP):
                load(n, n)
            with sp.Fori(1, T // DEEP) as turn:
                for n in range(DEEP):
                    sp.wait_ge(ld[n], 16 * turn)
                    sp.sem_inc(s["rows_in"], 1)
                    load(DEEP * turn + n, n)
            for n in range(DEEP):
                sp.wait_ge(ld[n], 16 * (T // DEEP))
                sp.sem_inc(s["rows_in"], 1)
            sp.wait_ge(s["out_sent0"], 8 * T)
            sp.wait_ge(s["out_sent1"], 8 * T)

        @block.scalar
        def _(act):
            def run(j, par, half, inside=False):
                if has(j + 1, inside):
                    after(act, "T_done", j + 1, inside)
                    nc.scalar.activation(t_t[:, 1 - par, :], ps_t[1 - par], ACT.Copy).then_inc(s["t_copied"], 1)
                if has(j, inside):
                    after(act, "h_done", j, inside)
                    for c in range(C):
                        last = nc.scalar.activation(h_t[:, par, c, :], ps_h[par][:, c * P:(c + 1) * P], ACT.Relu,
                                                    bias=w1_now[:, par, F + c:F + c + 1])
                    last.then_inc(s["relu_done"], 1)

            rounds(run, act)

        @block.gpsimd
        def _(pool):
            def run(j, par, half, inside=False):
                if has(j - 1, inside):
                    after(pool, "fin", j - 1, inside)
                if has(j, inside):
                    if not has(j - 1, inside):
                        pool.wait_ge(s["rows_in"], 1)
                    after(pool, "w2_set", j, inside)
                    nc.gpsimd.tensor_tensor(xb2[:, par, :], flat(rows[:, bass.ds(j, 1), 0:D]), w2_now[:, par, F:W2C],
                                            ALU.add).then_inc(s["xb_set"], 1)
                if has(j - 1, inside):
                    nc.gpsimd.indirect_dma_start(
                        out=out_rows, out_offset=bass.IndirectOffsetOnAxis(ap=o_idx[:, 1 - par, :], axis=0),
                        in_=o_now[:, 1 - par, :], in_offset=None, bounds_check=TOK - 1,
                        oob_is_err=False).then_inc(s[f"out_sent{1 - par}"], 16)

            rounds(run, pool)

        @block.vector
        def _(dve):
            def run(j, par, half, inside=False):
                if has(j + 1, inside):
                    e = dve.value_load(texp_i[0:1, bass.ds(j + 1, 1)], min_val=0, max_val=E - 1)
                    after(dve, "relu_done", j - 1, inside)
                    nc.vector.tensor_copy(w1_now[:, 1 - par, :], flat(w1_all[:, bass.ds(e, 1), :])).then_inc(s["w1_set"], 1)
                if has(j + 2, inside):
                    after(dve, "rows_in", j + 2, inside)
                    after(dve, "T_done", j, inside)
                    row = rows[:, bass.ds(j + 2, 1), :]
                    nc.vector.tensor_scalar(t_now[:, par, :], flat(row[:, :, 0:D]), flat(row[:, :, D:D + 1]),
                                            flat(row[:, :, D + 1:D + 2]), ALU.subtract, ALU.mult).then_inc(s["t_set"], 1)
                if has(j - 1, inside):
                    if inside or j > 2:
                        dve.wait_ge(s[f"out_sent{1 - par}"], 16 * (half - 1 + par))
                    after(dve, "xb_set", j - 1, inside)
                    after(dve, "y_done", j - 1, inside)
                    nc.vector.tensor_copy(o_idx[:, 1 - par, :], flat(rows[:, bass.ds(j - 1, 1), D + 2:D + 3]))
                    nc.vector.tensor_tensor(o_now[:, 1 - par, :], ps_y[1 - par], xb2[:, 1 - par, :],
                                            ALU.add).then_inc(s["fin"], 1)
                if has(j + 1, inside):
                    nc.vector.tensor_copy(w2_now[:, 1 - par, :], flat(w2_all[:, bass.ds(e, 1), :])).then_inc(s["w2_set"], 1)

            rounds(run, dve)

        @block.tensor
        def _(pe):
            def run(j, par, half, inside=False):
                if has(j + 1, inside):
                    after(pe, "t_set", j + 1, inside)
                    nc.tensor.transpose(ps_t[1 - par], t_now[:, 1 - par, :], ident[:, :]).then_inc(s["T_done"], 1)
                if has(j, inside):
                    after(pe, "t_copied", j, inside)
                    after(pe, "w1_set", j, inside)
                    for c in range(C):
                        last = nc.tensor.matmul(ps_h[par][:, c * P:(c + 1) * P], w1_now[:, par, c * P:(c + 1) * P],
                                                t_t[:, par, :], start=True, stop=True)
                    last.then_inc(s["h_done"], 1)
                if has(j - 1, inside):
                    after(pe, "relu_done", j - 1, inside)
                    after(pe, "w2_set", j - 1, inside)
                    for c in range(C):
                        last = nc.tensor.matmul(ps_y[1 - par], h_t[:, 1 - par, c, :],
                                                w2_now[:, 1 - par, c * P:(c + 1) * P], start=c == 0, stop=c == C - 1)
                    last.then_inc(s["y_done"], 1)

            rounds(run, pe)


def layers(nc, x, ctx, mask, ln_x_w, ln_x_b, ln_l_w, ln_l_b, Wq, Wkv, q_scale, k_scale, Wo, ln_o_w, ln_o_b,
           weight_q, weight_scale, bias, We, W2, Wr, br, F1, b1, F2, b2, out):
    B, S, D = x.shape
    M = ctx.shape[1]
    E = Wr.shape[0]
    mask = mask.bitcast(U8).rearrange("(b m) -> b m", m=M)
    weight_q = weight_q.bitcast(I8).rearrange("(o i) -> o i", i=D)
    tiles = -(-(B * S // P + E - 1) // DEEP) * DEEP
    sorted_rows = nc.dram_tensor("sorted_rows", (E * part_rows(B) + E * P, D + 3), F32, kind="Internal").ap()
    F = F1.shape[1]
    with ExitStack() as stack:
        def sb(name, shape):
            return stack.enter_context(nc.sbuf_tensor(name, shape, F32))

        x_res = sb("x_res", [P, B, D + 3])
        ctx_res = sb("ctx_res", [P, B, D])
        ident = sb("ident", [P, P])
        wq_raw = stack.enter_context(nc.sbuf_tensor("wq_raw", [P, D], I8))
        we_raw = sb("we_raw", [P, D])
        w2_raw = sb("w2_raw", [P, D])
        wr_t = sb("wr_t", [P, E])
        ws_b = sb("ws_b", [P, D])
        bias_b = sb("bias_b", [P, D])
        br_b = sb("br_b", [P, E])
        second = ((wq_raw[:, :], weight_q), (we_raw[:, :], We), (w2_raw[:, :], W2),
                  (wr_t[:, :], Wr.rearrange("e d -> d e")), (ws_b[:, :], weight_scale.partition_broadcast(P)),
                  (bias_b[:, :], bias.partition_broadcast(P)), (br_b[:, :], br.partition_broadcast(P)))
        latent_attention(nc, x_res, ctx_res, ident, sorted_rows, x, ctx, mask, ln_x_w, ln_x_b, ln_l_w, ln_l_b,
                         Wq, Wkv, q_scale, k_scale, Wo, ln_o_w, ln_o_b, E, second)
        w1_all = sb("w1_all", [P, E, F + F // P])
        w2_all = sb("w2_all", [P, E, F + D])
        shapes = dict(total=[E], iota_f=[tiles], base_f=[E], ntile=[E], tend=[2, E], skip=[E], pad_f=[E],
                      ended=[tiles, E], skipped=[tiles, E], texp=[tiles], trow=[tiles], fill=[D + 3])
        table = {name: sb("table_" + name, [P] + shape) for name, shape in shapes.items()}
        for name, size in (("iota_i", tiles), ("base_i", E), ("pad_i", E), ("texp_i", tiles), ("trow_i", tiles)):
            table[name] = stack.enter_context(nc.sbuf_tensor("table_" + name, [P, size], I32))
        stage = sb("stage", [P, 2, G, D + 3])
        idx = stack.enter_context(nc.sbuf_tensor("idx", [P, 2, G], U32))
        sent = [stack.enter_context(nc.semaphore(f"sent{n}")) for n in range(2)]
        padded = stack.enter_context(nc.semaphore("padded"))
        ffn_xattn_route(nc, x_res, ctx_res, ident, w1_all, w2_all, table, stage, idx, sent, padded, sorted_rows, wq_raw,
                        we_raw, w2_raw, wr_t, ws_b, bias_b, br_b, F1, b1, F2, b2)
        experts_program(nc, B, tiles, F, ident, w1_all, w2_all, table, sent, padded, sorted_rows, out)


INPUTS = ['x', 'ctx_1024', 'mask_BxS2_bk0', 'L0_xattn_ln_x_w', 'L0_xattn_ln_x_b', 'L0_xattn_ln_l_w', 'L0_xattn_ln_l_b',
          'L0_xattn_Wq', 'L0_xattn_Wkv', 'L0_xattn_q_scale', 'L0_xattn_k_scale', 'L0_xattn_Wo', 'L0_xattn_ln_o_w',
          'L0_xattn_ln_o_b', 'L0_ffn_weight_q', 'L0_ffn_weight_scale', 'L0_ffn_bias', 'L1_xattn_We', 'L1_xattn_W2',
          'L1_ffn_Wr', 'L1_ffn_br', 'L1_ffn_W1', 'L1_ffn_b1', 'L1_ffn_W2', 'L1_ffn_b2']


def kernel(**inputs):
    import numpy as np
    import concourse.bacc as bacc
    from concourse.bass_utils import run_bass_kernel_spmd

    nc = bacc.Bacc("TRN2", target_bir_lowering=False, num_devices=1)
    arrays, args = {}, []
    for name in INPUTS:
        a = np.ascontiguousarray(inputs[name])
        if a.dtype.itemsize == 1:
            a = a.reshape(-1).view(np.int32)
        arrays[f"in_{name}_dram"] = a
        args.append(nc.dram_tensor(f"in_{name}_dram", a.shape, mybir.dt.from_np(a.dtype), kind="ExternalInput").ap())
    out = nc.dram_tensor("out_dram", arrays["in_x_dram"].shape, F32, kind="ExternalOutput").ap()
    layers(nc, *args, out)
    r = run_bass_kernel_spmd(nc, [arrays], core_ids=[0])
    return r.results[0]["out_dram"]
```
